# Optimizing a Trainium2 kernel written in Bass

```python
import numpy as np
import jax
import jax.numpy as jnp

def _softmax(x, axis=-1):
    return jax.nn.softmax(x, axis=axis)

def _gelu(x):
    return jax.nn.gelu(x, approximate=True)

def _silu(x):
    return jax.nn.silu(x)

def _sigmoid(x):
    return jax.nn.sigmoid(x)

def _layernorm(x, axis=-1, eps=1e-05):
    m = jnp.mean(x, axis=axis, keepdims=True)
    v = jnp.var(x, axis=axis, keepdims=True)
    return (x - m) / jnp.sqrt(v + eps)

def _scatter_add(tgt, idx, src, axis=0):
    return tgt.at[idx].add(src)

def _segment_sum(src, seg, n):
    return jax.ops.segment_sum(src, seg, n)
kernel_name = 'mk_adaln_d1_jaxref_r8_2f5bc7'

def setup_inputs(seed: int=0):
    np.random.seed(seed)
    _w = jnp.asarray

    def _L0_attn_setup():
        import jax, jax.numpy as jnp
        import numpy as np
        D_MODEL, N_HEADS = (128, 16)
        D_H = D_MODEL // N_HEADS
        D_HR = D_H // 2
        D_LATENT = 32
        THETA = 10000.0

        def rope(x, theta=THETA):
            S, d = (x.shape[-2], x.shape[-1])
            inv = theta ** (-jnp.arange(0, d, 2, dtype=jnp.float32) / d)
            ang = jnp.arange(S, dtype=jnp.float32)[:, None] * inv
            cos, sin = (jnp.cos(ang), jnp.sin(ang))
            x1, x2 = (x[..., 0::2], x[..., 1::2])
            r1 = x1 * cos - x2 * sin
            r2 = x1 * sin + x2 * cos
            return jnp.stack([r1, r2], axis=-1).reshape(x.shape)
        key = jax.random.key(seed)
        ks = jax.random.split(key, 9)
        s = lambda fan_in: 1.0 / np.sqrt(fan_in)
        return {'x': jax.random.normal(ks[0], (4, 256, D_MODEL), jnp.float32), 'W_DQ': jax.random.normal(ks[1], (D_MODEL, D_LATENT), jnp.float32) * s(D_MODEL), 'W_UQ': jax.random.normal(ks[2], (D_LATENT, N_HEADS * D_H), jnp.float32) * s(D_LATENT), 'W_QR': jax.random.normal(ks[3], (D_LATENT, N_HEADS * D_HR), jnp.float32) * s(D_LATENT), 'W_DKV': jax.random.normal(ks[4], (D_MODEL, D_LATENT), jnp.float32) * s(D_MODEL), 'W_UK': jax.random.normal(ks[5], (D_LATENT, N_HEADS * D_H), jnp.float32) * s(D_LATENT), 'W_UV': jax.random.normal(ks[6], (D_LATENT, N_HEADS * D_H), jnp.float32) * s(D_LATENT), 'W_KR': jax.random.normal(ks[7], (D_MODEL, D_HR), jnp.float32) * s(D_MODEL), 'W_O': jax.random.normal(ks[8], (N_HEADS * D_H, D_MODEL), jnp.float32) * s(N_HEADS * D_H)}
    _L0_attn_in = _L0_attn_setup()

    def _L0_ffn_setup():
        import jax, jax.numpy as jnp
        import numpy as np
        DIM = 128
        HID = 352
        E = 8
        TOP_K = 2
        EPS = 1e-06

        def _rmsnorm(x, w):
            var = jnp.mean(jnp.square(x), axis=-1, keepdims=True)
            return x * jax.lax.rsqrt(var + EPS) * w
        key = jax.random.key(seed)
        ks = jax.random.split(key, 5)
        x = jax.random.normal(ks[0], (4, 256, DIM), dtype=jnp.float32)
        norm_weight = jnp.ones((DIM,), dtype=jnp.float32)
        router_weight = jax.random.normal(ks[1], (E, DIM), dtype=jnp.float32) * 0.02
        gate_up_weight = jax.random.normal(ks[2], (E, 2 * HID, DIM), dtype=jnp.float32) * (0.02 / np.sqrt(E))
        down_weight = jax.random.normal(ks[3], (E, DIM, HID), dtype=jnp.float32) * (0.02 / np.sqrt(E))
        residual_alpha = jnp.float32(1.0)
        return {'x': x, 'norm_weight': norm_weight, 'router_weight': router_weight, 'gate_up_weight': gate_up_weight, 'down_weight': down_weight, 'residual_alpha': residual_alpha}
    _L0_ffn_in = _L0_ffn_setup()
    _L0_c = _w((lambda *s: np.random.randn(*s).astype(np.float32) * 0.05)(16, 128))
    _L0_wmod = _w((lambda *s: np.random.randn(*s).astype(np.float32) * 0.05)(128, 6 * 128) * 128 ** (-0.5))
    _d = {'L0_attn_x': _L0_attn_in['x'], 'L0_attn_W_DQ': _L0_attn_in['W_DQ'], 'L0_attn_W_UQ': _L0_attn_in['W_UQ'], 'L0_attn_W_QR': _L0_attn_in['W_QR'], 'L0_attn_W_DKV': _L0_attn_in['W_DKV'], 'L0_attn_W_UK': _L0_attn_in['W_UK'], 'L0_attn_W_UV': _L0_attn_in['W_UV'], 'L0_attn_W_KR': _L0_attn_in['W_KR'], 'L0_attn_W_O': _L0_attn_in['W_O'], 'L0_ffn_norm_weight': _L0_ffn_in['norm_weight'], 'L0_ffn_router_weight': _L0_ffn_in['router_weight'], 'L0_ffn_gate_up_weight': _L0_ffn_in['gate_up_weight'], 'L0_ffn_down_weight': _L0_ffn_in['down_weight'], 'L0_ffn_residual_alpha': _L0_ffn_in['residual_alpha'], 'L0_c': _L0_c, 'L0_wmod': _L0_wmod}
    _x0 = _d['L0_attn_x']
    _d['L0_attn_x'] = jax.random.normal(jax.random.fold_in(jax.random.key(seed), 1), (16, 256, 128), dtype=_x0.dtype)
    del _x0
    return _d

def reference(L0_attn_x, L0_attn_W_DQ, L0_attn_W_UQ, L0_attn_W_QR, L0_attn_W_DKV, L0_attn_W_UK, L0_attn_W_UV, L0_attn_W_KR, L0_attn_W_O, L0_ffn_norm_weight, L0_ffn_router_weight, L0_ffn_gate_up_weight, L0_ffn_down_weight, L0_ffn_residual_alpha, L0_c, L0_wmod):

    def _L0_attn_ref(x, W_DQ, W_UQ, W_QR, W_DKV, W_UK, W_UV, W_KR, W_O):
        import jax, jax.numpy as jnp
        import numpy as np
        D_MODEL, N_HEADS = (128, 16)
        D_H = D_MODEL // N_HEADS
        D_HR = D_H // 2
        D_LATENT = 32
        THETA = 10000.0

        def rope(x, theta=THETA):
            S, d = (x.shape[-2], x.shape[-1])
            inv = theta ** (-jnp.arange(0, d, 2, dtype=jnp.float32) / d)
            ang = jnp.arange(S, dtype=jnp.float32)[:, None] * inv
            cos, sin = (jnp.cos(ang), jnp.sin(ang))
            x1, x2 = (x[..., 0::2], x[..., 1::2])
            r1 = x1 * cos - x2 * sin
            r2 = x1 * sin + x2 * cos
            return jnp.stack([r1, r2], axis=-1).reshape(x.shape)
        B, S, _ = x.shape
        d_qk = D_H + D_HR
        c_q = x @ W_DQ
        Qc = (c_q @ W_UQ).reshape(B, S, N_HEADS, D_H).transpose(0, 2, 1, 3)
        Qr = (c_q @ W_QR).reshape(B, S, N_HEADS, D_HR).transpose(0, 2, 1, 3)
        Qr = rope(Qr)
        c_kv = x @ W_DKV
        Kc = (c_kv @ W_UK).reshape(B, S, N_HEADS, D_H).transpose(0, 2, 1, 3)
        Kr = rope((x @ W_KR)[:, None, :, :])
        Kr = jnp.broadcast_to(Kr, (B, N_HEADS, S, D_HR))
        V = (c_kv @ W_UV).reshape(B, S, N_HEADS, D_H).transpose(0, 2, 1, 3)
        Q = jnp.concatenate([Qc, Qr], axis=-1)
        K = jnp.concatenate([Kc, Kr], axis=-1)
        scores = jnp.einsum('bhqd,bhkd->bhqk', Q, K)
        scores = jnp.clip(scores, -80.0, 80.0)
        causal = jnp.tril(jnp.ones((S, S), dtype=bool))
        scores = jnp.where(causal, scores, -jnp.inf)
        weights = jax.nn.softmax(scores / jnp.sqrt(jnp.float32(d_qk)), axis=-1)
        attn = jnp.einsum('bhqk,bhkd->bhqd', weights, V)
        attn = attn.transpose(0, 2, 1, 3).reshape(B, S, N_HEADS * D_H)
        return attn @ W_O

    def _L0_ffn_ref(x, norm_weight, router_weight, gate_up_weight, down_weight, residual_alpha):
        import jax, jax.numpy as jnp
        import numpy as np
        DIM = 128
        HID = 352
        E = 8
        TOP_K = 2
        EPS = 1e-06

        def _rmsnorm(x, w):
            var = jnp.mean(jnp.square(x), axis=-1, keepdims=True)
            return x * jax.lax.rsqrt(var + EPS) * w
        normed = _rmsnorm(x, norm_weight)
        logits = jnp.einsum('bsd,ed->bse', normed, router_weight)
        probs = jax.nn.softmax(logits, axis=-1)
        topk_w, topk_idx = jax.lax.top_k(probs, TOP_K)
        topk_w = topk_w / jnp.sum(topk_w, axis=-1, keepdims=True)
        combine = jnp.sum(jax.nn.one_hot(topk_idx, E, dtype=normed.dtype) * topk_w[..., None], axis=-2)
        moe_out = jnp.zeros_like(x)
        for e in range(E):
            gu = jnp.einsum('bsd,hd->bsh', normed, gate_up_weight[e])
            gate, up = (gu[..., :HID], gu[..., HID:])
            hidden = jax.nn.silu(gate) * up
            out_e = jnp.einsum('bsh,dh->bsd', hidden, down_weight[e])
            moe_out = moe_out + combine[..., e, None] * out_e
        alpha = jnp.clip(residual_alpha, -0.5, 2.0)
        return x + alpha * moe_out
    x = L0_attn_x
    mod = (_silu(L0_c) @ L0_wmod).reshape(L0_c.shape[0], 6, 1, -1)
    sa, ca, ga, sb, cb, gb = (mod[:, 0], mod[:, 1], mod[:, 2], mod[:, 3], mod[:, 4], mod[:, 5])
    ga = (2 * (ga >= 0) - 1) * jnp.maximum(jnp.abs(ga), 0.25)
    gb = (2 * (gb >= 0) - 1) * jnp.maximum(jnp.abs(gb), 0.25)
    h = _layernorm(x, axis=-1) * (1 + ca) + sa
    x = x + ga * _L0_attn_ref(h, L0_attn_W_DQ, L0_attn_W_UQ, L0_attn_W_QR, L0_attn_W_DKV, L0_attn_W_UK, L0_attn_W_UV, L0_attn_W_KR, L0_attn_W_O)
    h = _layernorm(x, axis=-1) * (1 + cb) + sb
    x = x + gb * _L0_ffn_ref(h, L0_ffn_norm_weight, L0_ffn_router_weight, L0_ffn_gate_up_weight, L0_ffn_down_weight, L0_ffn_residual_alpha)
    return x

_drawn_inputs = setup_inputs


def setup_inputs(seed=0):
    import zlib

    import numpy as np

    out = dict(_drawn_inputs(seed))
    spreads = {'L0_ffn_norm_weight': (1.0, 0.6)}
    factors = {'L0_ffn_router_weight': 8.0, 'L0_ffn_gate_up_weight': 8.0, 'L0_ffn_down_weight': 8.0}
    for name, (base, spread) in spreads.items():
        noise = np.random.default_rng([zlib.crc32(name.encode()), seed]).standard_normal(out[name].shape)
        drawn = base * np.exp(spread * noise) if base else spread * noise
        out[name] = jnp.asarray(drawn.astype(out[name].dtype))
    for name, factor in factors.items():
        out[name] = (out[name] * factor).astype(out[name].dtype)
    return out
```

```python
import math

import numpy as np

import concourse.bass as bass
from concourse import mybir
from contextlib import ExitStack

B, S, D = 16, 256, 128
P = 128
T = S // P
H, DH, DR, DL = 16, 8, 4, 32
DQK = DH + DR
E, HID = 8, 352
HW = 3 * P
NT = B * T
NTOK = B * S
LN_EPS, RMS_EPS = 1e-5, 1e-6
SC = 1.0 / math.sqrt(DQK)
E_HI = float(np.exp(np.float32(80.0) * np.float32(SC)))
E_LO = float(np.exp(np.float32(-80.0) * np.float32(SC)))

HG = 8
QR = HG * DQK
NG = H // HG
COMBOS = [(0, 0), (0, 1), (1, 0), (0, 2), (2, 0), (1, 1)]
NC = len(COMBOS)
KST = 96
NPAIR = H // 2
VW = 32

QBLK = NTOK // P + 1
QROWS = QBLK * P
DUMMY = E * QBLK
NBLK = (2 * NTOK) // P + E - 1
PAYW = D + 2
PADID = 1 << 20

C_ID, C_UT, C_ONE, C_MASK, C_TRIG, C_SIGN = 0, 128, 256, 384, 512, 1024
C_IOTA = C_SIGN + NG * QR
C_BASE0 = C_IOTA + E
C_ID0 = C_BASE0 + E
C_BLK = C_ID0 + 4
C_PAD = C_BLK + NBLK
CW = C_PAD + PAYW
W_A, W_B, W_QA, W_QB, W_K, W_V, W_O, W_R = 0, 128, 256, 448, 640, 832, 960, 1088
W_NW, W_AL, W_CT, WW = 1096, 1097, 1098, 1114


def adaln_kernel(nc, x, consts, wsmall, wmod, gup, down, out):
    fp32, bf16 = mybir.dt.float32, mybir.dt.bfloat16
    i32, u32 = mybir.dt.int32, mybir.dt.uint32
    ALU, ACT, AX = mybir.AluOpType, mybir.ActivationFunctionType, mybir.AxisListType

    queue = nc.dram_tensor("queue", [(DUMMY + 1) * P, PAYW], fp32).ap()
    ydram = nc.dram_tensor("ydram", [2 * NTOK, D], fp32).ap()
    qdram = nc.dram_tensor("qdram", [2, 3, QR, NG * S], bf16).ap()
    kdram = nc.dram_tensor("kdram", [2, 3, QR, NG * S], bf16).ap()
    modrow = nc.dram_tensor("modrow", [B, 5 * D], fp32).ap()

    ctx = ExitStack()
    with ctx:
        def sb(name, shape, dt=fp32):
            return ctx.enter_context(nc.sbuf_tensor(name, shape, dt))

        def sem(name):
            return ctx.enter_context(nc.semaphore(name))

        cst = sb("cst", [P, CW])
        ws = sb("ws", [P, WW])
        wm = sb("wm", [P, 6 * D])
        xall = sb("xall", [P, NT * D])
        gu = sb("gu", [P, E * 2 * HID])
        dn = sb("dn", [P, E * 3 * D])
        ut_bf = sb("ut_bf", [P, P], bf16)
        one_bf = sb("one_bf", [P, P], bf16)
        mask4 = sb("mask4", [P, 4, P])
        st6 = sb("st6", [P, NT, 6])
        mean1 = sb("mean1", [P, NT])
        rstd1 = sb("rstd1", [P, NT])
        tmp1 = sb("tmp1", [P, 2, NT])
        mhalf = sb("mhalf", [P, NT])
        epst = sb("epst", [P, 2 * T])
        scT = sb("scT", [P, B])
        saT = sb("saT", [P, B])
        ca1T = sb("ca1T", [P, B])
        mrow = sb("mrow", [B, 5 * D])
        msgn = sb("msgn", [B, D])
        mabs = sb("mabs", [B, D])
        alpha = sb("alpha", [P, 1])
        bc = sb("bc", [P, 2, 4 * D])
        xn = sb("xn", [P, T * D])
        hT = sb("hT", [P, S])
        cc = sb("cc", [P, 2 * S])
        qs = sb("qs", [QR, 3, NG * S], bf16)
        ks = sb("ks", [QR, 3, NG * S], bf16)
        rq = sb("rq", [QR, NG * S])
        rk = sb("rk", [QR, NG * S])
        stq = sb("stq", [P, 2, H, S], bf16)
        stk = sb("stk", [P, 2, H, S], bf16)
        va = sb("va", [P, 2, T, H * VW])
        pt = sb("pt", [P, 4, 2, 512])
        ot = sb("ot", [P, 4, S])
        rden = sb("rden", [P, T, H])
        at = sb("at", [P, T, H * DH])
        aTs = sb("aTs", [P, S])
        wog = sb("wog", [P, D])
        st2 = sb("st2", [P, T, 6])
        mv2 = sb("mv2", [P, T, 2])
        ve2 = sb("ve2", [P, T])
        rstd2 = sb("rstd2", [P, T])
        t1 = sb("t1", [P, T, D])
        h2 = sb("h2", [P, T, D])
        gbh = sb("gbh", [P, T, D])
        h2Ts = sb("h2Ts", [P, S])
        sqj = sb("sqj", [P, D])
        ss = sb("ss", [P, T])
        ve3 = sb("ve3", [P, T])
        rstd3 = sb("rstd3", [P, T])
        pl = sb("pl", [P, 2, T, 2, PAYW])
        lg = sb("lg", [P, T, E])
        mx = sb("mx", [P, T, 8])
        mi = sb("mi", [P, T, 8], u32)
        mif = sb("mif", [P, T, 2])
        oh = sb("oh", [P, 2, T, 2, E])
        tot = sb("tot", [P, T * E], bf16)
        dif = sb("dif", [P, T])
        ex = sb("ex", [P, 2, T])
        den = sb("den", [P, T])
        base = sb("base", [P, E])
        pos = sb("pos", [P, T, E])
        pd = sb("pd", [P, T, 2, E])
        destf = sb("destf", [P, T * 2])
        dest = sb("dest", [P, 2, T * 2], u32)
        idf = sb("idf", [P, T * 2])

        SCB = [ctx.enter_context(nc.psum_tensor(f"SC{n}", [P, 2, 512], fp32)) for n in range(2)]
        OB, FA, FB, BK = (ctx.enter_context(nc.psum_tensor(n, [P, 512], fp32)) for n in ("OB", "FA", "FB", "BK"))

        ident = cst[:, C_ID:C_ID + P]

        names = """cst_in x_in ws_in wm_in w_in bc_in0 bc_in1 modrow_out dummy_out
            z_stack z_va z_half bf_ready mask_ready st6_ready mv1_ready rstd1_ready sil_ready mod_done modt_ready
            mod_step mrow_ready sign_ready stat_step base_init
            xn_ready xT_done hT_ready ab_done c_ready q_done k_done v_done q1_ready k1_ready rq_ready rk_ready
            q2_ready k2_ready q3_ready k3_ready v_ready stq0 stq1 stk0 stk1
            sc_done exp_done clip_done pv_done o_ready ot_done rden_ready norm_done at_done ats_ready wog_ready
            wo_done x2_ready st2_ready mv2_ready ve2_ready rstd2_ready t1_ready h2_ready h2t_done h2ts_ready
            ss_ready ve3_ready rstd3_ready pl_ready gbh_ready base_ready lg_done lg_ready mx_ready mi_ready
            mif_ready oh_ready tot_ready dif_ready ex_ready rank_done pos_ready bank_free pd_ready destf_ready
            den_ready q_out k_out dest_ready c0_ready id_ready scat0 scat1""".split()
        s = {n: sem(n) for n in names}
        stq_in, stk_in = [s["stq0"], s["stq1"]], [s["stk0"], s["stk1"]]
        bc_in, scat = [s["bc_in0"], s["bc_in1"]], [s["scat0"], s["scat1"]]
        DMA = 16

        def need(eng, sm, value):
            if isinstance(value, int) and value <= 0:
                return
            eng.wait_ge(sm, value)

        def apart(eng):
            eng.wait_ge(s["cst_in"], DMA)

        def schedule(eng, emit):
            emit(0, -1, True, False, False, False)
            emit(0, 0, True, True, False, False)
            emit(0, 1, True, True, True, False)
            emit(0, 2, True, True, True, True)
            emit(0, 3, True, True, True, True)
            with eng.Fori(2, 7) as j:
                emit(j, 0, True, True, True, True)
                emit(j, 1, True, True, True, True)
            emit(0, 14, True, True, True, True)
            emit(0, 15, False, True, True, True)
            emit(0, 16, False, False, True, True)
            emit(0, 17, False, False, False, True)

        def num(b):
            return 2 * b[0] + b[1]

        def par(b):
            return b[1] % 2

        def half(b):
            return b[0] + b[1] // 2

        def xtile(b, t=0, n=T):
            if isinstance(b[0], int):
                return slice((num(b) * T + t) * D, (num(b) * T + t + n) * D)
            return bass.ds(b[0] * (2 * T * D) + (b[1] * T + t) * D, n * D)

        def col(b, n=1):
            if isinstance(b[0], int):
                return slice(num(b) * n, num(b) * n + n)
            return bass.ds(b[0] * (2 * n) + b[1] * n, n)

        first = ExitStack()
        block = first.enter_context(nc.Block())

        @block.sync
        def _(sp):
            xv = x.rearrange("b (t p) d -> p (b t) d", p=P)
            xs = xall[:, :].rearrange("p (n d) -> p n d", d=D)
            sp.dma_start(ws[:, :], wsmall).then_inc(s["ws_in"], DMA)
            sp.dma_start(wm[:, :], wmod).then_inc(s["wm_in"], DMA)
            for n in range(4):
                sp.dma_start(xs[:, 8 * n:8 * n + 8, :], xv[:, 8 * n:8 * n + 8, :]).then_inc(s["x_in"], DMA)
            sp.dma_start(cst[:, :], consts).then_inc(s["cst_in"], DMA)
            sp.dma_start(gu[:, :], gup).then_inc(s["w_in"], DMA)
            sp.dma_start(dn[:, :], down).then_inc(s["w_in"], DMA)
            sp.wait_ge(s["mrow_ready"], 1)
            sp.dma_start(modrow, mrow[:, :]).then_inc(s["modrow_out"], DMA)
            sp.wait_ge(s["cst_in"], DMA)
            sp.dma_start(queue[DUMMY * P:(DUMMY + 1) * P, :], cst[:, C_PAD:C_PAD + PAYW]).then_inc(s["dummy_out"], DMA)
            sp.wait_ge(s["modrow_out"], DMA)
            sp.wait_ge(s["z_stack"], 4)

            def load_bc(a):
                need(sp, s["base_ready"], num(a) - 1)
                src = modrow[col(a), 0:4 * D].to_broadcast([P, 4 * D])
                sp.dma_start(bc[:, par(a), :], src).then_inc(bc_in[par(a)], DMA)

            def part_out(parts, dram, arrived, ready, written, f):
                apart(sp)
                for r in ready:
                    need(sp, s[r], num(f) + 1)
                need(sp, s["pv_done"], 4 * num(f) - 7)
                sp.dma_start(dram[par(f)].rearrange("s q n -> q s n"), parts[:, :, :]).then_inc(s[written], DMA)

            def stack(dram, dst, arrived, written, side, f):
                need(sp, s[written], DMA * num(f) + DMA)
                need(sp, s["sc_done"], NPAIR * num(f) - NPAIR)
                for n, combo in enumerate(COMBOS):
                    sp.dma_start(dst[n * DQK:(n + 1) * DQK, par(f), :, :],
                                 dram[par(f), combo[side]].rearrange("(r h) (g n) -> r (h g) n", h=HG, g=NG))\
                      .then_inc(arrived[par(f)], DMA)

            def emit(j, c, front, attn, back, route):
                f, a = (j, c + 1), (j, c)
                if attn:
                    load_bc(a)
                if front:
                    part_out(qs, qdram, stq_in, ("q1_ready", "q2_ready", "q3_ready"), "q_out", f)
                    part_out(ks, kdram, stk_in, ("k1_ready", "k2_ready", "k3_ready"), "k_out", f)
                    stack(qdram, stq, stq_in, "q_out", 0, f)
                    stack(kdram, stk, stk_in, "k_out", 1, f)

            schedule(sp, emit)

        @block.tensor
        def _(pe):
            mm = nc.tensor.matmul
            pe.wait_ge(s["sil_ready"], 1)
            pe.wait_ge(s["wm_in"], DMA)
            mm(FA[:, 0:B], wm[:, 0:D], scT[:, :], start=True, stop=True)
            mm(FA[:, B:2 * B], wm[:, D:2 * D], scT[:, :], start=True, stop=True)
            mm(FB[0:B, 0:4 * D], scT[:, :], wm[:, 2 * D:6 * D], start=True, stop=True).then_inc(s["mod_done"], 1)
            pe.wait_ge(s["cst_in"], DMA)
            pe.wait_ge(s["modt_ready"], 1)
            pe.wait_ge(s["mrow_ready"], 1)
            pe.wait_ge(s["sign_ready"], 1)
            pe.wait_ge(s["z_stack"], 4)
            pe.wait_ge(s["z_va"], 1)
            pe.wait_ge(s["bf_ready"], 2)

            def scores(a, p):
                if p == 0:
                    need(pe, stq_in[par(a)], (half(a) + 1) * (DMA * NC))
                    need(pe, stk_in[par(a)], (half(a) + 1) * (DMA * NC))
                need(pe, s["exp_done"], NPAIR * num(a) + (p - 1))
                for hh in range(2):
                    h = 2 * p + hh
                    dst = SCB[p % 2][:, hh, :]
                    mm(dst[:, 0:S], stk[0:KST, par(a), h, 0:P], stq[0:KST, par(a), h, 0:S], start=True, stop=True)
                    last = mm(dst[:, S:S + P], stk[0:KST, par(a), h, P:S], stq[0:KST, par(a), h, P:S],
                              start=True, stop=True)
                last.then_inc(s["sc_done"], 1)

            def values(a, g):
                need(pe, s["clip_done"], NPAIR * num(a) + (2 * g + 2))
                if g == 0:
                    need(pe, s["v_ready"], num(a) + 1)
                if g % 2 == 0:
                    need(pe, s["o_ready"], 2 * num(a) + g // 2)
                for kt in range(T):
                    for n in range(4):
                        h = 4 * g + n
                        src = pt[:, (h // 2) % 4, h % 2, 0:S] if kt == 0 else pt[:, (h // 2) % 4, h % 2, S:S + P]
                        last = mm(OB[VW * n:VW * n + VW, (g % 2) * S + kt * P:(g % 2) * S + S],
                                  va[:, par(a), kt, h * VW:(h + 1) * VW], src, start=(kt == 0), stop=(kt == 1))
                last.then_inc(s["pv_done"], 1)

            def emit(j, c, front, attn, back, route):
                f, a, r, q = (j, c + 1), (j, c), (j, c - 1), (j, c - 2)
                if attn:
                    scores(a, 0)
                if route:
                    need(pe, s["tot_ready"], num(q) + 1)
                    R = BK[:, 256:256 + 3 * E]
                    mm(R[:, 0:E], ut_bf[:, :], tot[:, 0:E], start=True, stop=True)
                    mm(R[:, E:2 * E], ut_bf[:, :], tot[:, E:2 * E], start=True, stop=False)
                    mm(R[:, E:2 * E], one_bf[:, :], tot[:, 0:E], start=False, stop=True)
                    mm(R[:, 2 * E:3 * E], one_bf[:, :], tot[:, 0:E], start=True, stop=False)
                    mm(R[:, 2 * E:3 * E], one_bf[:, :], tot[:, E:2 * E], start=False, stop=True)\
                        .then_inc(s["rank_done"], 1)
                if attn:
                    scores(a, 1)
                if front:
                    need(pe, s["xn_ready"], num(f) + 1)
                    need(pe, s["k1_ready"], num(f))
                    need(pe, s["rk_ready"], num(f))
                    for t in range(T):
                        last = nc.tensor.transpose(FA[:, t * P:(t + 1) * P], xn[:, t * D:(t + 1) * D], ident)
                    last.then_inc(s["xT_done"], 1)
                if back:
                    values(r, 3)
                if attn:
                    scores(a, 2)
                if front:
                    need(pe, s["hT_ready"], num(f) + 1)
                    mm(FA[:, 0:S], ws[:, W_A:W_A + P], hT[:, :], start=True, stop=True)
                    mm(FA[:, S:2 * S], ws[:, W_B:W_B + P], hT[:, :], start=True, stop=True)\
                        .then_inc(s["ab_done"], 1)
                if back:
                    need(pe, s["o_ready"], 2 * num(r) + 2)
                    need(pe, s["bank_free"], num(r))
                    if attn:
                        need(pe, s["v_ready"], num(a) + 1)
                    for t in range(T):
                        for g in range(4):
                            last = nc.tensor.transpose((BK, FB)[t][:, g * P:(g + 1) * P],
                                                       ot[:, g, t * P:(t + 1) * P], ident)
                    last.then_inc(s["ot_done"], 1)
                if attn:
                    scores(a, 3)
                    values(a, 0)
                if back:
                    need(pe, s["norm_done"], num(r) + 1)
                    for t in range(T):
                        last = nc.tensor.transpose(BK[:, t * P:(t + 1) * P], at[:, t, :], ident)
                    last.then_inc(s["at_done"], 1)
                if front:
                    need(pe, s["c_ready"], num(f) + 1)
                    need(pe, s["v_ready"], num(f))
                    for g in range(NG):
                        mm(FB[0:QR, g * S:(g + 1) * S], ws[:, W_QA + g * QR:W_QA + (g + 1) * QR], cc[:, 0:S],
                           start=True, stop=False)
                        last = mm(FB[0:QR, g * S:(g + 1) * S], ws[:, W_QB + g * QR:W_QB + (g + 1) * QR],
                                  cc[:, S:2 * S], start=False, stop=True)
                    last.then_inc(s["q_done"], 1)
                if attn:
                    scores(a, 4)
                if front:
                    for g in range(NG):
                        last = mm(FA[0:QR, g * S:(g + 1) * S], ws[:, W_K + g * QR:W_K + (g + 1) * QR],
                                  cc[:, S:2 * S], start=True, stop=True)
                    last.then_inc(s["k_done"], 1)
                if back:
                    need(pe, s["ats_ready"], num(r) + 1)
                    need(pe, s["wog_ready"], num(r) + 1)
                    for t in range(T):
                        last = mm(BK[:, S + t * D:S + (t + 1) * D], aTs[:, t * P:(t + 1) * P], wog[:, :],
                                  start=True, stop=True)
                    last.then_inc(s["wo_done"], 1)
                if attn:
                    scores(a, 5)
                    values(a, 1)
                if front:
                    need(pe, s["q1_ready"], num(f) + 1)
                    need(pe, s["rq_ready"], num(f) + 1)
                    for t in range(T):
                        last = mm(FB[:, t * P:(t + 1) * P], cc[:, S + t * P:S + (t + 1) * P],
                                  ws[:, W_V:W_V + P], start=True, stop=True)
                    last.then_inc(s["v_done"], 1)
                if attn:
                    scores(a, 6)
                if back:
                    need(pe, s["h2_ready"], num(r) + 1)
                    for t in range(T):
                        last = nc.tensor.transpose(BK[:, t * P:(t + 1) * P], h2[:, t, :], ident)
                    last.then_inc(s["h2t_done"], 1)
                if attn:
                    scores(a, 7)
                    values(a, 2)
                if back:
                    need(pe, s["h2ts_ready"], num(r) + 1)
                    for t in range(T):
                        last = mm(BK[:, S + t * E:S + (t + 1) * E], h2Ts[:, t * P:(t + 1) * P],
                                  ws[:, W_R:W_R + E], start=True, stop=True)
                    last.then_inc(s["lg_done"], 1)

            schedule(pe, emit)

        @block.scalar
        def _(act):
            af = nc.scalar.activation
            act.wait_ge(s["ws_in"], DMA)
            af(scT[:, :], ws[:, W_CT:W_CT + B], ACT.Silu).then_inc(s["sil_ready"], 1)
            act.wait_ge(s["modt_ready"], 1)

            def exps(a, p):
                need(act, s["sc_done"], NPAIR * num(a) + (p + 1))
                need(act, s["pv_done"], 4 * num(a) + (p // 2 - 1))
                af(pt[:, p % 4, :, 0:S + P], SCB[p % 2][:, :, 0:S + P], ACT.Exp, scale=SC)\
                    .then_inc(s["exp_done"], 1)

            def copy_out(a, hf):
                need(act, s["pv_done"], 4 * num(a) + (2 * hf + 2))
                need(act, s["ot_done"], num(a))
                af(ot[:, 2 * hf:2 * hf + 2, :].rearrange("p g n -> p (g n)"), OB[:, :], ACT.Copy)\
                    .then_inc(s["o_ready"], 1)

            def emit(j, c, front, attn, back, route):
                f, a, r, q = (j, c + 1), (j, c), (j, c - 1), (j, c - 2)
                if attn:
                    exps(a, 0)
                    exps(a, 1)
                if front:
                    need(act, s["xT_done"], num(f) + 1)
                    need(act, s["ab_done"], num(f))
                    af(hT[:, :], FA[:, 0:S], ACT.Identity, scale=ca1T[:, col(f)], bias=saT[:, col(f)])\
                        .then_inc(s["hT_ready"], 1)
                if back:
                    copy_out(r, 1)
                if attn:
                    exps(a, 2)
                    exps(a, 3)
                if back:
                    need(act, s["at_done"], num(r) + 1)
                    need(act, s["wo_done"], num(r))
                    af(aTs[:, :], BK[:, 0:S], ACT.Copy).then_inc(s["ats_ready"], 1)
                if front:
                    need(act, s["q_done"], num(f) + 1)
                    need(act, s["q_out"], DMA * num(f))
                    af(qs[:, 0, :], FB[0:QR, :], ACT.Copy).then_inc(s["q1_ready"], 1)
                if attn:
                    exps(a, 4)
                if front:
                    need(act, s["k_done"], num(f) + 1)
                    need(act, s["k_out"], DMA * num(f))
                    af(ks[:, 0, :], FA[0:QR, :], ACT.Copy).then_inc(s["k1_ready"], 1)
                if attn:
                    exps(a, 5)
                if front:
                    need(act, s["rq_ready"], num(f) + 1)
                    af(qs[:, 1, :], rq[:, :], ACT.Copy).then_inc(s["q2_ready"], 1)
                    need(act, s["rk_ready"], num(f) + 1)
                    af(ks[:, 1, :], rk[:, :], ACT.Copy).then_inc(s["k2_ready"], 1)
                    need(act, s["v_done"], num(f) + 1)
                    need(act, s["pv_done"], 4 * num(f) - 4)
                    af(va[:, par(f), :, :].rearrange("p t (h v) -> p (t h) v", v=VW)[:, :, 0:DH],
                       FB[:, 0:S].rearrange("p (n v) -> p n v", v=DH), ACT.Copy).then_inc(s["v_ready"], 1)
                if attn:
                    exps(a, 6)
                    copy_out(a, 0)
                if back:
                    need(act, s["h2t_done"], num(r) + 1)
                    need(act, s["lg_done"], num(r))
                    af(h2Ts[:, :], BK[:, 0:S], ACT.Copy).then_inc(s["h2ts_ready"], 1)
                    need(act, s["ve3_ready"], num(r))
                    for t in range(T):
                        need(act, s["ss_ready"], 2 * num(r) + t)
                        af(sqj[:, :], h2[:, t, :], ACT.Square, scale=D ** -0.5, accum_out=ss[:, t:t + 1]).then_inc(s["ss_ready"], 1)
                if attn:
                    exps(a, 7)
                if back:
                    need(act, s["rstd3_ready"], num(r) + 1)
                    need(act, scat[par(r)], half(r) * (DMA * 4))
                    for t in range(T):
                        last = af(pl[:, par(r), t, :, 0:D], h2[:, t:t + 1, :].to_broadcast([P, 2, D]), ACT.Copy,
                                  scale=rstd3[:, t:t + 1])
                    last.then_inc(s["pl_ready"], 1)
                    need(act, s["dif_ready"], num(r) + 1)
                    af(ex[:, par(r), :], dif[:, :], ACT.Exp).then_inc(s["ex_ready"], 1)

            schedule(act, emit)

        @block.vector
        def _(dve):
            V = nc.vector
            tt, ts, stt, cp = V.tensor_tensor, V.tensor_scalar, V.scalar_tensor_tensor, V.tensor_copy
            dve.wait_ge(s["mod_done"], 1)
            cp(saT[:, :], FA[:, 0:B])
            ts(ca1T[:, :], FA[:, B:2 * B], 1.0, None, ALU.add).then_inc(s["modt_ready"], 1)
            dve.wait_ge(s["ws_in"], DMA)
            ts(alpha[:, :], ws[:, W_AL:W_AL + 1], -0.5, 2.0, ALU.max, ALU.min).then_inc(s["mod_step"], 1)
            ts(mrow[:, D:2 * D], FB[0:B, 2 * D:3 * D], 1.0, None, ALU.add)
            cp(mrow[:, 2 * D:3 * D], FB[0:B, D:2 * D])
            step = 1
            for src, dst in ((0, 0), (3, 3)):
                g_in = FB[0:B, src * D:(src + 1) * D]
                dve.wait_ge(s["mod_step"], step)
                ts(msgn[:, :], g_in, 0.0, 0.5, ALU.is_ge, ALU.subtract)
                ts(mabs[:, :], g_in, -2.0, None, ALU.mult).then_inc(s["mod_step"], 1)
                dve.wait_ge(s["mod_step"], step + 1)
                stt(out=mabs[:, :], in0=g_in, scalar=2.0, in1=mabs[:, :], op0=ALU.mult, op1=ALU.max)\
                    .then_inc(s["mod_step"], 1)
                dve.wait_ge(s["mod_step"], step + 2)
                stt(out=mrow[:, dst * D:(dst + 1) * D], in0=mabs[:, :], scalar=0.5, in1=msgn[:, :],
                    op0=ALU.max, op1=ALU.mult).then_inc(s["mod_step"], 1)
                step += 3
            dve.wait_ge(s["mod_step"], step)
            ts(mrow[:, 4 * D:5 * D], mrow[:, 3 * D:4 * D], alpha[0:B, :], None, ALU.mult).then_inc(s["mrow_ready"], 1)
            dve.wait_ge(s["cst_in"], DMA)
            cp(ut_bf[:, :], cst[:, C_UT:C_UT + P]).then_inc(s["bf_ready"], 1)
            cp(one_bf[:, :], cst[:, C_ONE:C_ONE + P]).then_inc(s["bf_ready"], 1)
            for n in range(4):
                cp(mask4[:, n, :], cst[:, C_MASK:C_MASK + P]).then_inc(s["mask_ready"], 1)
            tt(ws[:, W_QA:W_QA + NG * QR], ws[:, W_QA:W_QA + NG * QR], cst[:, C_SIGN:C_SIGN + NG * QR], ALU.mult)
            ts(ws[:, W_R:W_R + E], ws[:, W_R:W_R + E], ws[:, W_NW:W_NW + 1], None, ALU.mult)\
                .then_inc(s["sign_ready"], 1)
            cp(base[:, :], cst[:, C_BASE0:C_BASE0 + E])
            cp(idf[:, :], cst[:, C_ID0:C_ID0 + 2 * T]).then_inc(s["base_init"], 1)
            dve.wait_ge(s["x_in"], 4 * DMA)
            with dve.Fori(0, NT // 8) as m:
                for n in range(8):
                    V.bn_stats(st6[:, bass.ds(m * 8 + n, 1), :].rearrange("p a b -> p (a b)"),
                               xall[:, bass.ds(m * (8 * D) + n * D, D)]).then_inc(s["st6_ready"], 1)
            dve.wait_ge(s["st6_ready"], NT)
            tt(mean1[:, :], st6[:, :, 1], st6[:, :, 4], ALU.add)
            tt(tmp1[:, 0, :], st6[:, :, 1], st6[:, :, 4], ALU.subtract)
            tt(tmp1[:, 1, :], st6[:, :, 2], st6[:, :, 5], ALU.add).then_inc(s["stat_step"], 1)
            dve.wait_ge(s["stat_step"], 1)
            ts(mean1[:, :], mean1[:, :], 0.5, None, ALU.mult)
            tt(tmp1[:, 0, :], tmp1[:, 0, :], tmp1[:, 0, :], ALU.mult)
            ts(tmp1[:, 1, :], tmp1[:, 1, :], 1.0 / D, LN_EPS, ALU.mult, ALU.add).then_inc(s["stat_step"], 1)
            dve.wait_ge(s["stat_step"], 2)
            stt(out=tmp1[:, 1, :], in0=tmp1[:, 0, :], scalar=0.25, in1=tmp1[:, 1, :], op0=ALU.mult, op1=ALU.add)\
                .then_inc(s["mv1_ready"], 1)
            dve.wait_ge(s["rstd1_ready"], 1)

            def clip(a, p):
                need(dve, s["exp_done"], NPAIR * num(a) + (p + 1))
                diag = pt[:, p % 4, :, :].rearrange("p h (n c) -> p (h n) c", c=2 * P)[:, :, 0:P]
                stt(out=diag, in0=diag, scalar=E_LO, in1=mask4[:, :, :], op0=ALU.max, op1=ALU.min)
                off = pt[:, p % 4, :, P:2 * P]
                ts(off, off, E_LO, E_HI, ALU.max, ALU.min).then_inc(s["clip_done"], 1)

            def emit(j, c, front, attn, back, route):
                f, a, r, q = (j, c + 1), (j, c), (j, c - 1), (j, c - 2)
                if front:
                    need(dve, s["xT_done"], num(f))
                    for t in range(T):
                        cols = slice(num(f) * T + t, num(f) * T + t + 1) if isinstance(j, int) else \
                            bass.ds(j * (2 * T) + (c + 1) * T + t, 1)
                        last = ts(xn[:, t * D:(t + 1) * D], xall[:, xtile(f, t, 1)], mean1[:, cols], rstd1[:, cols],
                                  ALU.subtract, ALU.mult)
                    last.then_inc(s["xn_ready"], 1)
                if attn:
                    clip(a, 0)
                if route:
                    need(dve, s["rank_done"], num(q) + 1)
                    rank = BK[:, 256:256 + 3 * E]
                    tt(pos[:, :, :], rank[:, 0:T * E].rearrange("p (t e) -> p t e", e=E),
                       base[:, :].rearrange("p (o e) -> p o e", o=1).to_broadcast([P, T, E]), ALU.add)\
                        .then_inc(s["pos_ready"], 1)
                    need(dve, s["ex_ready"], num(q) + 1)
                    need(dve, s["dest_ready"], num(q))
                    ts(den[:, :], ex[:, par(q), :], 1.0, None, ALU.add).then_inc(s["den_ready"], 1)
                    need(dve, s["pos_ready"], num(q) + 1)
                    tt(base[:, :], rank[:, 2 * E:3 * E], base[:, :], ALU.add).then_inc(s["bank_free"], 1)
                    ohq = oh[:, par(q), :, :, :]
                    for t in range(T):
                        last = tt(pd[:, t, :, :], ohq[:, t, :, :],
                                  pos[:, t:t + 1, :].to_broadcast([P, 2, E]), ALU.mult)
                    last.then_inc(s["pd_ready"], 1)
                    need(dve, s["pl_ready"], num(q) + 1)
                    need(dve, s["den_ready"], num(q) + 1)
                    V.reciprocal(pl[:, par(q), :, 0, D], den[:, :]).then_inc(s["c0_ready"], 1)
                if attn:
                    clip(a, 1)
                if route:
                    need(dve, s["pd_ready"], num(q) + 1)
                    V.tensor_reduce(destf[:, :], pd[:, :, :, :].rearrange("p t k e -> p (t k) e"), AX.X, ALU.add)\
                        .then_inc(s["destf_ready"], 1)
                    need(dve, s["c0_ready"], num(q) + 1)
                    tt(pl[:, par(q), :, 1, D], ex[:, par(q), :], pl[:, par(q), :, 0, D], ALU.mult)
                    cp(pl[:, par(q), :, :, D + 1].bitcast(i32), idf[:, :].rearrange("p (t k) -> p t k", k=2))\
                        .then_inc(s["id_ready"], 1)
                    need(dve, s["destf_ready"], num(q) + 1)
                    cp(dest[:, par(q), :], destf[:, :]).then_inc(s["dest_ready"], 1)
                    need(dve, s["id_ready"], num(q) + 1)
                    ts(idf[:, :], idf[:, :], float(S), None, ALU.add).then_inc(s["base_init"], 1)
                if attn:
                    clip(a, 2)
                if front:
                    need(dve, s["ab_done"], num(f) + 1)
                    need(dve, s["v_done"], num(f))
                    tt(cc[:, :], FA[:, :], cst[:, C_TRIG:C_TRIG + 2 * S], ALU.mult).then_inc(s["c_ready"], 1)
                if back:
                    need(dve, s["ot_done"], num(r) + 1)
                    need(dve, s["at_done"], num(r))
                    for t in range(T):
                        last = V.reciprocal(rden[:, t, :], (BK, FB)[t][:, :].rearrange("p (h v) -> p h v", v=VW)[:, :, DH])
                    last.then_inc(s["rden_ready"], 1)
                    need(dve, s["rden_ready"], num(r) + 1)
                    for t in range(T):
                        last = tt(at[:, t, :].rearrange("p (h v) -> p h v", v=DH),
                                  (BK, FB)[t][:, :].rearrange("p (h v) -> p h v", v=VW)[:, :, 0:DH],
                                  rden[:, t, :].rearrange("p (h o) -> p h o", o=1).to_broadcast([P, H, DH]), ALU.mult)
                    last.then_inc(s["norm_done"], 1)
                if attn:
                    clip(a, 3)
                if front:
                    need(dve, s["q1_ready"], num(f) + 1)
                    need(dve, s["q2_ready"], num(f))
                    need(dve, s["q3_ready"], num(f))
                    tt(rq[:, :], FB[0:QR, :], qs[:, 0, :], ALU.subtract).then_inc(s["rq_ready"], 1)
                if attn:
                    clip(a, 4)
                if front:
                    need(dve, s["k1_ready"], num(f) + 1)
                    need(dve, s["k2_ready"], num(f))
                    need(dve, s["k3_ready"], num(f))
                    tt(rk[:, :], FA[0:QR, :], ks[:, 0, :], ALU.subtract).then_inc(s["rk_ready"], 1)
                if back:
                    need(dve, s["wo_done"], num(r) + 1)
                    tt(xall[:, xtile(r)], BK[:, S:S + T * D], xall[:, xtile(r)], ALU.add).then_inc(s["x2_ready"], 1)
                    apart(dve)
                    need(dve, s["x2_ready"], num(r) + 1)
                    for t in range(T):
                        last = V.bn_stats(st2[:, t, :], xall[:, xtile(r, t, 1)])
                    last.then_inc(s["st2_ready"], 1)
                if attn:
                    clip(a, 5)
                if back:
                    apart(dve)
                    need(dve, s["st2_ready"], num(r) + 1)
                    need(dve, s["ve2_ready"], num(r))
                    for t in range(T):
                        last = V.bn_aggr(mv2[:, t, :], st2[:, t, :])
                    last.then_inc(s["mv2_ready"], 1)
                    need(dve, s["mv2_ready"], num(r) + 1)
                    need(dve, bc_in[par(r)], (half(r) + 1) * DMA)
                    need(dve, s["pl_ready"], num(r))
                    need(dve, s["gbh_ready"], num(r))
                    for t in range(T):
                        last = stt(out=t1[:, t, :], in0=xall[:, xtile(r, t, 1)], scalar=mv2[:, t, 0:1],
                                   in1=bc[:, par(r), D:2 * D], op0=ALU.subtract, op1=ALU.mult)
                    last.then_inc(s["t1_ready"], 1)
                    need(dve, s["t1_ready"], num(r) + 1)
                    need(dve, s["rstd2_ready"], num(r) + 1)
                    for t in range(T):
                        last = stt(out=h2[:, t, :], in0=t1[:, t, :], scalar=rstd2[:, t:t + 1],
                                   in1=bc[:, par(r), 2 * D:3 * D], op0=ALU.mult, op1=ALU.add)
                    last.then_inc(s["h2_ready"], 1)
                if attn:
                    clip(a, 6)
                    clip(a, 7)
                if back:
                    need(dve, s["lg_done"], num(r) + 1)
                    need(dve, s["rstd3_ready"], num(r) + 1)
                    for t in range(T):
                        last = ts(lg[:, t, :], BK[:, S + t * E:S + (t + 1) * E], rstd3[:, t:t + 1], None, ALU.mult)
                    last.then_inc(s["lg_ready"], 1)
                    apart(dve)
                    need(dve, s["lg_ready"], num(r) + 1)
                    for t in range(T):
                        last = V.max(mx[:, t, :], lg[:, t, :])
                    last.then_inc(s["mx_ready"], 1)
                    apart(dve)
                    need(dve, s["mx_ready"], num(r) + 1)
                    for t in range(T):
                        last = V.max_index(mi[:, t, :], mx[:, t, :], lg[:, t, :])
                    last.then_inc(s["mi_ready"], 1)
                    need(dve, s["ex_ready"], num(r))
                    tt(dif[:, :], mx[:, :, 1], mx[:, :, 0], ALU.subtract).then_inc(s["dif_ready"], 1)
                    need(dve, s["mi_ready"], num(r) + 1)
                    cp(mif[:, :, :], mi[:, :, 0:2]).then_inc(s["mif_ready"], 1)
                    need(dve, s["mif_ready"], num(r) + 1)
                    ohr = oh[:, par(r), :, :, :]
                    for t in range(T):
                        last = tt(ohr[:, t, :, :],
                                  cst[:, C_IOTA:C_IOTA + E].rearrange("p (o e) -> p o e", o=1).to_broadcast([P, 2, E]),
                                  mif[:, t, :].rearrange("p (k o) -> p k o", o=1).to_broadcast([P, 2, E]), ALU.is_equal)
                    last.then_inc(s["oh_ready"], 1)
                    need(dve, s["oh_ready"], num(r) + 1)
                    need(dve, s["rank_done"], num(r))
                    tt(tot[:, :].rearrange("p (t e) -> p t e", e=E), ohr[:, :, 0, :], ohr[:, :, 1, :], ALU.add)\
                        .then_inc(s["tot_ready"], 1)

            schedule(dve, emit)

        @block.gpsimd
        def _(pool):
            G = nc.gpsimd
            for st in (stq, stk):
                for par_ in range(2):
                    G.memset(st[64:KST, par_, :, :], 0.0).then_inc(s["z_stack"], 1)
            pool.wait_ge(s["z_stack"], 4)
            G.memset(epst[:, 0:T], LN_EPS)
            G.memset(epst[:, T:2 * T], RMS_EPS)
            G.memset(mhalf[:, :], -0.5).then_inc(s["z_half"], 1)
            G.memset(va[:, :, :, :], 1.0).then_inc(s["z_va"], 1)
            pool.wait_ge(s["z_half"], 1)
            pool.wait_ge(s["mv1_ready"], 1)
            G.tensor_tensor(rstd1[:, :], tmp1[:, 1, :], mhalf[:, :], ALU.pow).then_inc(s["rstd1_ready"], 1)

            def emit(j, c, front, attn, back, route):
                f, a, r, q = (j, c + 1), (j, c), (j, c - 1), (j, c - 2)
                if back:
                    need(pool, bc_in[par(r)], (half(r) + 1) * DMA)
                    need(pool, s["wo_done"], num(r))
                    G.tensor_tensor(wog[:, :], ws[:, W_O:W_O + D], bc[:, par(r), 0:D], ALU.mult)\
                        .then_inc(s["wog_ready"], 1)
                if route:
                    apart(pool)
                    need(pool, s["dest_ready"], num(q) + 1)
                    need(pool, s["pl_ready"], num(q) + 1)
                    for t in range(T):
                        for k in range(2):
                            G.indirect_dma_start(
                                queue, bass.IndirectOffsetOnAxis(dest[:, par(q), 2 * t + k:2 * t + k + 1], 0),
                                pl[:, par(q), t, k, :], None).then_inc(scat[par(q)], DMA)
                if front:
                    need(pool, s["q2_ready"], num(f) + 1)
                    G.tensor_tensor(qs[:, 2, :], rq[:, :], qs[:, 1, :], ALU.subtract).then_inc(s["q3_ready"], 1)
                    need(pool, s["k2_ready"], num(f) + 1)
                    G.tensor_tensor(ks[:, 2, :], rk[:, :], ks[:, 1, :], ALU.subtract).then_inc(s["k3_ready"], 1)
                if back:
                    need(pool, s["mv2_ready"], num(r) + 1)
                    G.tensor_tensor(ve2[:, :], mv2[:, :, 1], epst[:, 0:T], ALU.add).then_inc(s["ve2_ready"], 1)
                    need(pool, s["ve2_ready"], num(r) + 1)
                    need(pool, s["h2_ready"], num(r))
                    G.tensor_tensor(rstd2[:, :], ve2[:, :], mhalf[:, 0:T], ALU.pow).then_inc(s["rstd2_ready"], 1)
                    need(pool, s["ss_ready"], 2 * num(r) + 2)
                    G.tensor_tensor(ve3[:, :], ss[:, :], epst[:, T:2 * T], ALU.add)\
                        .then_inc(s["ve3_ready"], 1)
                    need(pool, s["ve3_ready"], num(r) + 1)
                    need(pool, s["lg_ready"], num(r))
                    need(pool, s["pl_ready"], num(r))
                    G.tensor_tensor(rstd3[:, :], ve3[:, :], mhalf[:, 0:T], ALU.pow).then_inc(s["rstd3_ready"], 1)
                    for t in range(T):
                        last = G.tensor_tensor(gbh[:, t, :], h2[:, t, :], bc[:, par(r), 3 * D:4 * D], ALU.mult)
                    last.then_inc(s["gbh_ready"], 1)
                    need(pool, s["gbh_ready"], num(r) + 1)
                    G.tensor_tensor(xall[:, xtile(r)], xall[:, xtile(r)], gbh[:, :, :].rearrange("p t d -> p (t d)"),
                                    ALU.add).then_inc(s["base_ready"], 1)

            schedule(pool, emit)

        first.close()

        block = ctx.enter_context(nc.Block())
        NE1 = E - 1
        XBUF = 8
        UNR2 = XBUF
        M0, M1 = 2, (NBLK - 2) // UNR2

        cnt = sb("cnt", [P, E])
        cnti = sb("cnti", [P, E], i32)
        nbf = sb("nbf", [P, E])
        bend = sb("bend", [P, E])
        padi = sb("padi", [1, E], i32)
        wrow = sb("wrow", [P, E])
        ge = sb("ge", [1, NBLK, E])
        gw = sb("gw", [1, NBLK, NE1])
        bf_ = sb("bf_", [1, 3, NBLK])
        bi = sb("bi", [1, 2, NBLK], i32)
        xb = sb("xb", [P, XBUF, PAYW])
        xTs = sb("xTs", [P, 2, P])
        sg = sb("sg", [P, 2, HID])
        hid = sb("hid", [P, 2, HW])
        hTs = sb("hTs", [P, 2, HW])
        ysb = sb("ysb", [P, XBUF, D])
        gba = sb("gba", [P, B, D])
        NCH = 8
        TCH = NT // NCH
        ybuf = [st[:, :, :, :].rearrange("p a h n -> p (a h n)").bitcast(fp32) for st in (stq, stk)]
        GUB, HB, XP, YP = SCB, (OB, FA), FB, BK

        names2 = """table_step table_ready pad_ready padded gu_ready gba_in xt_done xts_ready gu_done
            sg_ready hid_ready z_hid ht_done hts_ready y_done y_ready yin0 yin1 yin2 yin3 yin4 yin5 yin6 yin7
            sum1 sum2 sum3 out_done""".split()
        s.update({n: sem(n) for n in names2})
        xb_in = [sem(f"xb_in{n}") for n in range(XBUF)]
        yscat = [sem(f"yscat{n}") for n in range(XBUF)]

        def nb_(k):
            return UNR2 * k[0] + k[1]

        def slot(k):
            return k[1] % XBUF

        def uses(k):
            return k[0] + k[1] // XBUF

        def at_block(k):
            return slice(nb_(k), nb_(k) + 1) if isinstance(k[0], int) else bass.ds(k[0] * UNR2 + k[1], 1)

        def block_steps(eng, step):
            step((0, -2), True, False, False, False)
            step((0, -1), True, True, False, False)
            step((0, 0), True, True, True, False)
            for n in range(1, M0 * UNR2):
                step((0, n), True, True, True, True)
            with eng.Fori(M0, M1) as m:
                for n in range(UNR2):
                    step((m, n), True, True, True, True)
            for n in range(M1 * UNR2, NBLK - 2):
                step((0, n), True, True, True, True)
            step((0, NBLK - 2), False, True, True, True)
            step((0, NBLK - 1), False, False, True, True)
            step((0, NBLK), False, False, False, True)

        def plus(k, n):
            return (k[0], k[1] + n)

        @block.sync
        def _(sp):
            sp.wait_ge(s["pad_ready"], 1)
            for e in range(E):
                row = sp.value_load(padi[0:1, e:e + 1], min_val=0, max_val=DUMMY * P - P)
                sp.dma_start(queue[bass.ds(row, P), :], cst[:, C_PAD:C_PAD + PAYW]).then_inc(s["padded"], DMA)
            sp.wait_ge(scat[0], B // 2 * 4 * DMA)
            sp.wait_ge(scat[1], B // 2 * 4 * DMA)
            sp.wait_ge(s["dummy_out"], DMA)
            sp.wait_ge(s["padded"], E * DMA)
            sp.wait_ge(s["table_ready"], 1)

            def load(b):
                apart(sp)
                need(sp, yscat[slot(b)], uses(b) * DMA)
                row = sp.value_load(bi[0:1, 1, at_block(b)], min_val=0, max_val=DUMMY * P)
                sp.dma_start(xb[:, slot(b), :], queue[bass.ds(row, P), :]).then_inc(xb_in[slot(b)], DMA)

            for n in range(UNR2):
                load((0, n))
            gb_rows = modrow[:, 4 * D:5 * D].rearrange("(o b) d -> o b d", o=1)
            sp.dma_start(gba[:, :, :], gb_rows.to_broadcast([P, B, D])).then_inc(s["gba_in"], DMA)
            with sp.Fori(1, M1) as m:
                for n in range(UNR2):
                    load((m, n))
            for n in range(M1 * UNR2, NBLK):
                load((0, n))
            for n in range(XBUF):
                sp.wait_ge(yscat[n], (NBLK - n + XBUF - 1) // XBUF * DMA)
            yv = ydram.rearrange("(k n p) d -> p k n d", p=P, k=2)
            ov = out.rearrange("b (t p) d -> p (b t) d", p=P)
            for n in range(NCH):
                for k in range(2):
                    sp.dma_start(ybuf[k][:, n * TCH * D:(n + 1) * TCH * D].rearrange("p (t d) -> p t d", d=D),
                                 yv[:, k, n * TCH:(n + 1) * TCH, :]).then_inc(s[f"yin{n}"], DMA)
            for n in range(NCH):
                sp.wait_ge(s["sum3"], n + 1)
                sp.dma_start(ov[:, n * TCH:(n + 1) * TCH, :],
                             xall[:, n * TCH * D:(n + 1) * TCH * D].rearrange("p (t d) -> p t d", d=D))\
                  .then_inc(s["out_done"], DMA)
            sp.wait_ge(s["out_done"], NCH * DMA)

        @block.tensor
        def _(pe):
            mm = nc.tensor.matmul
            pe.wait_ge(s["table_ready"], 1)
            pe.wait_ge(s["gu_ready"], 1)
            pe.wait_ge(s["z_hid"], 1)

            def step(k, x, g, h, d):
                if g:
                    b = plus(k, 1)
                    apart(pe)
                    need(pe, s["xts_ready"], nb_(b) + 1)
                    need(pe, s["hid_ready"], nb_(b) - 1)
                    e = pe.value_load(bi[0:1, 0, at_block(b)], min_val=0, max_val=E - 1)
                    for n in range(2):
                        last = mm(GUB[b[1] % 2][:, n, 0:HID], xTs[:, b[1] % 2, :],
                                  gu[:, bass.ds(e * (2 * HID) + n * HID, HID)], start=True, stop=True)
                    last.then_inc(s["gu_done"], 1)
                if h:
                    need(pe, s["hid_ready"], nb_(k) + 1)
                    need(pe, s["hts_ready"], nb_(k) - 1)
                    for n in range(3):
                        last = nc.tensor.transpose(HB[k[1] % 2][:, n * P:(n + 1) * P],
                                                   hid[:, k[1] % 2, n * P:(n + 1) * P], ident)
                    last.then_inc(s["ht_done"], 1)
                if x:
                    b = plus(k, 2)
                    need(pe, xb_in[slot(b)], (uses(b) + 1) * DMA)
                    need(pe, s["xts_ready"], nb_(b))
                    nc.tensor.transpose(XP[:, 0:P], xb[:, slot(b), 0:D], ident).then_inc(s["xt_done"], 1)
                if d:
                    b = plus(k, -1)
                    apart(pe)
                    need(pe, s["hts_ready"], nb_(b) + 1)
                    need(pe, s["y_ready"], nb_(b))
                    e = pe.value_load(bi[0:1, 0, at_block(b)], min_val=0, max_val=E - 1)
                    for n in range(3):
                        last = mm(YP[:, 0:D], hTs[:, b[1] % 2, n * P:(n + 1) * P],
                                  dn[:, bass.ds(e * (3 * D) + n * D, D)], start=(n == 0), stop=(n == 2))
                    last.then_inc(s["y_done"], 1)

            block_steps(pe, step)

        @block.scalar
        def _(act):
            af = nc.scalar.activation
            act.wait_ge(s["w_in"], 2 * DMA)
            af(gu[:, :], gu[:, :], ACT.Copy, scale=ws[:, W_NW:W_NW + 1]).then_inc(s["gu_ready"], 1)

            def step(k, x, g, h, d):
                if g:
                    b = plus(k, 1)
                    need(act, s["gu_done"], nb_(b) + 1)
                    need(act, s["hid_ready"], nb_(b) - 1)
                    af(sg[:, b[1] % 2, :], GUB[b[1] % 2][:, 0, 0:HID], ACT.Silu).then_inc(s["sg_ready"], 1)
                if h:
                    need(act, s["ht_done"], nb_(k) + 1)
                    need(act, s["y_done"], nb_(k) - 1)
                    af(hTs[:, k[1] % 2, :], HB[k[1] % 2][:, 0:HW], ACT.Copy).then_inc(s["hts_ready"], 1)

            block_steps(act, step)

        @block.vector
        def _(dve):
            V = nc.vector
            tt, ts, stt, cp = V.tensor_tensor, V.tensor_scalar, V.scalar_tensor_tensor, V.tensor_copy
            steps = [0]

            def chain(ins):
                steps[0] += 1
                ins.then_inc(s["table_step"], 1)
                dve.wait_ge(s["table_step"], steps[0])

            dve.wait_ge(s["bank_free"], B)
            cp(padi[:, :], base[0:1, :]).then_inc(s["pad_ready"], 1)
            tt(cnt[:, :], base[:, :], cst[:, C_BASE0:C_BASE0 + E], ALU.subtract)
            chain(V.memset(wrow[:, :], 1.0))
            chain(ts(cnti[:, :], cnt[:, :], float(P - 1), None, ALU.add))
            chain(ts(cnti[:, :], cnti[:, :], P.bit_length() - 1, None, ALU.arith_shift_right))
            chain(cp(nbf[:, :], cnti[:, :]))
            chain(V.tensor_tensor_scan(bend[:, :], wrow[:, :], nbf[:, :], 0.0, ALU.mult, ALU.add))
            J = cst[0:1, C_BLK:C_BLK + NBLK]
            tt(ge[:, :, :], J.rearrange("p (j o) -> p j o", o=1).to_broadcast([1, NBLK, E]),
               bend[0:1, :].rearrange("p (o e) -> p o e", o=1).to_broadcast([1, NBLK, E]), ALU.is_ge)
            chain(ts(wrow[:, :], nbf[:, :], -1.0, float(QBLK), ALU.mult, ALU.add))
            V.tensor_reduce(bf_[:, 0, :], ge[:, :, 0:NE1], AX.X, ALU.add)
            chain(tt(gw[:, :, :], ge[:, :, 0:NE1],
                     wrow[0:1, 0:NE1].rearrange("p (o e) -> p o e", o=1).to_broadcast([1, NBLK, NE1]), ALU.mult))
            chain(V.tensor_reduce(bf_[:, 1, :], gw[:, :, :], AX.X, ALU.add))
            chain(tt(bf_[:, 1, :], bf_[:, 1, :], J, ALU.add))
            chain(ts(bf_[:, 2, :], bf_[:, 1, :], -1.0, float(DUMMY), ALU.mult, ALU.add))
            chain(tt(bf_[:, 2, :], bf_[:, 2, :], ge[:, :, NE1], ALU.mult))
            chain(tt(bf_[:, 1, :], bf_[:, 1, :], bf_[:, 2, :], ALU.add))
            cp(bi[:, 0, :], bf_[:, 0, :])
            ts(bi[:, 1, :], bf_[:, 1, :], float(P), None, ALU.mult).then_inc(s["table_ready"], 1)

            V.memset(hid[:, :, HID:HW], 0.0).then_inc(s["z_hid"], 1)

            def step(k, x, g, h, d):
                if x:
                    b = plus(k, 2)
                    need(dve, s["xt_done"], nb_(b) + 1)
                    need(dve, s["gu_done"], nb_(b) - 1)
                    cp(xTs[:, b[1] % 2, :], XP[:, 0:P]).then_inc(s["xts_ready"], 1)
                if g:
                    b = plus(k, 1)
                    need(dve, s["sg_ready"], nb_(b) + 1)
                    need(dve, s["ht_done"], nb_(b) - 1)
                    tt(hid[:, b[1] % 2, 0:HID], sg[:, b[1] % 2, :], GUB[b[1] % 2][:, 1, 0:HID], ALU.mult)\
                        .then_inc(s["hid_ready"], 1)
                if d:
                    b = plus(k, -1)
                    need(dve, s["y_done"], nb_(b) + 1)
                    need(dve, yscat[slot(b)], uses(b) * DMA)
                    ts(ysb[:, slot(b), :], YP[:, 0:D], xb[:, slot(b), D:D + 1], None, ALU.mult)\
                        .then_inc(s["y_ready"], 1)

            block_steps(dve, step)
            dve.wait_ge(s["gba_in"], DMA)
            bch = TCH // T
            for n in range(NCH):
                dve.wait_ge(s[f"yin{n}"], 2 * DMA)
                c0, c1 = n * TCH * D, (n + 1) * TCH * D
                tt(ybuf[0][:, c0:c1], ybuf[0][:, c0:c1], ybuf[1][:, c0:c1], ALU.add).then_inc(s["sum1"], 1)
                dve.wait_ge(s["sum1"], n + 1)
                for m in range(bch):
                    y = ybuf[0][:, c0 + m * T * D:c0 + (m + 1) * T * D].rearrange("p (t d) -> p t d", d=D)
                    last = tt(y, y, gba[:, n * bch + m:n * bch + m + 1, :].to_broadcast([P, T, D]), ALU.mult)
                last.then_inc(s["sum2"], 1)

        @block.gpsimd
        def _(pool):
            G = nc.gpsimd
            below = G.to_reg(2 * NTOK - 2)
            bound = pool.alloc_register("bound")

            def step(k, x, g, h, d):
                if not d:
                    return
                b = plus(k, -1)
                need(pool, s["y_ready"], nb_(b) + 1)
                pool.reg_add(bound, below, 1)
                G.indirect_dma_start(ydram, bass.IndirectOffsetOnAxis(xb[:, slot(b), D + 1:D + 2].bitcast(u32), 0),
                                     ysb[:, slot(b), :], None, bounds_check=bound, oob_is_err=False)\
                 .then_inc(yscat[slot(b)], DMA)

            block_steps(pool, step)
            for n in range(NCH):
                pool.wait_ge(s["sum2"], n + 1)
                c0, c1 = n * TCH * D, (n + 1) * TCH * D
                G.tensor_tensor(xall[:, c0:c1], xall[:, c0:c1], ybuf[0][:, c0:c1], ALU.add).then_inc(s["sum3"], 1)


def host_constants():
    c = np.zeros((P, CW), np.float32)
    p = np.arange(P)
    c[:, C_ID:C_ID + P] = np.eye(P)
    c[:, C_UT:C_UT + P] = p[:, None] < p[None, :]
    c[:, C_ONE:C_ONE + P] = 1.0
    c[:, C_MASK:C_MASK + P] = np.where(p[None, :] >= p[:, None], np.float32(E_HI), 0.0)
    inv = np.float32(10000.0) ** (-np.arange(0, DR, 2, dtype=np.float32) / np.float32(DR))
    ang = np.arange(S, dtype=np.float32)[:, None] * inv
    cos, sin = np.cos(ang).T, np.sin(ang).T
    for n, row in enumerate((cos[0], sin[0], cos[1], sin[1])):
        c[n * DL:(n + 1) * DL, C_TRIG:C_TRIG + S] = row
    second = slice(C_TRIG + S, C_TRIG + 2 * S)
    c[0:DL, second] = 1.0
    for d in range(DR):
        c[DL + d, second] = cos[d // 2]
        c[DL + DR + d, second] = sin[d // 2] * (1.0 if d % 2 else -1.0)
    c[2 * DL:3 * DL, second] = 1.0
    sign = np.ones((P, NG, DQK, HG), np.float32)
    sign[DL:2 * DL, :, DH, :] = -1.0
    sign[3 * DL:4 * DL, :, DH + 2, :] = -1.0
    c[:, C_SIGN:C_SIGN + NG * QR] = sign.reshape(P, -1)
    c[:, C_IOTA:C_IOTA + E] = np.arange(E)
    c[:, C_BASE0:C_BASE0 + E] = np.arange(E) * QROWS
    for t in range(T):
        for k in range(2):
            c[:, C_ID0 + 2 * t + k] = k * NTOK + t * P + p
    c[:, C_BLK:C_BLK + NBLK] = np.arange(NBLK)
    c[:, C_PAD + D + 1] = np.full(P, PADID, np.int32).view(np.float32)
    return c


def host_layout(a):
    w = np.zeros((P, WW), np.float32)
    dq, uq, qr = a["L0_attn_W_DQ"], a["L0_attn_W_UQ"], a["L0_attn_W_QR"]
    for n in range(4):
        w[:, W_A + n * DL:W_A + (n + 1) * DL] = dq
    w[:, W_B:W_B + DL] = a["L0_attn_W_DKV"]
    w[:, W_B + DL:W_B + DL + DR] = a["L0_attn_W_KR"]
    w[:, W_B + DL + DR:W_B + DL + 2 * DR] = a["L0_attn_W_KR"][:, [1, 0, 3, 2]]
    w[:, W_B + 2 * DL:W_B + 3 * DL] = dq
    qa = np.zeros((P, NG, DQK, HG), np.float32)
    q4 = qr.reshape(DL, HG, NG, DR).transpose(0, 2, 1, 3)
    for freq in range(2):
        c_rows = slice(2 * freq * DL, (2 * freq + 1) * DL)
        s_rows = slice((2 * freq + 1) * DL, (2 * freq + 2) * DL)
        for d in range(2):
            qa[c_rows, :, DH + 2 * freq + d, :] = q4[:, :, :, 2 * freq + d]
            qa[s_rows, :, DH + 2 * freq + d, :] = q4[:, :, :, 2 * freq + 1 - d]
    w[:, W_QA:W_QA + NG * QR] = qa.reshape(P, -1)
    qb = np.zeros((P, NG, DQK, HG), np.float32)
    qb[2 * DL:3 * DL, :, 0:DH, :] = uq.reshape(DL, HG, NG, DH).transpose(0, 2, 3, 1)
    w[:, W_QB:W_QB + NG * QR] = qb.reshape(P, -1)
    kb = np.zeros((P, NG, DQK, HG), np.float32)
    kb[0:DL, :, 0:DH, :] = a["L0_attn_W_UK"].reshape(DL, HG, NG, DH).transpose(0, 2, 3, 1)
    for d in range(DR):
        kb[DL + d, :, DH + d, :] = 1.0
        kb[DL + DR + d, :, DH + d, :] = 1.0
    w[:, W_K:W_K + NG * QR] = kb.reshape(P, -1)
    w[0:DL, W_V:W_V + H * DH] = a["L0_attn_W_UV"]
    w[:, W_O:W_O + D] = a["L0_attn_W_O"]
    w[:, W_R:W_R + E] = a["L0_ffn_router_weight"].T
    w[:, W_NW] = a["L0_ffn_norm_weight"]
    w[:, W_AL] = a["L0_ffn_residual_alpha"]
    w[:, W_CT:W_CT + B] = a["L0_c"].T
    gup = np.ascontiguousarray(a["L0_ffn_gate_up_weight"].transpose(2, 0, 1).reshape(P, E * 2 * HID))
    dn = np.zeros((E, 3 * P, D), np.float32)
    dn[:, 0:HID, :] = a["L0_ffn_down_weight"].transpose(0, 2, 1)
    dn = np.ascontiguousarray(dn.reshape(E, 3, P, D).transpose(2, 0, 1, 3).reshape(P, E * 3 * D))
    return w, gup, dn


def kernel(**inputs):
    import concourse.bacc as bacc
    from concourse.bass_utils import run_bass_kernel_spmd

    a = {k: np.asarray(v) for k, v in inputs.items()}
    w, gup, dn = host_layout(a)
    arrays = {"x": np.ascontiguousarray(a["L0_attn_x"]), "consts": host_constants(), "wsmall": w,
              "wmod": np.ascontiguousarray(a["L0_wmod"]), "gup": gup, "down": dn}
    nc = bacc.Bacc("TRN2", target_bir_lowering=False, num_devices=1)
    args = [nc.dram_tensor(n, v.shape, mybir.dt.float32, kind="ExternalInput").ap() for n, v in arrays.items()]
    out = nc.dram_tensor("out", (B, S, D), mybir.dt.float32, kind="ExternalOutput").ap()
    adaln_kernel(nc, *args, out)
    r = run_bass_kernel_spmd(nc, [arrays], core_ids=[0])
    return r.results[0]["out"]
```

```python
import math

import numpy as np

import concourse.bass as bass
from concourse import mybir
from contextlib import ExitStack

B, S, D = 16, 256, 128
P = 128
T = S // P
H, DH, DR, DL = 16, 8, 4, 32
DQK = DH + DR
E, HID = 8, 352
HW = 3 * P
NT = B * T
NTOK = B * S
SG = 8
STATS_AFTER = {-2: 1, -1: 2, 0: 3}
LN_EPS, RMS_EPS = 1e-5, 1e-6
SC = 1.0 / math.sqrt(DQK)
E_HI = float(np.exp(np.float32(80.0) * np.float32(SC)))
E_LO = float(np.exp(np.float32(-80.0) * np.float32(SC)))

HG = 8
QR = HG * DQK
NG = H // HG
COMBOS = [(0, 0), (0, 1), (1, 0), (0, 2), (2, 0), (1, 1)]
NC = len(COMBOS)
STAGES = (-2, -1, 0, 1, 2, 3)
KST = 96
NPAIR = H // 2
VW = 32

QBLK = NTOK // P + 1
QROWS = QBLK * P
DUMMY = E * QBLK
NBLK = (2 * NTOK) // P + E - 1
PAYW = D + 2
PADID = 1 << 20

C_ID, C_UT, C_ONE, C_MASK, C_TRIG, C_SIGN = 0, 128, 256, 384, 512, 1024
C_IOTA = C_SIGN + NG * QR
C_BASE0 = C_IOTA + E
C_ID0 = C_BASE0 + E
C_BLK = C_ID0 + 4
C_PAD = C_BLK + NBLK
CW = C_PAD + PAYW
W_A, W_B, W_QA, W_QB, W_K, W_V, W_O, W_R = 0, 128, 256, 448, 640, 832, 960, 1088
W_NW, W_AL, W_CT, WW = 1096, 1097, 1098, 1114


def adaln_kernel(nc, x, consts, wsmall, wmod, gup, down, out):
    fp32, bf16 = mybir.dt.float32, mybir.dt.bfloat16
    i32, u32 = mybir.dt.int32, mybir.dt.uint32
    ALU, ACT, AX = mybir.AluOpType, mybir.ActivationFunctionType, mybir.AxisListType

    queue = nc.dram_tensor("queue", [(DUMMY + 1) * P, PAYW], fp32).ap()
    ydram = nc.dram_tensor("ydram", [2 * NTOK, D], fp32).ap()
    qdram = nc.dram_tensor("qdram", [2, 3, QR, NG * S], bf16).ap()
    kdram = nc.dram_tensor("kdram", [2, 3, QR, NG * S], bf16).ap()
    modrow = nc.dram_tensor("modrow", [B, 5 * D], fp32).ap()

    ctx = ExitStack()
    with ctx:
        def sb(name, shape, dt=fp32):
            return ctx.enter_context(nc.sbuf_tensor(name, shape, dt))

        def sem(name):
            return ctx.enter_context(nc.semaphore(name))

        cst = sb("cst", [P, CW])
        ws = sb("ws", [P, WW])
        wm = sb("wm", [P, 6 * D])
        xall = sb("xall", [P, NT * D])
        gu = sb("gu", [P, E * 2 * HID])
        dn = sb("dn", [P, E * 3 * D])
        ut_bf = sb("ut_bf", [P, P], bf16)
        one_bf = sb("one_bf", [P, P], bf16)
        mask4 = sb("mask4", [P, 4, P])
        st6 = sb("st6", [P, NT, 6])
        mean1 = sb("mean1", [P, NT])
        rstd1 = sb("rstd1", [P, NT])
        shift1 = sb("shift1", [P, NT])
        var1 = sb("var1", [P, NT])
        dm1 = sb("dm1", [P, SG])
        mhalf = sb("mhalf", [P, NT])
        epst = sb("epst", [P, 2 * T])
        scT = sb("scT", [P, B])
        saT = sb("saT", [P, B])
        ca1T = sb("ca1T", [P, B])
        mrow = sb("mrow", [B, 5 * D])
        msgn = sb("msgn", [B, D])
        mabs = sb("mabs", [B, D])
        alpha = sb("alpha", [P, 1])
        bc = sb("bc", [P, 2, 4 * D])
        xn = sb("xn", [P, T * D])
        hT = sb("hT", [P, S])
        cc = sb("cc", [P, 2, 2 * S])
        qs = sb("qs", [QR, 3, NG * S], bf16)
        ks = sb("ks", [QR, 3, NG * S], bf16)
        rq = sb("rq", [QR, NG * S])
        rk = sb("rk", [QR, NG * S])
        stq = sb("stq", [P, 2, H, S], bf16)
        stk = sb("stk", [P, 2, H, S], bf16)
        va = sb("va", [P, 2, T, H * VW])
        pt = sb("pt", [P, NPAIR, 2, 2 * S])
        ot = sb("ot", [P, 4, S])
        rden = sb("rden", [P, T, H])
        at = sb("at", [P, T, H * DH])
        aTs = sb("aTs", [P, S])
        wog = sb("wog", [P, D])
        st2 = sb("st2", [P, T, 6])
        mv2 = sb("mv2", [P, T, 2])
        ve2 = sb("ve2", [P, T])
        rstd2 = sb("rstd2", [P, T])
        t1 = sb("t1", [P, T, D])
        h2 = sb("h2", [P, T, D])
        gbh = sb("gbh", [P, T, D])
        h2Ts = sb("h2Ts", [P, S])
        sqj = sb("sqj", [P, D])
        ss = sb("ss", [P, T])
        ve3 = sb("ve3", [P, T])
        rstd3 = sb("rstd3", [P, T])
        pl = sb("pl", [P, 2, T, 2, PAYW])
        lg = sb("lg", [P, T, E])
        mx = sb("mx", [P, T, 8])
        mi = sb("mi", [P, T, 8], u32)
        mif = sb("mif", [P, T, 2])
        oh = sb("oh", [P, 2, T, 2, E])
        tot = sb("tot", [P, T * E], bf16)
        dif = sb("dif", [P, T])
        ex = sb("ex", [P, 2, T])
        den = sb("den", [P, T])
        base = sb("base", [P, E])
        pos = sb("pos", [P, T, E])
        pd = sb("pd", [P, T, 2, E])
        destf = sb("destf", [P, T * 2])
        dest = sb("dest", [P, 2, T * 2], u32)
        idf = sb("idf", [P, T * 2])

        SCB = [ctx.enter_context(nc.psum_tensor(f"SC{n}", [P, 2, 512], fp32)) for n in range(2)]
        OB, FA, FB, BK = (ctx.enter_context(nc.psum_tensor(n, [P, 512], fp32)) for n in ("OB", "FA", "FB", "BK"))

        ident = cst[:, C_ID:C_ID + P]

        names = """cst_in x_in0 x_in ws_in wm_in w_in bc_in0 bc_in1 modrow_out dummy_out
            z_stack z_va z_half bf_ready mask_ready st6_ready shift1_ready mv1_ready rstd1_ready sil_ready mod_done modt_ready
            mod_step mrow_ready sign_ready stat_step base_init
            xn_ready xT_done hT_ready ab_done c_ready q_done k_done v_done q1_ready k1_ready rq_ready rk_ready
            q2_ready k2_ready q3_ready k3_ready v_ready stq0 stq1 stk0 stk1
            sc_done exp_done clip_done pv_done o_ready ot_done rden_ready norm_done at_done ats_ready wog_ready
            wo_done x2_ready st2_ready mv2_ready ve2_ready rstd2_ready t1_ready h2_ready h2t_done h2ts_ready
            ss_ready ve3_ready rstd3_ready pl_ready gbh_ready base_ready lg_done lg_ready mx_ready mi_ready
            mif_ready oh_ready tot_ready dif_ready ex_ready rank_done pos_ready bank_free pd_ready destf_ready
            den_ready q_out k_out dest_ready c0_ready id_ready scat0 scat1""".split()
        s = {n: sem(n) for n in names}
        stq_in, stk_in = [s["stq0"], s["stq1"]], [s["stk0"], s["stk1"]]
        bc_in, scat = [s["bc_in0"], s["bc_in1"]], [s["scat0"], s["scat1"]]
        DMA = 16

        def need(eng, sm, value):
            if isinstance(value, int) and value <= 0:
                return
            eng.wait_ge(sm, value)

        def apart(eng):
            eng.wait_ge(s["cst_in"], DMA)

        def schedule(eng, emit):
            def stages(i):
                return [0 <= i - behind < B for behind in STAGES]

            for i in range(-2, 4):
                emit((0, i), *stages(i))
            with eng.Fori(2, 7) as j:
                emit((j, 0), *stages(4))
                emit((j, 1), *stages(5))
            for i in range(14, B + 3):
                emit((0, i), *stages(i))

        def batches(i):
            return [(i[0], i[1] - behind) for behind in STAGES]

        def num(b):
            return 2 * b[0] + b[1]

        def peeled(i):
            return num(i) if isinstance(i[0], int) else None

        def par(b):
            return b[1] % 2

        def half(b):
            return b[0] + b[1] // 2

        def xtile(b, t=0, n=T):
            if isinstance(b[0], int):
                return slice((num(b) * T + t) * D, (num(b) * T + t + n) * D)
            return bass.ds(b[0] * (2 * T * D) + (b[1] * T + t) * D, n * D)

        def col(b, n=1):
            if isinstance(b[0], int):
                return slice(num(b) * n, num(b) * n + n)
            return bass.ds(b[0] * (2 * n) + b[1] * n, n)

        NE1 = E - 1
        XBUF = 8
        UNR2 = XBUF
        M0, M1 = 2, (NBLK - 2) // UNR2

        cnt = sb("cnt", [P, E])
        cnti = sb("cnti", [P, E], i32)
        nbf = sb("nbf", [P, E])
        bend = sb("bend", [P, E])
        padi = sb("padi", [1, E], i32)
        wrow = sb("wrow", [P, E])
        ge = sb("ge", [1, NBLK, E])
        gw = sb("gw", [1, NBLK, NE1])
        bf_ = sb("bf_", [1, 3, NBLK])
        bi = sb("bi", [1, 2, NBLK], i32)
        xb = sb("xb", [P, XBUF, PAYW])
        xTs = sb("xTs", [P, 2, P])
        sg = sb("sg", [P, 2, HID])
        hid = sb("hid", [P, 2, HW])
        hTs = sb("hTs", [P, 2, HW])
        ysb = sb("ysb", [P, XBUF, D])
        gba = pt[:, 0:2, :, :].rearrange("p s h c -> p (s h c)").rearrange("p (b d) -> p b d", d=D)
        NCH = 8
        TCH = NT // NCH
        ybuf = [st[:, :, :, :].rearrange("p a h n -> p (a h n)").bitcast(fp32) for st in (stq, stk)]
        GUB, HB, XP, YP = SCB, (OB, FA), FB, BK

        names2 = """table_step table_ready pad_ready padded gu_ready gba_in xt_done xts_ready gu_done
            sg_ready hid_ready z_hid ht_done hts_ready y_done y_ready yin0 yin1 yin2 yin3 yin4 yin5 yin6 yin7
            sum1 sum2 sum3 out_done""".split()
        s.update({n: sem(n) for n in names2})
        xb_in = [sem(f"xb_in{n}") for n in range(XBUF)]
        yscat = [sem(f"yscat{n}") for n in range(XBUF)]

        def nb_(k):
            return UNR2 * k[0] + k[1]

        def slot(k):
            return k[1] % XBUF

        def uses(k):
            return k[0] + k[1] // XBUF

        def at_block(k):
            return slice(nb_(k), nb_(k) + 1) if isinstance(k[0], int) else bass.ds(k[0] * UNR2 + k[1], 1)

        def block_steps(eng, step):
            step((0, -2), True, False, False, False)
            step((0, -1), True, True, False, False)
            step((0, 0), True, True, True, False)
            for n in range(1, M0 * UNR2):
                step((0, n), True, True, True, True)
            with eng.Fori(M0, M1) as m:
                for n in range(UNR2):
                    step((m, n), True, True, True, True)
            for n in range(M1 * UNR2, NBLK - 2):
                step((0, n), True, True, True, True)
            step((0, NBLK - 2), False, True, True, True)
            step((0, NBLK - 1), False, False, True, True)
            step((0, NBLK), False, False, False, True)

        def plus(k, n):
            return (k[0], k[1] + n)

        block = ctx.enter_context(nc.Block())

        @block.sync
        def _(sp):
            xv = x.rearrange("b (t p) d -> p (b t) d", p=P)
            xs = xall[:, :].rearrange("p (n d) -> p n d", d=D)
            sp.dma_start(xs[:, 0:8, :], xv[:, 0:8, :]).then_inc(s["x_in0"], DMA)
            sp.dma_start(ws[:, :], wsmall).then_inc(s["ws_in"], DMA)
            sp.dma_start(cst[:, :], consts).then_inc(s["cst_in"], DMA)
            sp.dma_start(wm[:, :], wmod).then_inc(s["wm_in"], DMA)
            for n in range(1, 4):
                sp.dma_start(xs[:, 8 * n:8 * n + 8, :], xv[:, 8 * n:8 * n + 8, :]).then_inc(s["x_in"], DMA)
            sp.dma_start(gu[:, :], gup).then_inc(s["w_in"], DMA)
            sp.dma_start(dn[:, :], down).then_inc(s["w_in"], DMA)
            sp.wait_ge(s["mrow_ready"], 1)
            sp.dma_start(modrow, mrow[:, :]).then_inc(s["modrow_out"], DMA)
            sp.wait_ge(s["cst_in"], DMA)
            sp.dma_start(queue[DUMMY * P:(DUMMY + 1) * P, :], cst[:, C_PAD:C_PAD + PAYW]).then_inc(s["dummy_out"], DMA)
            sp.wait_ge(s["modrow_out"], DMA)
            sp.wait_ge(s["z_stack"], 4)

            def load_bc(a):
                need(sp, s["base_ready"], num(a) - 1)
                src = modrow[col(a), 0:4 * D].to_broadcast([P, 4 * D])
                sp.dma_start(bc[:, par(a), :], src).then_inc(bc_in[par(a)], DMA)

            def part_out(parts, dram, arrived, ready, written, f):
                apart(sp)
                for r in ready:
                    need(sp, s[r], num(f) + 1)
                need(sp, s["pv_done"], 4 * num(f) - 7)
                sp.dma_start(dram[par(f)].rearrange("s q n -> q s n"), parts[:, :, :]).then_inc(s[written], DMA)

            def stack(dram, dst, arrived, written, side, f):
                need(sp, s[written], DMA * num(f) + DMA)
                need(sp, s["sc_done"], NPAIR * num(f) - NPAIR)
                for n, combo in enumerate(COMBOS):
                    sp.dma_start(dst[n * DQK:(n + 1) * DQK, par(f), :, :],
                                 dram[par(f), combo[side]].rearrange("(r h) (g n) -> r (h g) n", h=HG, g=NG))\
                      .then_inc(arrived[par(f)], DMA)

            def emit(i, front, vproj, attn, back, norm, route):
                f, v, a, r, u, q = batches(i)
                if front:
                    part_out(qs, qdram, stq_in, ("q1_ready", "q2_ready", "q3_ready"), "q_out", f)
                    part_out(ks, kdram, stk_in, ("k1_ready", "k2_ready", "k3_ready"), "k_out", f)
                if attn:
                    load_bc(a)
                if front:
                    stack(qdram, stq, stq_in, "q_out", 0, f)
                    stack(kdram, stk, stk_in, "k_out", 1, f)

            schedule(sp, emit)

            sp.wait_ge(s["pad_ready"], 1)
            _, rows = nc.values_load_multi_w_load_instructions(
                padi[0:1, :], engines=[mybir.EngineType.SP], min_val=0, max_val=DUMMY * P - P)
            for row in rows:
                sp.dma_start(queue[bass.ds(row, P), :], cst[:, C_PAD:C_PAD + PAYW]).then_inc(s["padded"], DMA)
            sp.wait_ge(scat[0], B // 2 * 4 * DMA)
            sp.wait_ge(scat[1], B // 2 * 4 * DMA)
            sp.wait_ge(s["dummy_out"], DMA)
            sp.wait_ge(s["padded"], E * DMA)
            sp.wait_ge(s["table_ready"], 1)

            def load(k, count):
                first = nb_(k)
                at = slice(first, first + count) if isinstance(k[0], int) else bass.ds(k[0] * UNR2, count)
                apart(sp)
                _, rows = nc.values_load_multi_w_load_instructions(
                    bi[0:1, 1, at], engines=[mybir.EngineType.SP], min_val=0, max_val=DUMMY * P)
                for n, row in enumerate(rows):
                    b = plus(k, n)
                    need(sp, yscat[slot(b)], uses(b) * DMA)
                    sp.dma_start(xb[:, slot(b), :], queue[bass.ds(row, P), :]).then_inc(xb_in[slot(b)], DMA)

            load((0, 0), UNR2)
            sp.wait_ge(s["pv_done"], 4 * B)
            gb_rows = modrow[:, 4 * D:5 * D].rearrange("(o b) d -> o b d", o=1)
            sp.dma_start(gba[:, :, :], gb_rows.to_broadcast([P, B, D])).then_inc(s["gba_in"], DMA)
            with sp.Fori(1, M1) as m:
                load((m, 0), UNR2)
            load((M1, 0), NBLK - M1 * UNR2)
            for n in range(XBUF):
                sp.wait_ge(yscat[n], (NBLK - n + XBUF - 1) // XBUF * DMA)
            yv = ydram.rearrange("(k n p) d -> p k n d", p=P, k=2)
            ov = out.rearrange("b (t p) d -> p (b t) d", p=P)
            for n in range(NCH):
                for k in range(2):
                    sp.dma_start(ybuf[k][:, n * TCH * D:(n + 1) * TCH * D].rearrange("p (t d) -> p t d", d=D),
                                 yv[:, k, n * TCH:(n + 1) * TCH, :]).then_inc(s[f"yin{n}"], DMA)
            for n in range(NCH):
                sp.wait_ge(s["sum3"], n + 1)
                sp.dma_start(ov[:, n * TCH:(n + 1) * TCH, :],
                             xall[:, n * TCH * D:(n + 1) * TCH * D].rearrange("p (t d) -> p t d", d=D))\
                  .then_inc(s["out_done"], DMA)
            sp.wait_ge(s["out_done"], NCH * DMA)

        @block.tensor
        def _(pe):
            mm = nc.tensor.matmul
            pe.wait_ge(s["sil_ready"], 1)
            pe.wait_ge(s["wm_in"], DMA)
            mm(FA[:, 0:B], wm[:, 0:D], scT[:, :], start=True, stop=True)
            mm(FA[:, B:2 * B], wm[:, D:2 * D], scT[:, :], start=True, stop=True)
            mm(FB[0:B, 0:4 * D], scT[:, :], wm[:, 2 * D:6 * D], start=True, stop=True).then_inc(s["mod_done"], 1)
            pe.wait_ge(s["cst_in"], DMA)
            pe.wait_ge(s["modt_ready"], 1)
            pe.wait_ge(s["mrow_ready"], 1)
            pe.wait_ge(s["sign_ready"], 1)
            pe.wait_ge(s["bf_ready"], 2)

            def scores(a, p):
                if p == 0:
                    need(pe, stq_in[par(a)], (half(a) + 1) * (DMA * NC))
                    need(pe, stk_in[par(a)], (half(a) + 1) * (DMA * NC))
                need(pe, s["exp_done"], NPAIR * num(a) + (p - 1))
                for hh in range(2):
                    h = 2 * p + hh
                    dst = SCB[p % 2][:, hh, :]
                    mm(dst[:, 0:S], stk[0:KST, par(a), h, 0:P], stq[0:KST, par(a), h, 0:S], start=True, stop=True)
                    last = mm(dst[:, S:S + P], stk[0:KST, par(a), h, P:S], stq[0:KST, par(a), h, P:S],
                              start=True, stop=True)
                last.then_inc(s["sc_done"], 1)

            def values(a, g):
                need(pe, s["clip_done"], NPAIR * num(a) + (2 * g + 2))
                if g == 0:
                    need(pe, s["v_ready"], num(a) + 1)
                if g % 2 == 0:
                    need(pe, s["o_ready"], 2 * num(a) + g // 2)
                for kt in range(T):
                    for n in range(4):
                        h = 4 * g + n
                        src = pt[:, h // 2, h % 2, 0:S] if kt == 0 else pt[:, h // 2, h % 2, S:S + P]
                        last = mm(OB[VW * n:VW * n + VW, (g % 2) * S + kt * P:(g % 2) * S + S],
                                  va[:, par(a), kt, h * VW:(h + 1) * VW], src, start=(kt == 0), stop=(kt == 1))
                last.then_inc(s["pv_done"], 1)

            def emit(i, front, vproj, attn, back, norm, route):
                f, v, a, r, u, q = batches(i)
                if attn:
                    scores(a, 0)
                if attn:
                    scores(a, 1)
                if route:
                    need(pe, s["tot_ready"], num(q) + 1)
                    if attn:
                        need(pe, s["v_ready"], num(a) + 1)
                    elif norm:
                        need(pe, s["x2_ready"], num(u) + 1)
                    R = FB[:, 0:3 * E]
                    mm(R[:, 0:E], ut_bf[:, :], tot[:, 0:E], start=True, stop=True)
                    mm(R[:, E:2 * E], ut_bf[:, :], tot[:, E:2 * E], start=True, stop=False)
                    mm(R[:, E:2 * E], one_bf[:, :], tot[:, 0:E], start=False, stop=True)
                    mm(R[:, 2 * E:3 * E], one_bf[:, :], tot[:, 0:E], start=True, stop=False)
                    mm(R[:, 2 * E:3 * E], one_bf[:, :], tot[:, E:2 * E], start=False, stop=True)\
                        .then_inc(s["rank_done"], 1)
                if back:
                    values(r, 3)
                if front:
                    need(pe, s["xn_ready"], num(f) + 1)
                    need(pe, s["k1_ready"], num(f))
                    need(pe, s["rk_ready"], num(f))
                    for t in range(T):
                        last = nc.tensor.transpose(FA[:, t * P:(t + 1) * P], xn[:, t * D:(t + 1) * D], ident)
                    last.then_inc(s["xT_done"], 1)
                if attn:
                    scores(a, 2)
                if norm:
                    need(pe, s["h2_ready"], num(u) + 1)
                    for t in range(T):
                        last = nc.tensor.transpose(BK[:, t * P:(t + 1) * P], h2[:, t, :], ident)
                    last.then_inc(s["h2t_done"], 1)
                if front:
                    need(pe, s["hT_ready"], num(f) + 1)
                    mm(FA[:, 0:S], ws[:, W_A:W_A + P], hT[:, :], start=True, stop=True)
                    mm(FA[:, S:2 * S], ws[:, W_B:W_B + P], hT[:, :], start=True, stop=True)\
                        .then_inc(s["ab_done"], 1)
                if attn:
                    scores(a, 3)
                if norm:
                    need(pe, s["h2ts_ready"], num(u) + 1)
                    for t in range(T):
                        last = mm(BK[:, S + t * E:S + (t + 1) * E], h2Ts[:, t * P:(t + 1) * P],
                                  ws[:, W_R:W_R + E], start=True, stop=True)
                    last.then_inc(s["lg_done"], 1)
                if attn:
                    scores(a, 4)
                if back:
                    need(pe, s["o_ready"], 2 * num(r) + 2)
                    if norm:
                        need(pe, s["lg_ready"], num(u) + 1)
                    need(pe, s["bank_free"], num(u))
                    if attn:
                        need(pe, s["v_ready"], num(a) + 1)
                    for t in range(T):
                        for g in range(4):
                            last = nc.tensor.transpose((BK, FB)[t][:, g * P:(g + 1) * P],
                                                       ot[:, g, t * P:(t + 1) * P], ident)
                    last.then_inc(s["ot_done"], 1)
                if attn:
                    values(a, 0)
                if attn:
                    scores(a, 5)
                if back:
                    need(pe, s["norm_done"], num(r) + 1)
                    for t in range(T):
                        last = nc.tensor.transpose(BK[:, t * P:(t + 1) * P], at[:, t, :], ident)
                    last.then_inc(s["at_done"], 1)
                if front:
                    need(pe, s["c_ready"], num(f) + 1)
                    for g in range(NG):
                        last = mm(FA[0:QR, g * S:(g + 1) * S], ws[:, W_K + g * QR:W_K + (g + 1) * QR],
                                  cc[:, par(f), S:2 * S], start=True, stop=True)
                    last.then_inc(s["k_done"], 1)
                if back:
                    need(pe, s["ats_ready"], num(r) + 1)
                    need(pe, s["wog_ready"], num(r) + 1)
                    for t in range(T):
                        last = mm(BK[:, S + t * D:S + (t + 1) * D], aTs[:, t * P:(t + 1) * P], wog[:, :],
                                  start=True, stop=True)
                    last.then_inc(s["wo_done"], 1)
                if attn:
                    scores(a, 6)
                if attn:
                    values(a, 1)
                if front:
                    need(pe, s["v_ready"], num(v))
                    for g in range(NG):
                        mm(FB[0:QR, g * S:(g + 1) * S], ws[:, W_QA + g * QR:W_QA + (g + 1) * QR],
                           cc[:, par(f), 0:S], start=True, stop=False)
                        last = mm(FB[0:QR, g * S:(g + 1) * S], ws[:, W_QB + g * QR:W_QB + (g + 1) * QR],
                                  cc[:, par(f), S:2 * S], start=False, stop=True)
                    last.then_inc(s["q_done"], 1)
                if attn:
                    scores(a, 7)
                if attn:
                    values(a, 2)
                if vproj:
                    if front:
                        need(pe, s["q1_ready"], num(f) + 1)
                        need(pe, s["rq_ready"], num(f) + 1)
                    for t in range(T):
                        last = mm(FB[:, t * P:(t + 1) * P], cc[:, par(v), S + t * P:S + (t + 1) * P],
                                  ws[:, W_V:W_V + P], start=True, stop=True)
                    last.then_inc(s["v_done"], 1)

            schedule(pe, emit)

            mm = nc.tensor.matmul
            pe.wait_ge(s["table_ready"], 1)
            pe.wait_ge(s["gu_ready"], 1)
            pe.wait_ge(s["exp_done"], NPAIR * B)
            pe.wait_ge(s["o_ready"], 2 * B)
            pe.wait_ge(s["rk_ready"], B)
            pe.wait_ge(s["bank_free"], B)
            pe.wait_ge(s["lg_ready"], B)
            pe.wait_ge(s["z_hid"], 1)

            REGS, LOADED = 8, 4
            experts = [pe.alloc_register(f"expert{n}") for n in range(REGS)]

            def load_experts(k):
                n = LOADED if not isinstance(k[0], int) else min(LOADED, NBLK - nb_(k))
                if n <= 0:
                    return
                at = slice(nb_(k), nb_(k) + n) if isinstance(k[0], int) else bass.ds(k[0] * UNR2 + k[1], n)
                pe.reg_load([experts[(k[1] + c) % REGS] for c in range(n)], bi[0:1, 0, at])

            def expert(b):
                return nc.snap(experts[b[1] % REGS]).with_bounds(min_val=0, max_val=E - 1)

            load_experts((0, 0))
            load_experts((0, LOADED - 3))

            def step(k, x, g, h, d):
                if g:
                    b = plus(k, 1)
                    need(pe, s["xts_ready"], nb_(b) + 1)
                    need(pe, s["hid_ready"], nb_(b) - 1)
                    e = expert(b)
                    for n in range(2):
                        last = mm(GUB[b[1] % 2][:, n, 0:HID], xTs[:, b[1] % 2, :],
                                  gu[:, bass.ds(e * (2 * HID) + n * HID, HID)], start=True, stop=True)
                    last.then_inc(s["gu_done"], 1)
                if x:
                    b = plus(k, 2)
                    need(pe, xb_in[slot(b)], (uses(b) + 1) * DMA)
                    need(pe, s["xts_ready"], nb_(b))
                    nc.tensor.transpose(XP[:, 0:P], xb[:, slot(b), 0:D], ident).then_inc(s["xt_done"], 1)
                if d:
                    b = plus(k, -1)
                    need(pe, s["hts_ready"], nb_(b) + 1)
                    need(pe, s["y_ready"], nb_(b))
                    e = expert(b)
                    for n in range(3):
                        last = mm(YP[:, 0:D], hTs[:, b[1] % 2, n * P:(n + 1) * P],
                                  dn[:, bass.ds(e * (3 * D) + n * D, D)], start=(n == 0), stop=(n == 2))
                    last.then_inc(s["y_done"], 1)
                if k[1] % LOADED == LOADED - 1 and k[1] > 0:
                    load_experts(plus(k, 2))
                if h:
                    need(pe, s["hid_ready"], nb_(k) + 1)
                    need(pe, s["hts_ready"], nb_(k) - 1)
                    for n in range(3):
                        last = nc.tensor.transpose(HB[k[1] % 2][:, n * P:(n + 1) * P],
                                                   hid[:, k[1] % 2, n * P:(n + 1) * P], ident)
                    last.then_inc(s["ht_done"], 1)

            block_steps(pe, step)

        @block.scalar
        def _(act):
            af = nc.scalar.activation
            act.wait_ge(s["ws_in"], DMA)
            af(scT[:, :], ws[:, W_CT:W_CT + B], ACT.Silu).then_inc(s["sil_ready"], 1)
            act.wait_ge(s["modt_ready"], 1)

            def exps(a, p):
                need(act, s["sc_done"], NPAIR * num(a) + (p + 1))
                need(act, s["pv_done"], 4 * num(a) + (p // 2 - 3))
                af(pt[:, p, :, 0:S + P], SCB[p % 2][:, :, 0:S + P], ACT.Exp, scale=SC)\
                    .then_inc(s["exp_done"], 1)

            def copy_out(a, hf):
                need(act, s["pv_done"], 4 * num(a) + (2 * hf + 2))
                need(act, s["ot_done"], num(a))
                af(ot[:, 2 * hf:2 * hf + 2, :].rearrange("p g n -> p (g n)"), OB[:, :], ACT.Copy)\
                    .then_inc(s["o_ready"], 1)

            def emit(i, front, vproj, attn, back, norm, route):
                f, v, a, r, u, q = batches(i)
                if front:
                    if peeled(i) == -2:
                        need(act, s["shift1_ready"], 1)
                    elif peeled(i) == SG // T - 2:
                        need(act, s["shift1_ready"], NT // SG)
                    need(act, s["xT_done"], num(f))
                    for t in range(T):
                        cols = slice(num(f) * T + t, num(f) * T + t + 1) if isinstance(f[0], int) else \
                            bass.ds(f[0] * (2 * T) + f[1] * T + t, 1)
                        last = af(xn[:, t * D:(t + 1) * D], xall[:, xtile(f, t, 1)], ACT.Identity,
                                  scale=rstd1[:, cols], bias=shift1[:, cols])
                    last.then_inc(s["xn_ready"], 1)
                if attn:
                    exps(a, 0)
                if norm:
                    need(act, s["h2_ready"], num(u) + 1)
                    need(act, s["ve3_ready"], num(u))
                    for t in range(T):
                        need(act, s["ss_ready"], 2 * num(u) + t)
                        af(sqj[:, :], h2[:, t, :], ACT.Square, scale=D ** -0.5, accum_out=ss[:, t:t + 1])\
                            .then_inc(s["ss_ready"], 1)
                if attn:
                    exps(a, 1)
                if back:
                    copy_out(r, 1)
                if front:
                    need(act, s["xT_done"], num(f) + 1)
                    need(act, s["ab_done"], num(f))
                    af(hT[:, :], FA[:, 0:S], ACT.Identity, scale=ca1T[:, col(f)], bias=saT[:, col(f)])\
                        .then_inc(s["hT_ready"], 1)
                if attn:
                    exps(a, 2)
                if norm:
                    need(act, s["h2t_done"], num(u) + 1)
                    need(act, s["lg_done"], num(u))
                    af(h2Ts[:, :], BK[:, 0:S], ACT.Copy).then_inc(s["h2ts_ready"], 1)
                if attn:
                    exps(a, 3)
                if norm:
                    need(act, s["rstd3_ready"], num(u) + 1)
                    need(act, scat[par(u)], half(u) * (DMA * 4))
                    for t in range(T):
                        last = af(pl[:, par(u), t, :, 0:D], h2[:, t:t + 1, :].to_broadcast([P, 2, D]), ACT.Copy,
                                  scale=rstd3[:, t:t + 1])
                    last.then_inc(s["pl_ready"], 1)
                if attn:
                    exps(a, 4)
                if back:
                    need(act, s["at_done"], num(r) + 1)
                    need(act, s["wo_done"], num(r))
                    af(aTs[:, :], BK[:, 0:S], ACT.Copy).then_inc(s["ats_ready"], 1)
                if attn:
                    exps(a, 5)
                if front:
                    need(act, s["k_done"], num(f) + 1)
                    need(act, s["k_out"], DMA * num(f))
                    af(ks[:, 0, :], FA[0:QR, :], ACT.Copy).then_inc(s["k1_ready"], 1)
                if front:
                    need(act, s["rk_ready"], num(f) + 1)
                    af(ks[:, 1, :], rk[:, :], ACT.Copy).then_inc(s["k2_ready"], 1)
                if attn:
                    copy_out(a, 0)
                if attn:
                    exps(a, 6)
                if norm:
                    need(act, s["dif_ready"], num(u) + 1)
                    af(ex[:, par(u), :], dif[:, :], ACT.Exp).then_inc(s["ex_ready"], 1)
                if front:
                    need(act, s["q_done"], num(f) + 1)
                    need(act, s["q_out"], DMA * num(f))
                    af(qs[:, 0, :], FB[0:QR, :], ACT.Copy).then_inc(s["q1_ready"], 1)
                if attn:
                    exps(a, 7)
                if front:
                    need(act, s["rq_ready"], num(f) + 1)
                    af(qs[:, 1, :], rq[:, :], ACT.Copy).then_inc(s["q2_ready"], 1)
                if vproj:
                    if peeled(i) == -1:
                        act.wait_ge(s["z_va"], 1)
                    need(act, s["v_done"], num(v) + 1)
                    need(act, s["pv_done"], 4 * num(v) - 4)
                    af(va[:, par(v), :, :].rearrange("p t (h v) -> p (t h) v", v=VW)[:, :, 0:DH],
                       FB[:, 0:S].rearrange("p (n v) -> p n v", v=DH), ACT.Copy).then_inc(s["v_ready"], 1)

            schedule(act, emit)

            af = nc.scalar.activation
            act.wait_ge(s["w_in"], 2 * DMA)
            af(gu[:, :], gu[:, :], ACT.Copy, scale=ws[:, W_NW:W_NW + 1]).then_inc(s["gu_ready"], 1)

            def step(k, x, g, h, d):
                if g:
                    b = plus(k, 1)
                    need(act, s["gu_done"], nb_(b) + 1)
                    need(act, s["hid_ready"], nb_(b) - 1)
                    af(sg[:, b[1] % 2, :], GUB[b[1] % 2][:, 0, 0:HID], ACT.Silu).then_inc(s["sg_ready"], 1)
                if h:
                    need(act, s["ht_done"], nb_(k) + 1)
                    need(act, s["y_done"], nb_(k) - 1)
                    af(hTs[:, k[1] % 2, :], HB[k[1] % 2][:, 0:HW], ACT.Copy).then_inc(s["hts_ready"], 1)

            block_steps(act, step)

        @block.vector
        def _(dve):
            V = nc.vector
            tt, ts, stt, cp = V.tensor_tensor, V.tensor_scalar, V.scalar_tensor_tensor, V.tensor_copy
            def stats(m):
                grp = slice(m * SG, (m + 1) * SG)
                for n in range(SG):
                    t = m * SG + n
                    V.bn_stats(st6[:, t, :], xall[:, t * D:(t + 1) * D]).then_inc(s["st6_ready"], 1)
                me, va_, rs, sh = mean1[:, grp], var1[:, grp], rstd1[:, grp], shift1[:, grp]
                st = st6[:, grp, :]
                need(dve, s["st6_ready"], m * SG + SG)
                tt(me, st[:, :, 1], st[:, :, 4], ALU.add)
                tt(dm1[:, :], st[:, :, 1], st[:, :, 4], ALU.subtract)
                tt(va_, st[:, :, 2], st[:, :, 5], ALU.add).then_inc(s["stat_step"], 1)
                need(dve, s["stat_step"], m * 2 + 1)
                ts(me, me, 0.5, None, ALU.mult)
                tt(dm1[:, :], dm1[:, :], dm1[:, :], ALU.mult)
                ts(va_, va_, 1.0 / D, LN_EPS, ALU.mult, ALU.add).then_inc(s["stat_step"], 1)
                need(dve, s["stat_step"], m * 2 + 2)
                stt(out=va_, in0=dm1[:, :], scalar=0.25, in1=va_, op0=ALU.mult, op1=ALU.add)\
                    .then_inc(s["mv1_ready"], 1)
                need(dve, s["rstd1_ready"], m + 1)
                stt(out=sh, in0=me, scalar=-1.0, in1=rs, op0=ALU.mult, op1=ALU.mult)\
                    .then_inc(s["shift1_ready"], 1)

            dve.wait_ge(s["x_in0"], DMA)
            stats(0)
            dve.wait_ge(s["mod_done"], 1)
            cp(saT[:, :], FA[:, 0:B])
            ts(ca1T[:, :], FA[:, B:2 * B], 1.0, None, ALU.add).then_inc(s["modt_ready"], 1)
            dve.wait_ge(s["ws_in"], DMA)
            ts(alpha[:, :], ws[:, W_AL:W_AL + 1], -0.5, 2.0, ALU.max, ALU.min).then_inc(s["mod_step"], 1)
            ts(mrow[:, D:2 * D], FB[0:B, 2 * D:3 * D], 1.0, None, ALU.add)
            cp(mrow[:, 2 * D:3 * D], FB[0:B, D:2 * D])
            step = 1
            for src, dst in ((0, 0), (3, 3)):
                g_in = FB[0:B, src * D:(src + 1) * D]
                dve.wait_ge(s["mod_step"], step)
                ts(msgn[:, :], g_in, 0.0, 0.5, ALU.is_ge, ALU.subtract)
                ts(mabs[:, :], g_in, -2.0, None, ALU.mult).then_inc(s["mod_step"], 1)
                dve.wait_ge(s["mod_step"], step + 1)
                stt(out=mabs[:, :], in0=g_in, scalar=2.0, in1=mabs[:, :], op0=ALU.mult, op1=ALU.max)\
                    .then_inc(s["mod_step"], 1)
                dve.wait_ge(s["mod_step"], step + 2)
                stt(out=mrow[:, dst * D:(dst + 1) * D], in0=mabs[:, :], scalar=0.5, in1=msgn[:, :],
                    op0=ALU.max, op1=ALU.mult).then_inc(s["mod_step"], 1)
                step += 3
            dve.wait_ge(s["mod_step"], step)
            ts(mrow[:, 4 * D:5 * D], mrow[:, 3 * D:4 * D], alpha[0:B, :], None, ALU.mult).then_inc(s["mrow_ready"], 1)
            dve.wait_ge(s["cst_in"], DMA)
            cp(ut_bf[:, :], cst[:, C_UT:C_UT + P]).then_inc(s["bf_ready"], 1)
            cp(one_bf[:, :], cst[:, C_ONE:C_ONE + P]).then_inc(s["bf_ready"], 1)
            for n in range(4):
                cp(mask4[:, n, :], cst[:, C_MASK:C_MASK + P]).then_inc(s["mask_ready"], 1)
            tt(ws[:, W_QA:W_QA + NG * QR], ws[:, W_QA:W_QA + NG * QR], cst[:, C_SIGN:C_SIGN + NG * QR], ALU.mult)
            ts(ws[:, W_R:W_R + E], ws[:, W_R:W_R + E], ws[:, W_NW:W_NW + 1], None, ALU.mult)\
                .then_inc(s["sign_ready"], 1)
            cp(base[:, :], cst[:, C_BASE0:C_BASE0 + E])
            cp(idf[:, :], cst[:, C_ID0:C_ID0 + 2 * T]).then_inc(s["base_init"], 1)
            def clip(a, p):
                need(dve, s["exp_done"], NPAIR * num(a) + (p + 1))
                diag = pt[:, p, :, :].rearrange("p h (n c) -> p (h n) c", c=2 * P)[:, :, 0:P]
                stt(out=diag, in0=diag, scalar=E_LO, in1=mask4[:, :, :], op0=ALU.max, op1=ALU.min)
                off = pt[:, p, :, P:2 * P]
                ts(off, off, E_LO, E_HI, ALU.max, ALU.min).then_inc(s["clip_done"], 1)

            def emit(i, front, vproj, attn, back, norm, route):
                f, v, a, r, u, q = batches(i)
                if norm:
                    need(dve, s["t1_ready"], num(u) + 1)
                    need(dve, s["rstd2_ready"], num(u) + 1)
                    need(dve, s["pl_ready"], num(u))
                    need(dve, s["gbh_ready"], num(u))
                    for t in range(T):
                        last = stt(out=h2[:, t, :], in0=t1[:, t, :], scalar=rstd2[:, t:t + 1],
                                   in1=bc[:, par(u), 2 * D:3 * D], op0=ALU.mult, op1=ALU.add)
                    last.then_inc(s["h2_ready"], 1)
                if attn:
                    clip(a, 0)
                if route:
                    need(dve, s["rank_done"], num(q) + 1)
                    rank = FB[:, 0:3 * E]
                    tt(pos[:, :, :], rank[:, 0:T * E].rearrange("p (t e) -> p t e", e=E),
                       base[:, :].rearrange("p (o e) -> p o e", o=1).to_broadcast([P, T, E]), ALU.add)\
                        .then_inc(s["pos_ready"], 1)
                    need(dve, s["ex_ready"], num(q) + 1)
                    need(dve, s["dest_ready"], num(q))
                    ts(den[:, :], ex[:, par(q), :], 1.0, None, ALU.add).then_inc(s["den_ready"], 1)
                    need(dve, s["pos_ready"], num(q) + 1)
                    tt(base[:, :], rank[:, 2 * E:3 * E], base[:, :], ALU.add).then_inc(s["bank_free"], 1)
                    ohq = oh[:, par(q), :, :, :]
                    for t in range(T):
                        last = tt(pd[:, t, :, :], ohq[:, t, :, :],
                                  pos[:, t:t + 1, :].to_broadcast([P, 2, E]), ALU.mult)
                    last.then_inc(s["pd_ready"], 1)
                    need(dve, s["pl_ready"], num(q) + 1)
                    need(dve, s["den_ready"], num(q) + 1)
                    V.reciprocal(pl[:, par(q), :, 0, D], den[:, :]).then_inc(s["c0_ready"], 1)
                if attn:
                    clip(a, 1)
                if route:
                    need(dve, s["pd_ready"], num(q) + 1)
                    V.tensor_reduce(destf[:, :], pd[:, :, :, :].rearrange("p t k e -> p (t k) e"), AX.X, ALU.add)\
                        .then_inc(s["destf_ready"], 1)
                    need(dve, s["c0_ready"], num(q) + 1)
                    tt(pl[:, par(q), :, 1, D], ex[:, par(q), :], pl[:, par(q), :, 0, D], ALU.mult)
                    cp(pl[:, par(q), :, :, D + 1].bitcast(i32), idf[:, :].rearrange("p (t k) -> p t k", k=2))\
                        .then_inc(s["id_ready"], 1)
                    need(dve, s["destf_ready"], num(q) + 1)
                    cp(dest[:, par(q), :], destf[:, :]).then_inc(s["dest_ready"], 1)
                    need(dve, s["id_ready"], num(q) + 1)
                    ts(idf[:, :], idf[:, :], float(S), None, ALU.add).then_inc(s["base_init"], 1)
                if attn:
                    clip(a, 2)
                if norm:
                    need(dve, s["lg_done"], num(u) + 1)
                    need(dve, s["rstd3_ready"], num(u) + 1)
                    for t in range(T):
                        last = ts(lg[:, t, :], BK[:, S + t * E:S + (t + 1) * E], rstd3[:, t:t + 1], None, ALU.mult)
                    last.then_inc(s["lg_ready"], 1)
                if front:
                    need(dve, s["ab_done"], num(f) + 1)
                    need(dve, s["v_done"], num(f) - 1)
                    tt(cc[:, par(f), :], FA[:, :], cst[:, C_TRIG:C_TRIG + 2 * S], ALU.mult)\
                        .then_inc(s["c_ready"], 1)
                if norm:
                    apart(dve)
                    need(dve, s["lg_ready"], num(u) + 1)
                    for t in range(T):
                        last = V.max(mx[:, t, :], lg[:, t, :])
                    last.then_inc(s["mx_ready"], 1)
                if attn:
                    clip(a, 3)
                if back:
                    need(dve, s["ot_done"], num(r) + 1)
                    need(dve, s["at_done"], num(r))
                    for t in range(T):
                        last = V.reciprocal(rden[:, t, :], (BK, FB)[t][:, :].rearrange("p (h v) -> p h v", v=VW)[:, :, DH])
                    last.then_inc(s["rden_ready"], 1)
                if norm:
                    apart(dve)
                    need(dve, s["mx_ready"], num(u) + 1)
                    for t in range(T):
                        last = V.max_index(mi[:, t, :], mx[:, t, :], lg[:, t, :])
                    last.then_inc(s["mi_ready"], 1)
                    need(dve, s["ex_ready"], num(u))
                    tt(dif[:, :], mx[:, :, 1], mx[:, :, 0], ALU.subtract).then_inc(s["dif_ready"], 1)
                if back:
                    need(dve, s["rden_ready"], num(r) + 1)
                    for t in range(T):
                        last = tt(at[:, t, :].rearrange("p (h v) -> p h v", v=DH),
                                  (BK, FB)[t][:, :].rearrange("p (h v) -> p h v", v=VW)[:, :, 0:DH],
                                  rden[:, t, :].rearrange("p (h o) -> p h o", o=1).to_broadcast([P, H, DH]), ALU.mult)
                    last.then_inc(s["norm_done"], 1)
                if norm:
                    need(dve, s["mi_ready"], num(u) + 1)
                    cp(mif[:, :, :], mi[:, :, 0:2]).then_inc(s["mif_ready"], 1)
                if attn:
                    clip(a, 4)
                if norm:
                    need(dve, s["mif_ready"], num(u) + 1)
                    ohr = oh[:, par(u), :, :, :]
                    for t in range(T):
                        last = tt(ohr[:, t, :, :],
                                  cst[:, C_IOTA:C_IOTA + E].rearrange("p (o e) -> p o e", o=1).to_broadcast([P, 2, E]),
                                  mif[:, t, :].rearrange("p (k o) -> p k o", o=1).to_broadcast([P, 2, E]), ALU.is_equal)
                    last.then_inc(s["oh_ready"], 1)
                if front:
                    need(dve, s["k1_ready"], num(f) + 1)
                    need(dve, s["k2_ready"], num(f))
                    need(dve, s["k3_ready"], num(f))
                    tt(rk[:, :], FA[0:QR, :], ks[:, 0, :], ALU.subtract).then_inc(s["rk_ready"], 1)
                if attn:
                    clip(a, 5)
                if norm:
                    need(dve, s["oh_ready"], num(u) + 1)
                    need(dve, s["rank_done"], num(u))
                    tt(tot[:, :].rearrange("p (t e) -> p t e", e=E), ohr[:, :, 0, :], ohr[:, :, 1, :], ALU.add)\
                        .then_inc(s["tot_ready"], 1)
                if back:
                    need(dve, s["wo_done"], num(r) + 1)
                    tt(xall[:, xtile(r)], BK[:, S:S + T * D], xall[:, xtile(r)], ALU.add).then_inc(s["x2_ready"], 1)
                if front:
                    need(dve, s["q1_ready"], num(f) + 1)
                    need(dve, s["q2_ready"], num(f))
                    need(dve, s["q3_ready"], num(f))
                    tt(rq[:, :], FB[0:QR, :], qs[:, 0, :], ALU.subtract).then_inc(s["rq_ready"], 1)
                if back:
                    apart(dve)
                    need(dve, s["x2_ready"], num(r) + 1)
                    for t in range(T):
                        last = V.bn_stats(st2[:, t, :], xall[:, xtile(r, t, 1)])
                    last.then_inc(s["st2_ready"], 1)
                if attn:
                    clip(a, 6)
                if back:
                    apart(dve)
                    need(dve, s["st2_ready"], num(r) + 1)
                    need(dve, s["ve2_ready"], num(r))
                    for t in range(T):
                        last = V.bn_aggr(mv2[:, t, :], st2[:, t, :])
                    last.then_inc(s["mv2_ready"], 1)
                if back:
                    need(dve, s["mv2_ready"], num(r) + 1)
                    need(dve, bc_in[par(r)], (half(r) + 1) * DMA)
                    for t in range(T):
                        last = stt(out=t1[:, t, :], in0=xall[:, xtile(r, t, 1)], scalar=mv2[:, t, 0:1],
                                   in1=bc[:, par(r), D:2 * D], op0=ALU.subtract, op1=ALU.mult)
                    last.then_inc(s["t1_ready"], 1)
                if attn:
                    clip(a, 7)
                if peeled(i) in STATS_AFTER:
                    dve.wait_ge(s["x_in"], 3 * DMA)
                    stats(STATS_AFTER[peeled(i)])

            schedule(dve, emit)

            V = nc.vector
            tt, ts, stt, cp = V.tensor_tensor, V.tensor_scalar, V.scalar_tensor_tensor, V.tensor_copy
            steps = [0]

            def chain(ins):
                steps[0] += 1
                ins.then_inc(s["table_step"], 1)
                dve.wait_ge(s["table_step"], steps[0])

            dve.wait_ge(s["bank_free"], B)
            cp(padi[:, :], base[0:1, :]).then_inc(s["pad_ready"], 1)
            tt(cnt[:, :], base[:, :], cst[:, C_BASE0:C_BASE0 + E], ALU.subtract)
            chain(V.memset(wrow[:, :], 1.0))
            chain(ts(cnti[:, :], cnt[:, :], float(P - 1), None, ALU.add))
            chain(ts(cnti[:, :], cnti[:, :], P.bit_length() - 1, None, ALU.arith_shift_right))
            chain(cp(nbf[:, :], cnti[:, :]))
            chain(V.tensor_tensor_scan(bend[:, :], wrow[:, :], nbf[:, :], 0.0, ALU.mult, ALU.add))
            J = cst[0:1, C_BLK:C_BLK + NBLK]
            tt(ge[:, :, :], J.rearrange("p (j o) -> p j o", o=1).to_broadcast([1, NBLK, E]),
               bend[0:1, :].rearrange("p (o e) -> p o e", o=1).to_broadcast([1, NBLK, E]), ALU.is_ge)
            chain(ts(wrow[:, :], nbf[:, :], -1.0, float(QBLK), ALU.mult, ALU.add))
            V.tensor_reduce(bf_[:, 0, :], ge[:, :, 0:NE1], AX.X, ALU.add)
            chain(tt(gw[:, :, :], ge[:, :, 0:NE1],
                     wrow[0:1, 0:NE1].rearrange("p (o e) -> p o e", o=1).to_broadcast([1, NBLK, NE1]), ALU.mult))
            chain(V.tensor_reduce(bf_[:, 1, :], gw[:, :, :], AX.X, ALU.add))
            chain(tt(bf_[:, 1, :], bf_[:, 1, :], J, ALU.add))
            chain(ts(bf_[:, 2, :], bf_[:, 1, :], -1.0, float(DUMMY), ALU.mult, ALU.add))
            chain(tt(bf_[:, 2, :], bf_[:, 2, :], ge[:, :, NE1], ALU.mult))
            chain(tt(bf_[:, 1, :], bf_[:, 1, :], bf_[:, 2, :], ALU.add))
            cp(bi[:, 0, :], bf_[:, 0, :])
            ts(bi[:, 1, :], bf_[:, 1, :], float(P), None, ALU.mult).then_inc(s["table_ready"], 1)

            V.memset(hid[:, :, HID:HW], 0.0).then_inc(s["z_hid"], 1)

            def step(k, x, g, h, d):
                if x:
                    b = plus(k, 2)
                    need(dve, s["xt_done"], nb_(b) + 1)
                    need(dve, s["gu_done"], nb_(b) - 1)
                    cp(xTs[:, b[1] % 2, :], XP[:, 0:P]).then_inc(s["xts_ready"], 1)
                if g:
                    b = plus(k, 1)
                    need(dve, s["sg_ready"], nb_(b) + 1)
                    need(dve, s["ht_done"], nb_(b) - 1)
                    tt(hid[:, b[1] % 2, 0:HID], sg[:, b[1] % 2, :], GUB[b[1] % 2][:, 1, 0:HID], ALU.mult)\
                        .then_inc(s["hid_ready"], 1)
                if d:
                    b = plus(k, -1)
                    need(dve, s["y_done"], nb_(b) + 1)
                    need(dve, yscat[slot(b)], uses(b) * DMA)
                    ts(ysb[:, slot(b), :], YP[:, 0:D], xb[:, slot(b), D:D + 1], None, ALU.mult)\
                        .then_inc(s["y_ready"], 1)

            block_steps(dve, step)
            dve.wait_ge(s["gba_in"], DMA)
            bch = TCH // T
            for n in range(NCH):
                dve.wait_ge(s[f"yin{n}"], 2 * DMA)
                c0, c1 = n * TCH * D, (n + 1) * TCH * D
                tt(ybuf[0][:, c0:c1], ybuf[0][:, c0:c1], ybuf[1][:, c0:c1], ALU.add).then_inc(s["sum1"], 1)
                dve.wait_ge(s["sum1"], n + 1)
                for m in range(bch):
                    y = ybuf[0][:, c0 + m * T * D:c0 + (m + 1) * T * D].rearrange("p (t d) -> p t d", d=D)
                    last = tt(y, y, gba[:, n * bch + m:n * bch + m + 1, :].to_broadcast([P, T, D]), ALU.mult)
                last.then_inc(s["sum2"], 1)

        @block.gpsimd
        def _(pool):
            G = nc.gpsimd
            G.memset(epst[:, 0:T], LN_EPS)
            G.memset(epst[:, T:2 * T], RMS_EPS)
            G.memset(mhalf[:, :], -0.5).then_inc(s["z_half"], 1)
            pool.wait_ge(s["z_half"], 1)
            pool.wait_ge(s["mv1_ready"], 1)
            G.tensor_tensor(rstd1[:, 0:SG], var1[:, 0:SG], mhalf[:, 0:SG], ALU.pow).then_inc(s["rstd1_ready"], 1)
            pool.wait_ge(s["rstd1_ready"], 1)
            for st in (stq, stk):
                for par_ in range(2):
                    G.memset(st[64:KST, par_, :, :].rearrange("p h n -> p (h n)").bitcast(fp32), 0.0)\
                        .then_inc(s["z_stack"], 1)
            pool.wait_ge(s["z_stack"], 4)
            G.memset(va[:, :, :, :], 1.0).then_inc(s["z_va"], 1)
            pool.wait_ge(s["z_va"], 1)

            def emit(i, front, vproj, attn, back, norm, route):
                f, v, a, r, u, q = batches(i)
                if norm:
                    need(pool, s["ss_ready"], 2 * num(u) + 2)
                    G.tensor_tensor(ve3[:, :], ss[:, :], epst[:, T:2 * T], ALU.add)\
                        .then_inc(s["ve3_ready"], 1)
                    need(pool, s["ve3_ready"], num(u) + 1)
                    need(pool, s["lg_ready"], num(u))
                    need(pool, s["pl_ready"], num(u))
                    G.tensor_tensor(rstd3[:, :], ve3[:, :], mhalf[:, 0:T], ALU.pow).then_inc(s["rstd3_ready"], 1)
                    for t in range(T):
                        last = G.tensor_tensor(gbh[:, t, :], h2[:, t, :], bc[:, par(u), 3 * D:4 * D], ALU.mult)
                    last.then_inc(s["gbh_ready"], 1)
                    need(pool, s["gbh_ready"], num(u) + 1)
                    G.tensor_tensor(xall[:, xtile(u)], xall[:, xtile(u)], gbh[:, :, :].rearrange("p t d -> p (t d)"),
                                    ALU.add).then_inc(s["base_ready"], 1)
                if back:
                    need(pool, bc_in[par(r)], (half(r) + 1) * DMA)
                    need(pool, s["wo_done"], num(r))
                    G.tensor_tensor(wog[:, :], ws[:, W_O:W_O + D], bc[:, par(r), 0:D], ALU.mult)\
                        .then_inc(s["wog_ready"], 1)
                if route:
                    apart(pool)
                    need(pool, s["dest_ready"], num(q) + 1)
                    need(pool, s["pl_ready"], num(q) + 1)
                    for t in range(T):
                        for k in range(2):
                            G.indirect_dma_start(
                                queue, bass.IndirectOffsetOnAxis(dest[:, par(q), 2 * t + k:2 * t + k + 1], 0),
                                pl[:, par(q), t, k, :], None).then_inc(scat[par(q)], DMA)
                if front:
                    need(pool, s["k2_ready"], num(f) + 1)
                    G.tensor_tensor(ks[:, 2, :], rk[:, :], ks[:, 1, :], ALU.subtract).then_inc(s["k3_ready"], 1)
                    need(pool, s["q2_ready"], num(f) + 1)
                    G.tensor_tensor(qs[:, 2, :], rq[:, :], qs[:, 1, :], ALU.subtract).then_inc(s["q3_ready"], 1)
                if back:
                    need(pool, s["mv2_ready"], num(r) + 1)
                    G.tensor_tensor(ve2[:, :], mv2[:, :, 1], epst[:, 0:T], ALU.add).then_inc(s["ve2_ready"], 1)
                    need(pool, s["ve2_ready"], num(r) + 1)
                    need(pool, s["h2_ready"], num(r))
                    G.tensor_tensor(rstd2[:, :], ve2[:, :], mhalf[:, 0:T], ALU.pow).then_inc(s["rstd2_ready"], 1)
                if peeled(i) in STATS_AFTER:
                    m = STATS_AFTER[peeled(i)]
                    grp = slice(m * SG, (m + 1) * SG)
                    pool.wait_ge(s["mv1_ready"], m + 1)
                    G.tensor_tensor(rstd1[:, grp], var1[:, grp], mhalf[:, 0:SG], ALU.pow)\
                        .then_inc(s["rstd1_ready"], 1)

            schedule(pool, emit)

            G = nc.gpsimd
            below = G.to_reg(2 * NTOK - 2)
            bound = pool.alloc_register("bound")

            def step(k, x, g, h, d):
                if not d:
                    return
                b = plus(k, -1)
                need(pool, s["y_ready"], nb_(b) + 1)
                pool.reg_add(bound, below, 1)
                G.indirect_dma_start(ydram, bass.IndirectOffsetOnAxis(xb[:, slot(b), D + 1:D + 2].bitcast(u32), 0),
                                     ysb[:, slot(b), :], None, bounds_check=bound, oob_is_err=False)\
                 .then_inc(yscat[slot(b)], DMA)

            block_steps(pool, step)
            pool.wait_ge(s["base_ready"], B)
            for n in range(NCH):
                pool.wait_ge(s["sum2"], n + 1)
                c0, c1 = n * TCH * D, (n + 1) * TCH * D
                G.tensor_tensor(xall[:, c0:c1], xall[:, c0:c1], ybuf[0][:, c0:c1], ALU.add).then_inc(s["sum3"], 1)



def host_constants():
    c = np.zeros((P, CW), np.float32)
    p = np.arange(P)
    c[:, C_ID:C_ID + P] = np.eye(P)
    c[:, C_UT:C_UT + P] = p[:, None] < p[None, :]
    c[:, C_ONE:C_ONE + P] = 1.0
    c[:, C_MASK:C_MASK + P] = np.where(p[None, :] >= p[:, None], np.float32(E_HI), 0.0)
    inv = np.float32(10000.0) ** (-np.arange(0, DR, 2, dtype=np.float32) / np.float32(DR))
    ang = np.arange(S, dtype=np.float32)[:, None] * inv
    cos, sin = np.cos(ang).T, np.sin(ang).T
    for n, row in enumerate((cos[0], sin[0], cos[1], sin[1])):
        c[n * DL:(n + 1) * DL, C_TRIG:C_TRIG + S] = row
    second = slice(C_TRIG + S, C_TRIG + 2 * S)
    c[0:DL, second] = 1.0
    for d in range(DR):
        c[DL + d, second] = cos[d // 2]
        c[DL + DR + d, second] = sin[d // 2] * (1.0 if d % 2 else -1.0)
    c[2 * DL:3 * DL, second] = 1.0
    sign = np.ones((P, NG, DQK, HG), np.float32)
    sign[DL:2 * DL, :, DH, :] = -1.0
    sign[3 * DL:4 * DL, :, DH + 2, :] = -1.0
    c[:, C_SIGN:C_SIGN + NG * QR] = sign.reshape(P, -1)
    c[:, C_IOTA:C_IOTA + E] = np.arange(E)
    c[:, C_BASE0:C_BASE0 + E] = np.arange(E) * QROWS
    for t in range(T):
        for k in range(2):
            c[:, C_ID0 + 2 * t + k] = k * NTOK + t * P + p
    c[:, C_BLK:C_BLK + NBLK] = np.arange(NBLK)
    c[:, C_PAD + D + 1] = np.full(P, PADID, np.int32).view(np.float32)
    return c


def host_layout(a):
    w = np.zeros((P, WW), np.float32)
    dq, uq, qr = a["L0_attn_W_DQ"], a["L0_attn_W_UQ"], a["L0_attn_W_QR"]
    for n in range(4):
        w[:, W_A + n * DL:W_A + (n + 1) * DL] = dq
    w[:, W_B:W_B + DL] = a["L0_attn_W_DKV"]
    w[:, W_B + DL:W_B + DL + DR] = a["L0_attn_W_KR"]
    w[:, W_B + DL + DR:W_B + DL + 2 * DR] = a["L0_attn_W_KR"][:, [1, 0, 3, 2]]
    w[:, W_B + 2 * DL:W_B + 3 * DL] = dq
    qa = np.zeros((P, NG, DQK, HG), np.float32)
    q4 = qr.reshape(DL, HG, NG, DR).transpose(0, 2, 1, 3)
    for freq in range(2):
        c_rows = slice(2 * freq * DL, (2 * freq + 1) * DL)
        s_rows = slice((2 * freq + 1) * DL, (2 * freq + 2) * DL)
        for d in range(2):
            qa[c_rows, :, DH + 2 * freq + d, :] = q4[:, :, :, 2 * freq + d]
            qa[s_rows, :, DH + 2 * freq + d, :] = q4[:, :, :, 2 * freq + 1 - d]
    w[:, W_QA:W_QA + NG * QR] = qa.reshape(P, -1)
    qb = np.zeros((P, NG, DQK, HG), np.float32)
    qb[2 * DL:3 * DL, :, 0:DH, :] = uq.reshape(DL, HG, NG, DH).transpose(0, 2, 3, 1)
    w[:, W_QB:W_QB + NG * QR] = qb.reshape(P, -1)
    kb = np.zeros((P, NG, DQK, HG), np.float32)
    kb[0:DL, :, 0:DH, :] = a["L0_attn_W_UK"].reshape(DL, HG, NG, DH).transpose(0, 2, 3, 1)
    for d in range(DR):
        kb[DL + d, :, DH + d, :] = 1.0
        kb[DL + DR + d, :, DH + d, :] = 1.0
    w[:, W_K:W_K + NG * QR] = kb.reshape(P, -1)
    w[0:DL, W_V:W_V + H * DH] = a["L0_attn_W_UV"]
    w[:, W_O:W_O + D] = a["L0_attn_W_O"]
    w[:, W_R:W_R + E] = a["L0_ffn_router_weight"].T
    w[:, W_NW] = a["L0_ffn_norm_weight"]
    w[:, W_AL] = a["L0_ffn_residual_alpha"]
    w[:, W_CT:W_CT + B] = a["L0_c"].T
    gup = np.ascontiguousarray(a["L0_ffn_gate_up_weight"].transpose(2, 0, 1).reshape(P, E * 2 * HID))
    dn = np.zeros((E, 3 * P, D), np.float32)
    dn[:, 0:HID, :] = a["L0_ffn_down_weight"].transpose(0, 2, 1)
    dn = np.ascontiguousarray(dn.reshape(E, 3, P, D).transpose(2, 0, 1, 3).reshape(P, E * 3 * D))
    return w, gup, dn


def kernel(**inputs):
    import concourse.bacc as bacc
    from concourse.bass_utils import run_bass_kernel_spmd

    a = {k: np.asarray(v) for k, v in inputs.items()}
    w, gup, dn = host_layout(a)
    arrays = {"x": np.ascontiguousarray(a["L0_attn_x"]), "consts": host_constants(), "wsmall": w,
              "wmod": np.ascontiguousarray(a["L0_wmod"]), "gup": gup, "down": dn}
    nc = bacc.Bacc("TRN2", target_bir_lowering=False, num_devices=1)
    args = [nc.dram_tensor(n, v.shape, mybir.dt.float32, kind="ExternalInput").ap() for n, v in arrays.items()]
    out = nc.dram_tensor("out", (B, S, D), mybir.dt.float32, kind="ExternalOutput").ap()
    adaln_kernel(nc, *args, out)
    r = run_bass_kernel_spmd(nc, [arrays], core_ids=[0])
    return r.results[0]["out"]
```

```python
import math

import numpy as np

import concourse.bass as bass
from concourse import mybir
from contextlib import ExitStack

B, S, D = 16, 256, 128
P = 128
T = S // P
H, DH, DR, DL = 16, 8, 4, 32
DQK = DH + DR
E, HID = 8, 352
HW = 3 * P
NT = B * T
NTOK = B * S
SG = 8
STATS_AFTER = {-1: 1, 0: 2, 1: 3}
LN_EPS, RMS_EPS = 1e-5, 1e-6
SC = 1.0 / math.sqrt(DQK)
E_HI = float(np.exp(np.float32(80.0) * np.float32(SC)))
E_LO = float(np.exp(np.float32(-80.0) * np.float32(SC)))

HG = 8
QR = HG * DQK
NG = H // HG
COMBOS = [(0, 0), (0, 1), (1, 0), (0, 2), (2, 0), (1, 1)]
NC = len(COMBOS)
STAGES = (-3, -2, -1, 0, 1, 2, 3)
KST = 96
NPAIR = H // 2
VW = 32

QBLK = NTOK // P + 1
QROWS = QBLK * P
DUMMY = E * QBLK
NBLK = (2 * NTOK) // P + E - 1
PAYW = D + 2
PADID = 1 << 20

C_ID, C_UT, C_ONE, C_MASK, C_TRIG, C_SIGN = 0, 128, 256, 384, 512, 1024
C_IOTA = C_SIGN + NG * QR
C_BASE0 = C_IOTA + E
C_ID0 = C_BASE0 + E
C_BLK = C_ID0 + 4
C_PAD = C_BLK + NBLK
CW = C_PAD + PAYW
W_A, W_B, W_QA, W_QB, W_K, W_V, W_O, W_R = 0, 128, 256, 448, 640, 832, 960, 1088
W_NW, W_AL, W_CT, WW = 1096, 1097, 1098, 1114


def adaln_kernel(nc, x, consts, wsmall, wmod, gup, down, out):
    fp32, bf16 = mybir.dt.float32, mybir.dt.bfloat16
    i32, u32 = mybir.dt.int32, mybir.dt.uint32
    ALU, ACT, AX = mybir.AluOpType, mybir.ActivationFunctionType, mybir.AxisListType

    queue = nc.dram_tensor("queue", [(DUMMY + 1) * P, PAYW], fp32).ap()
    ydram = nc.dram_tensor("ydram", [2 * NTOK, D], fp32).ap()
    qdram = nc.dram_tensor("qdram", [2, 3, QR, NG * S], bf16).ap()
    kdram = nc.dram_tensor("kdram", [2, 3, QR, NG * S], bf16).ap()
    modrow = nc.dram_tensor("modrow", [B, 5 * D], fp32).ap()

    ctx = ExitStack()
    with ctx:
        def sb(name, shape, dt=fp32):
            return ctx.enter_context(nc.sbuf_tensor(name, shape, dt))

        def sem(name):
            return ctx.enter_context(nc.semaphore(name))

        cst = sb("cst", [P, CW])
        ws = sb("ws", [P, WW])
        wm = sb("wm", [P, 6 * D])
        xall = sb("xall", [P, NT * D])
        gu = sb("gu", [P, E * 2 * HID])
        dn = sb("dn", [P, E * 3 * D])
        ut_bf = sb("ut_bf", [P, P], bf16)
        one_bf = sb("one_bf", [P, P], bf16)
        mask4 = sb("mask4", [P, 4, P])
        st6 = sb("st6", [P, NT, 6])
        nmean1 = sb("nmean1", [P, NT])
        rstd1 = sb("rstd1", [P, NT])
        shift1 = sb("shift1", [P, NT])
        var1 = sb("var1", [P, NT])
        dm1 = sb("dm1", [P, SG])
        mhalf = sb("mhalf", [P, NT])
        epst = sb("epst", [P, 2 * T])
        scT = sb("scT", [P, B])
        saT = sb("saT", [P, B])
        ca1T = sb("ca1T", [P, B])
        mrow = sb("mrow", [B, 5 * D])
        msgn = sb("msgn", [B, D])
        mabs = sb("mabs", [B, D])
        alpha = sb("alpha", [P, 1])
        bc = sb("bc", [P, 2, 4 * D])
        xn = sb("xn", [P, T * D])
        hT = sb("hT", [P, S])
        cc = sb("cc", [P, 2, 2 * S])
        qs = sb("qs", [QR, 3, NG * S], bf16)
        ks = sb("ks", [QR, 3, NG * S], bf16)
        rq = sb("rq", [QR, NG * S])
        rk = sb("rk", [QR, NG * S])
        stq = sb("stq", [P, 2, H, S], bf16)
        stk = sb("stk", [P, 2, H, S], bf16)
        va = sb("va", [P, 2, T, H * VW])
        pt = sb("pt", [P, NPAIR, 2, 2 * S])
        ot = sb("ot", [P, 4, S])
        rden = sb("rden", [P, T, H])
        at = sb("at", [P, T, H * DH])
        aTs = sb("aTs", [P, S])
        wog = sb("wog", [P, D])
        st2 = sb("st2", [P, T, 6])
        mv2 = sb("mv2", [P, T, 2])
        ve2 = sb("ve2", [P, T])
        rstd2 = sb("rstd2", [P, T])
        t1 = sb("t1", [P, T, D])
        h2 = sb("h2", [P, T, D])
        gbh = sb("gbh", [P, T, D])
        h2Ts = sb("h2Ts", [P, S])
        sqj = sb("sqj", [P, D])
        ss = sb("ss", [P, T])
        ve3 = sb("ve3", [P, T])
        rstd3 = sb("rstd3", [P, T])
        pl = sb("pl", [P, 2, T, 2, PAYW])
        lg = sb("lg", [P, T, E])
        mx = sb("mx", [P, T, 8])
        mi = sb("mi", [P, T, 8], u32)
        mif = sb("mif", [P, T, 2])
        oh = sb("oh", [P, 2, T, 2, E])
        tot = sb("tot", [P, T * E], bf16)
        dif = sb("dif", [P, T])
        ex = sb("ex", [P, 2, T])
        den = sb("den", [P, T])
        base = sb("base", [P, E])
        pos = sb("pos", [P, T, E])
        pd = sb("pd", [P, T, 2, E])
        destf = sb("destf", [P, T * 2])
        dest = sb("dest", [P, 2, T * 2], u32)
        idf = sb("idf", [P, T * 2])

        SCB = [ctx.enter_context(nc.psum_tensor(f"SC{n}", [P, 2, 512], fp32)) for n in range(2)]
        OB, FA, FB, BK = (ctx.enter_context(nc.psum_tensor(n, [P, 512], fp32)) for n in ("OB", "FA", "FB", "BK"))

        ident = cst[:, C_ID:C_ID + P]

        names = """cst_in x_in0 x_in ws_in wm_in w_in bc_in0 bc_in1 modrow_out dummy_out
            z_stack z_va z_half bf_ready mask_ready st6_ready shift1_ready mv1_ready rstd1_ready
            sil_ready mod_done modt_ready
            mod_step mrow_ready sign_ready stat_step base_init
            xn_ready xT_done hT_ready ab_done c_ready q_done k_done v_done q1_ready k1_ready rq_ready rk_ready
            q2_ready k2_ready q3_ready k3_ready v_ready stq0 stq1 stk0 stk1
            sc_done exp_done clip_done pv_done o_ready ot_done rden_ready norm_done at_done ats_ready wog_ready
            wo_done x2_ready st2_ready mv2_ready ve2_ready rstd2_ready t1_ready h2_ready h2t_done h2ts_ready
            ss_ready ve3_ready rstd3_ready pl_ready gbh_ready base_ready lg_done lg_ready mx_ready mi_ready
            mif_ready oh_ready tot_ready dif_ready ex_ready rank_done pos_ready bank_free pd_ready destf_ready
            den_ready q_out k_out dest_ready c0_ready id_ready scat0 scat1""".split()
        s = {n: sem(n) for n in names}
        stq_in, stk_in = [s["stq0"], s["stq1"]], [s["stk0"], s["stk1"]]
        bc_in, scat = [s["bc_in0"], s["bc_in1"]], [s["scat0"], s["scat1"]]
        DMA = 16

        def need(eng, sm, value):
            if isinstance(value, int) and value <= 0:
                return
            eng.wait_ge(sm, value)

        def apart(eng):
            eng.wait_ge(s["cst_in"], DMA)

        def schedule(eng, emit):
            def stages(i):
                return [0 <= i - behind < B for behind in STAGES]

            for i in range(-3, 4):
                emit((0, i), *stages(i))
            with eng.Fori(2, 6) as j:
                emit((j, 0), *stages(4))
                emit((j, 1), *stages(5))
            for i in range(12, B + 3):
                emit((0, i), *stages(i))

        def batches(i):
            return [(i[0], i[1] - behind) for behind in STAGES]

        def num(b):
            return 2 * b[0] + b[1]

        def peeled(i):
            return num(i) if isinstance(i[0], int) else None

        def par(b):
            return b[1] % 2

        def half(b):
            return b[0] + b[1] // 2

        def xtile(b, t=0, n=T):
            if isinstance(b[0], int):
                return slice((num(b) * T + t) * D, (num(b) * T + t + n) * D)
            return bass.ds(b[0] * (2 * T * D) + (b[1] * T + t) * D, n * D)

        def col(b, n=1):
            if isinstance(b[0], int):
                return slice(num(b) * n, num(b) * n + n)
            return bass.ds(b[0] * (2 * n) + b[1] * n, n)

        NE1 = E - 1
        XBUF = 8
        UNR2 = XBUF
        M0, M1 = 2, (NBLK - 2) // UNR2

        cnt = sb("cnt", [P, E])
        cnti = sb("cnti", [P, E], i32)
        nbf = sb("nbf", [P, E])
        bend = sb("bend", [P, E])
        padi = sb("padi", [1, E], i32)
        wrow = sb("wrow", [P, E])
        ge = sb("ge", [1, NBLK, E])
        gw = sb("gw", [1, NBLK, NE1])
        bf_ = sb("bf_", [1, 3, NBLK])
        bi = sb("bi", [1, 2, NBLK], i32)
        xb = sb("xb", [P, XBUF, PAYW])
        xTs = sb("xTs", [P, 2, P])
        sg = sb("sg", [P, 2, HW])
        hidT = sb("hidT", [P, 2, HW])
        wgu = sb("wgu", [P, 2, 2, HW])
        ysb = sb("ysb", [P, XBUF, D])
        gba = pt[:, 0:2, :, :].rearrange("p s h c -> p (s h c)").rearrange("p (b d) -> p b d", d=D)
        NCH = 8
        TCH = NT // NCH
        ybuf = [st[:, :, :, :].rearrange("p a h n -> p (a h n)").bitcast(fp32) for st in (stq, stk)]
        GUB, XP, YP = SCB, (OB, FA), (FB, BK)

        names2 = """table_step table_ready pad_ready padded z_wgu wgu_ready gba_in xt_done xts_ready gu_done
            sg_ready hid_ready y_done y_ready yin0 yin1 yin2 yin3 yin4 yin5 yin6 yin7
            sum1 sum2 sum3 out_done""".split()
        s.update({n: sem(n) for n in names2})
        xb_in = [sem(f"xb_in{n}") for n in range(XBUF)]
        yscat = [sem(f"yscat{n}") for n in range(XBUF)]

        def nb_(k):
            return UNR2 * k[0] + k[1]

        def slot(k):
            return k[1] % XBUF

        def uses(k):
            return k[0] + k[1] // XBUF

        def block_steps(eng, step):
            step((0, -2), True, False, False)
            step((0, -1), True, True, False)
            step((0, 0), True, True, False)
            for n in range(1, M0 * UNR2):
                step((0, n), True, True, True)
            with eng.Fori(M0, M1) as m:
                for n in range(UNR2):
                    step((m, n), True, True, True)
            for n in range(M1 * UNR2, NBLK - 2):
                step((0, n), True, True, True)
            step((0, NBLK - 2), False, True, True)
            step((0, NBLK - 1), False, False, True)
            step((0, NBLK), False, False, True)

        REGS, LOADED = 8, 4

        def expert_registers(eng):
            experts = [eng.alloc_register(f"expert{n}") for n in range(REGS)]

            def load(k):
                n = LOADED if not isinstance(k[0], int) else min(LOADED, NBLK - nb_(k))
                if n <= 0:
                    return
                at = slice(nb_(k), nb_(k) + n) if isinstance(k[0], int) else bass.ds(k[0] * UNR2 + k[1], n)
                eng.reg_load([experts[(k[1] + c) % REGS] for c in range(n)], bi[0:1, 0, at])

            def expert(b):
                return nc.snap(experts[b[1] % REGS]).with_bounds(min_val=0, max_val=E - 1)

            return load, expert

        def plus(k, n):
            return (k[0], k[1] + n)

        block = ctx.enter_context(nc.Block())

        @block.sync
        def _(sp):
            xv = x.rearrange("b (t p) d -> p (b t) d", p=P)
            xs = xall[:, :].rearrange("p (n d) -> p n d", d=D)
            sp.dma_start(xs[:, 0:8, :], xv[:, 0:8, :]).then_inc(s["x_in0"], DMA)
            sp.dma_start(ws[:, :], wsmall).then_inc(s["ws_in"], DMA)
            sp.dma_start(wm[:, :], wmod).then_inc(s["wm_in"], DMA)
            sp.dma_start(cst[:, :], consts).then_inc(s["cst_in"], DMA)
            for n in range(1, 4):
                sp.dma_start(xs[:, 8 * n:8 * n + 8, :], xv[:, 8 * n:8 * n + 8, :]).then_inc(s["x_in"], DMA)
            sp.wait_ge(s["mrow_ready"], 1)
            sp.dma_start(modrow, mrow[:, :]).then_inc(s["modrow_out"], DMA)
            sp.wait_ge(s["cst_in"], DMA)
            sp.dma_start(queue[DUMMY * P:(DUMMY + 1) * P, :], cst[:, C_PAD:C_PAD + PAYW]).then_inc(s["dummy_out"], DMA)
            sp.wait_ge(s["modrow_out"], DMA)
            sp.wait_ge(s["z_stack"], 4)

            def load_bc(a):
                need(sp, s["base_ready"], num(a) - 1)
                src = modrow[col(a), 0:4 * D].to_broadcast([P, 4 * D])
                sp.dma_start(bc[:, par(a), :], src).then_inc(bc_in[par(a)], DMA)

            def part_out(parts, dram, ready, written, f):
                apart(sp)
                for r in ready:
                    need(sp, s[r], num(f) + 1)
                need(sp, s["pv_done"], 4 * num(f) - 7)
                sp.dma_start(dram[par(f)].rearrange("s q n -> q s n"), parts[:, :, :]).then_inc(s[written], DMA)

            def stack(dram, dst, arrived, written, side, f):
                need(sp, s[written], DMA * num(f) + DMA)
                need(sp, s["sc_done"], NPAIR * num(f) - NPAIR)
                for n, combo in enumerate(COMBOS):
                    sp.dma_start(dst[n * DQK:(n + 1) * DQK, par(f), :, :],
                                 dram[par(f), combo[side]].rearrange("(r h) (g n) -> r (h g) n", h=HG, g=NG))\
                      .then_inc(arrived[par(f)], DMA)

            def emit(i, pre, front, vproj, attn, back, norm, route):
                g, f, v, a, r, u, q = batches(i)
                if front:
                    part_out(ks, kdram, ("k1_ready", "k2_ready", "k3_ready"), "k_out", f)
                    part_out(qs, qdram, ("q1_ready", "q2_ready", "q3_ready"), "q_out", f)
                if attn:
                    load_bc(a)
                if front:
                    stack(kdram, stk, stk_in, "k_out", 1, f)
                    stack(qdram, stq, stq_in, "q_out", 0, f)
                if peeled(i) == B - 1:
                    sp.dma_start(gu[:, :], gup).then_inc(s["w_in"], DMA)
                    sp.dma_start(dn[:, :], down).then_inc(s["w_in"], DMA)

            schedule(sp, emit)

            sp.wait_ge(s["pad_ready"], 1)
            _, rows = nc.values_load_multi_w_load_instructions(
                padi[0:1, :], engines=[mybir.EngineType.SP], min_val=0, max_val=DUMMY * P - P)
            for row in rows:
                sp.dma_start(queue[bass.ds(row, P), :], cst[:, C_PAD:C_PAD + PAYW]).then_inc(s["padded"], DMA)
            def load(k, count, ready=lambda: None):
                first = nb_(k)
                at = slice(first, first + count) if isinstance(k[0], int) else bass.ds(k[0] * UNR2, count)
                apart(sp)
                _, rows = nc.values_load_multi_w_load_instructions(
                    bi[0:1, 1, at], engines=[mybir.EngineType.SP], min_val=0, max_val=DUMMY * P)
                ready()
                for n, row in enumerate(rows):
                    b = plus(k, n)
                    need(sp, yscat[slot(b)], uses(b) * DMA)
                    sp.dma_start(xb[:, slot(b), :], queue[bass.ds(row, P), :]).then_inc(xb_in[slot(b)], DMA)

            def queues_written():
                sp.wait_ge(scat[0], B // 2 * 4 * DMA)
                sp.wait_ge(scat[1], B // 2 * 4 * DMA)
                sp.wait_ge(s["dummy_out"], DMA)
                sp.wait_ge(s["padded"], E * DMA)

            sp.wait_ge(s["table_ready"], 1)
            load((0, 0), UNR2, queues_written)
            sp.wait_ge(s["pv_done"], 4 * B)
            gb_rows = modrow[:, 4 * D:5 * D].rearrange("(o b) d -> o b d", o=1)
            sp.dma_start(gba[:, :, :], gb_rows.to_broadcast([P, B, D])).then_inc(s["gba_in"], DMA)
            with sp.Fori(1, M1) as m:
                load((m, 0), UNR2)
            load((M1, 0), NBLK - M1 * UNR2)
            for n in range(XBUF):
                sp.wait_ge(yscat[n], (NBLK - n + XBUF - 1) // XBUF * DMA)
            yv = ydram.rearrange("(k n p) d -> p k n d", p=P, k=2)
            ov = out.rearrange("b (t p) d -> p (b t) d", p=P)
            for n in range(NCH):
                for k in range(2):
                    sp.dma_start(ybuf[k][:, n * TCH * D:(n + 1) * TCH * D].rearrange("p (t d) -> p t d", d=D),
                                 yv[:, k, n * TCH:(n + 1) * TCH, :]).then_inc(s[f"yin{n}"], DMA)
            for n in range(NCH):
                sp.wait_ge(s["sum3"], n + 1)
                sp.dma_start(ov[:, n * TCH:(n + 1) * TCH, :],
                             xall[:, n * TCH * D:(n + 1) * TCH * D].rearrange("p (t d) -> p t d", d=D))\
                  .then_inc(s["out_done"], DMA)
            sp.wait_ge(s["out_done"], NCH * DMA)

        @block.tensor
        def _(pe):
            mm = nc.tensor.matmul
            pe.wait_ge(s["sil_ready"], 1)
            pe.wait_ge(s["wm_in"], DMA)
            mm(OB[:, 0:B], wm[:, 0:D], scT[:, :], start=True, stop=True)
            mm(OB[:, B:2 * B], wm[:, D:2 * D], scT[:, :], start=True, stop=True).then_inc(s["mod_done"], 1)
            mm(BK[0:B, 0:4 * D], scT[:, :], wm[:, 2 * D:6 * D], start=True, stop=True).then_inc(s["mod_done"], 1)
            pe.wait_ge(s["cst_in"], DMA)

            def scores(a, p):
                if p == 0:
                    need(pe, stq_in[par(a)], (half(a) + 1) * (DMA * NC))
                    need(pe, stk_in[par(a)], (half(a) + 1) * (DMA * NC))
                need(pe, s["exp_done"], NPAIR * num(a) + (p - 1))
                for hh in range(2):
                    h = 2 * p + hh
                    dst = SCB[p % 2][:, hh, :]
                    mm(dst[:, 0:S], stk[0:KST, par(a), h, 0:P], stq[0:KST, par(a), h, 0:S], start=True, stop=True)
                    last = mm(dst[:, S:S + P], stk[0:KST, par(a), h, P:S], stq[0:KST, par(a), h, P:S],
                              start=True, stop=True)
                last.then_inc(s["sc_done"], 1)

            def modulation_left():
                pe.wait_ge(s["modt_ready"], 1)
                pe.wait_ge(s["mrow_ready"], 1)
                pe.wait_ge(s["bf_ready"], 2)

            def values(a, g):
                need(pe, s["clip_done"], NPAIR * num(a) + (2 * g + 2))
                if g == 0:
                    need(pe, s["v_ready"], num(a) + 1)
                    if peeled(a) == 0:
                        modulation_left()
                if g % 2 == 0:
                    need(pe, s["o_ready"], 2 * num(a) + g // 2)
                for kt in range(T):
                    for n in range(4):
                        h = 4 * g + n
                        src = pt[:, h // 2, h % 2, 0:S] if kt == 0 else pt[:, h // 2, h % 2, S:S + P]
                        last = mm(OB[VW * n:VW * n + VW, (g % 2) * S + kt * P:(g % 2) * S + S],
                                  va[:, par(a), kt, h * VW:(h + 1) * VW], src, start=(kt == 0), stop=(kt == 1))
                last.then_inc(s["pv_done"], 1)

            def emit(i, pre, front, vproj, attn, back, norm, route):
                g, f, v, a, r, u, q = batches(i)
                if attn:
                    scores(a, 0)
                    scores(a, 1)
                if front:
                    need(pe, s["xn_ready"], num(f) + 1)
                    need(pe, s["k1_ready"], num(f))
                    need(pe, s["rk_ready"], num(f))
                    for t in range(T):
                        last = nc.tensor.transpose(FA[:, t * P:(t + 1) * P], xn[:, t * D:(t + 1) * D], ident)
                    last.then_inc(s["xT_done"], 1)
                if back:
                    values(r, 3)
                if attn:
                    scores(a, 2)
                if front:
                    need(pe, s["hT_ready"], num(f) + 1)
                    mm(FA[:, 0:S], ws[:, W_A:W_A + P], hT[:, :], start=True, stop=True)
                    mm(FA[:, S:2 * S], ws[:, W_B:W_B + P], hT[:, :], start=True, stop=True)\
                        .then_inc(s["ab_done"], 1)
                if attn:
                    scores(a, 3)
                    scores(a, 4)
                if back:
                    need(pe, s["o_ready"], 2 * num(r) + 2)
                    need(pe, s["lg_ready"], num(u))
                    need(pe, s["bank_free"], num(q))
                    if attn:
                        need(pe, s["v_ready"], num(a) + 1)
                    for t in range(T):
                        for g in range(4):
                            last = nc.tensor.transpose((BK, FB)[t][:, g * P:(g + 1) * P],
                                                       ot[:, g, t * P:(t + 1) * P], ident)
                    last.then_inc(s["ot_done"], 1)
                if attn:
                    values(a, 0)
                if front:
                    need(pe, s["c_ready"], num(f) + 1)
                    for g in range(NG):
                        last = mm(FA[0:QR, g * S:(g + 1) * S], ws[:, W_K + g * QR:W_K + (g + 1) * QR],
                                  cc[:, par(f), S:2 * S], start=True, stop=True)
                    last.then_inc(s["k_done"], 1)
                if back:
                    need(pe, s["norm_done"], num(r) + 1)
                    for t in range(T):
                        last = nc.tensor.transpose(BK[:, t * P:(t + 1) * P], at[:, t, :], ident)
                    last.then_inc(s["at_done"], 1)
                if attn:
                    scores(a, 5)
                if back:
                    need(pe, s["ats_ready"], num(r) + 1)
                    need(pe, s["wog_ready"], num(r) + 1)
                    for t in range(T):
                        last = mm(BK[:, S + t * D:S + (t + 1) * D], aTs[:, t * P:(t + 1) * P], wog[:, :],
                                  start=True, stop=True)
                    last.then_inc(s["wo_done"], 1)
                if route:
                    need(pe, s["tot_ready"], num(q) + 1)
                    if back:
                        need(pe, s["norm_done"], num(r) + 1)
                    need(pe, s["bank_free"], num(q))
                    R = FB[:, 0:3 * E]
                    mm(R[:, 0:E], ut_bf[:, :], tot[:, 0:E], start=True, stop=True)
                    mm(R[:, E:2 * E], ut_bf[:, :], tot[:, E:2 * E], start=True, stop=False)
                    mm(R[:, E:2 * E], one_bf[:, :], tot[:, 0:E], start=False, stop=True)
                    mm(R[:, 2 * E:3 * E], one_bf[:, :], tot[:, 0:E], start=True, stop=False)
                    mm(R[:, 2 * E:3 * E], one_bf[:, :], tot[:, E:2 * E], start=False, stop=True)\
                        .then_inc(s["rank_done"], 1)
                if front:
                    need(pe, s["v_ready"], num(v))
                    if peeled(i) == -2:
                        pe.wait_ge(s["sign_ready"], 1)
                    need(pe, s["bank_free"], num(q) + 1)
                    for g in range(NG):
                        mm(FB[0:QR, g * S:(g + 1) * S], ws[:, W_QA + g * QR:W_QA + (g + 1) * QR],
                           cc[:, par(f), 0:S], start=True, stop=False)
                        last = mm(FB[0:QR, g * S:(g + 1) * S], ws[:, W_QB + g * QR:W_QB + (g + 1) * QR],
                                  cc[:, par(f), S:2 * S], start=False, stop=True)
                    last.then_inc(s["q_done"], 1)
                if attn:
                    scores(a, 6)
                    values(a, 1)
                if norm:
                    need(pe, s["h2_ready"], num(u) + 1)
                    if back:
                        need(pe, s["x2_ready"], num(r) + 1)
                    for t in range(T):
                        last = nc.tensor.transpose(BK[:, t * P:(t + 1) * P], h2[:, t, :], ident)
                    last.then_inc(s["h2t_done"], 1)
                if attn:
                    scores(a, 7)
                    values(a, 2)
                if vproj:
                    if front:
                        need(pe, s["q1_ready"], num(f) + 1)
                        need(pe, s["rq_ready"], num(f) + 1)
                    need(pe, s["bank_free"], num(q) + 1)
                    for t in range(T):
                        last = mm(FB[:, t * P:(t + 1) * P], cc[:, par(v), S + t * P:S + (t + 1) * P],
                                  ws[:, W_V:W_V + P], start=True, stop=True)
                    last.then_inc(s["v_done"], 1)
                if norm:
                    need(pe, s["h2ts_ready"], num(u) + 1)
                    for t in range(T):
                        last = mm(BK[:, S + t * E:S + (t + 1) * E], h2Ts[:, t * P:(t + 1) * P],
                                  ws[:, W_R:W_R + E], start=True, stop=True)
                    last.then_inc(s["lg_done"], 1)

            schedule(pe, emit)

            mm = nc.tensor.matmul
            pe.wait_ge(s["table_ready"], 1)
            pe.wait_ge(s["exp_done"], NPAIR * B)
            pe.wait_ge(s["o_ready"], 2 * B)
            pe.wait_ge(s["rk_ready"], B)
            pe.wait_ge(s["bank_free"], B)
            pe.wait_ge(s["lg_ready"], B)

            load_experts, expert = expert_registers(pe)
            load_experts((0, 0))
            load_experts((0, LOADED - 3))

            def step(k, x, g, d):
                if g:
                    b = plus(k, 1)
                    need(pe, s["wgu_ready"], nb_(b) + 1)
                    need(pe, s["xts_ready"], nb_(b) + 1)
                    need(pe, s["hid_ready"], nb_(b) - 1)
                    for n in range(2):
                        for c in range(3):
                            last = mm(GUB[b[1] % 2][:, n, c * P:(c + 1) * P], wgu[:, b[1] % 2, n, c * P:(c + 1) * P],
                                      xTs[:, b[1] % 2, :], start=True, stop=True)
                    last.then_inc(s["gu_done"], 1)
                if x:
                    b = plus(k, 2)
                    need(pe, xb_in[slot(b)], (uses(b) + 1) * DMA)
                    need(pe, s["xts_ready"], nb_(b) - 1)
                    nc.tensor.transpose(XP[b[1] % 2][:, 0:P], xb[:, slot(b), 0:D], ident).then_inc(s["xt_done"], 1)
                if d:
                    b = plus(k, -1)
                    need(pe, s["hid_ready"], nb_(b) + 1)
                    need(pe, s["y_ready"], nb_(b) - 1)
                    e = expert(b)
                    for n in range(3):
                        last = mm(YP[b[1] % 2][:, 0:D], hidT[:, b[1] % 2, n * P:(n + 1) * P],
                                  dn[:, bass.ds(e * (3 * D) + n * D, D)], start=(n == 0), stop=(n == 2))
                    last.then_inc(s["y_done"], 1)
                if k[1] % LOADED == LOADED - 1 and k[1] > 0:
                    load_experts(plus(k, 2))

            block_steps(pe, step)

        @block.scalar
        def _(act):
            af = nc.scalar.activation
            act.wait_ge(s["ws_in"], DMA)
            af(scT[:, :], ws[:, W_CT:W_CT + B], ACT.Silu).then_inc(s["sil_ready"], 1)

            def exps(a, p):
                need(act, s["sc_done"], NPAIR * num(a) + (p + 1))
                need(act, s["pv_done"], 4 * num(a) + (p // 2 - 3))
                af(pt[:, p, :, 0:S + P], SCB[p % 2][:, :, 0:S + P], ACT.Exp, scale=SC)\
                    .then_inc(s["exp_done"], 1)

            def copy_out(a, hf):
                need(act, s["pv_done"], 4 * num(a) + (2 * hf + 2))
                need(act, s["ot_done"], num(a))
                af(ot[:, 2 * hf:2 * hf + 2, :].rearrange("p g n -> p (g n)"), OB[:, :], ACT.Copy)\
                    .then_inc(s["o_ready"], 1)

            def normalise(g):
                groups = {0: 1, SG // T: 2, SG // T + 2: NT // SG}
                if peeled(g) in groups:
                    act.wait_ge(s["shift1_ready"], groups[peeled(g)])
                need(act, s["xT_done"], num(g))
                for t in range(T):
                    cols = slice(num(g) * T + t, num(g) * T + t + 1) if isinstance(g[0], int) else \
                        bass.ds(g[0] * (2 * T) + g[1] * T + t, 1)
                    last = af(xn[:, t * D:(t + 1) * D], xall[:, xtile(g, t, 1)], ACT.Identity,
                              scale=rstd1[:, cols], bias=shift1[:, cols])
                last.then_inc(s["xn_ready"], 1)

            def emit(i, pre, front, vproj, attn, back, norm, route):
                g, f, v, a, r, u, q = batches(i)
                if attn:
                    exps(a, 0)
                    exps(a, 1)
                if front:
                    if peeled(i) == -2:
                        act.wait_ge(s["modt_ready"], 1)
                    need(act, s["xT_done"], num(f) + 1)
                    need(act, s["ab_done"], num(f))
                    af(hT[:, :], FA[:, 0:S], ACT.Identity, scale=ca1T[:, col(f)], bias=saT[:, col(f)])\
                        .then_inc(s["hT_ready"], 1)
                if pre and not attn:
                    normalise(g)
                if route:
                    need(act, s["dif_ready"], num(q) + 1)
                    af(ex[:, par(q), :], dif[:, :], ACT.Exp).then_inc(s["ex_ready"], 1)
                if attn:
                    exps(a, 2)
                if back:
                    copy_out(r, 1)
                if attn:
                    exps(a, 3)
                if norm:
                    need(act, s["h2_ready"], num(u) + 1)
                    need(act, s["ve3_ready"], num(u))
                    for t in range(T):
                        need(act, s["ss_ready"], 2 * num(u) + t)
                        af(sqj[:, :], h2[:, t, :], ACT.Square, scale=D ** -0.5, accum_out=ss[:, t:t + 1])\
                            .then_inc(s["ss_ready"], 1)
                if attn:
                    exps(a, 4)
                if back:
                    need(act, s["at_done"], num(r) + 1)
                    need(act, s["wo_done"], num(r))
                    af(aTs[:, :], BK[:, 0:S], ACT.Copy).then_inc(s["ats_ready"], 1)
                if front:
                    need(act, s["k_done"], num(f) + 1)
                    need(act, s["k_out"], DMA * num(f))
                    af(ks[:, 0, :], FA[0:QR, :], ACT.Copy).then_inc(s["k1_ready"], 1)
                if attn:
                    exps(a, 5)
                if front:
                    need(act, s["rk_ready"], num(f) + 1)
                    af(ks[:, 1, :], rk[:, :], ACT.Copy).then_inc(s["k2_ready"], 1)
                    need(act, s["q_done"], num(f) + 1)
                    need(act, s["q_out"], DMA * num(f))
                    af(qs[:, 0, :], FB[0:QR, :], ACT.Copy).then_inc(s["q1_ready"], 1)
                if attn:
                    exps(a, 6)
                    copy_out(a, 0)
                if norm:
                    need(act, s["h2t_done"], num(u) + 1)
                    need(act, s["lg_done"], num(u))
                    af(h2Ts[:, :], BK[:, 0:S], ACT.Copy).then_inc(s["h2ts_ready"], 1)
                if front:
                    need(act, s["rq_ready"], num(f) + 1)
                    af(qs[:, 1, :], rq[:, :], ACT.Copy).then_inc(s["q2_ready"], 1)
                if attn:
                    exps(a, 7)
                if pre and attn:
                    normalise(g)
                if vproj:
                    if peeled(i) == -1:
                        act.wait_ge(s["z_va"], 1)
                    need(act, s["v_done"], num(v) + 1)
                    need(act, s["pv_done"], 4 * num(v) - 4)
                    af(va[:, par(v), :, :].rearrange("p t (h v) -> p (t h) v", v=VW)[:, :, 0:DH],
                       FB[:, 0:S].rearrange("p (n v) -> p n v", v=DH), ACT.Copy).then_inc(s["v_ready"], 1)
                if norm:
                    need(act, s["rstd3_ready"], num(u) + 1)
                    need(act, scat[par(u)], half(u) * (DMA * 4))
                    for t in range(T):
                        last = af(pl[:, par(u), t, :, 0:D], h2[:, t:t + 1, :].to_broadcast([P, 2, D]), ACT.Copy,
                                  scale=rstd3[:, t:t + 1])
                    last.then_inc(s["pl_ready"], 1)

            schedule(act, emit)

            af = nc.scalar.activation
            act.wait_ge(s["w_in"], 2 * DMA)
            act.wait_ge(s["z_wgu"], 1)
            act.wait_ge(s["table_ready"], 1)
            load_experts, expert = expert_registers(act)
            load_experts((0, 0))
            load_experts((0, LOADED - 3))

            def step(k, x, g, d):
                if x:
                    b = plus(k, 2)
                    need(act, s["gu_done"], nb_(b) - 1)
                    af(wgu[:, b[1] % 2, :, 0:HID],
                       gu[:, bass.ds(expert(b) * (2 * HID), 2 * HID)].rearrange("p (n h) -> p n h", n=2), ACT.Copy,
                       scale=ws[:, W_NW:W_NW + 1]).then_inc(s["wgu_ready"], 1)
                if g:
                    b = plus(k, 1)
                    need(act, s["gu_done"], nb_(b) + 1)
                    need(act, s["hid_ready"], nb_(b) - 1)
                    af(sg[:, b[1] % 2, :], GUB[b[1] % 2][:, 0, 0:HW], ACT.Silu).then_inc(s["sg_ready"], 1)
                if k[1] % LOADED == LOADED - 2 and k[1] > 0:
                    load_experts(plus(k, 3))

            block_steps(act, step)

        @block.vector
        def _(dve):
            V = nc.vector
            tt, ts, stt, cp = V.tensor_tensor, V.tensor_scalar, V.scalar_tensor_tensor, V.tensor_copy
            def stats(m):
                grp = slice(m * SG, (m + 1) * SG)
                for n in range(SG):
                    t = m * SG + n
                    V.bn_stats(st6[:, t, :], xall[:, t * D:(t + 1) * D]).then_inc(s["st6_ready"], 1)
                me, va_ = nmean1[:, grp], var1[:, grp]
                st = st6[:, grp, :]
                need(dve, s["st6_ready"], m * SG + SG)
                tt(me, st[:, :, 1], st[:, :, 4], ALU.add)
                tt(dm1[:, :], st[:, :, 1], st[:, :, 4], ALU.subtract)
                tt(va_, st[:, :, 2], st[:, :, 5], ALU.add).then_inc(s["stat_step"], 1)
                need(dve, s["stat_step"], m * 2 + 1)
                ts(me, me, -0.5, None, ALU.mult)
                tt(dm1[:, :], dm1[:, :], dm1[:, :], ALU.mult)
                ts(va_, va_, 1.0 / D, LN_EPS, ALU.mult, ALU.add).then_inc(s["stat_step"], 1)
                need(dve, s["stat_step"], m * 2 + 2)
                stt(out=va_, in0=dm1[:, :], scalar=0.25, in1=va_, op0=ALU.mult, op1=ALU.add)\
                    .then_inc(s["mv1_ready"], 1)

            dve.wait_ge(s["x_in0"], DMA)
            stats(0)
            dve.wait_ge(s["mod_done"], 1)
            cp(saT[:, :], OB[:, 0:B])
            ts(ca1T[:, :], OB[:, B:2 * B], 1.0, None, ALU.add).then_inc(s["modt_ready"], 1)
            dve.wait_ge(s["cst_in"], DMA)
            dve.wait_ge(s["ws_in"], DMA)
            tt(ws[:, W_QA:W_QA + NG * QR], ws[:, W_QA:W_QA + NG * QR], cst[:, C_SIGN:C_SIGN + NG * QR], ALU.mult)
            ts(ws[:, W_R:W_R + E], ws[:, W_R:W_R + E], ws[:, W_NW:W_NW + 1], None, ALU.mult)\
                .then_inc(s["sign_ready"], 1)
            cp(ut_bf[:, :], cst[:, C_UT:C_UT + P]).then_inc(s["bf_ready"], 1)
            cp(one_bf[:, :], cst[:, C_ONE:C_ONE + P]).then_inc(s["bf_ready"], 1)
            for n in range(4):
                cp(mask4[:, n, :], cst[:, C_MASK:C_MASK + P]).then_inc(s["mask_ready"], 1)
            cp(base[:, :], cst[:, C_BASE0:C_BASE0 + E])
            cp(idf[:, :], cst[:, C_ID0:C_ID0 + 2 * T]).then_inc(s["base_init"], 1)
            dve.wait_ge(s["mod_done"], 2)
            dve.wait_ge(s["ws_in"], DMA)
            ts(alpha[:, :], ws[:, W_AL:W_AL + 1], -0.5, 2.0, ALU.max, ALU.min).then_inc(s["mod_step"], 1)
            ts(mrow[:, D:2 * D], BK[0:B, 2 * D:3 * D], 1.0, None, ALU.add)
            cp(mrow[:, 2 * D:3 * D], BK[0:B, D:2 * D])
            step = 1
            for src, dst in ((0, 0), (3, 3)):
                g_in = BK[0:B, src * D:(src + 1) * D]
                dve.wait_ge(s["mod_step"], step)
                ts(msgn[:, :], g_in, 0.0, 0.5, ALU.is_ge, ALU.subtract)
                ts(mabs[:, :], g_in, -2.0, None, ALU.mult).then_inc(s["mod_step"], 1)
                dve.wait_ge(s["mod_step"], step + 1)
                stt(out=mabs[:, :], in0=g_in, scalar=2.0, in1=mabs[:, :], op0=ALU.mult, op1=ALU.max)\
                    .then_inc(s["mod_step"], 1)
                dve.wait_ge(s["mod_step"], step + 2)
                stt(out=mrow[:, dst * D:(dst + 1) * D], in0=mabs[:, :], scalar=0.5, in1=msgn[:, :],
                    op0=ALU.max, op1=ALU.mult).then_inc(s["mod_step"], 1)
                step += 3
            dve.wait_ge(s["mod_step"], step)
            ts(mrow[:, 4 * D:5 * D], mrow[:, 3 * D:4 * D], alpha[0:B, :], None, ALU.mult).then_inc(s["mrow_ready"], 1)

            def clip(a, p):
                need(dve, s["exp_done"], NPAIR * num(a) + (p + 1))
                diag = pt[:, p, :, :].rearrange("p h (n c) -> p (h n) c", c=2 * P)[:, :, 0:P]
                stt(out=diag, in0=diag, scalar=E_LO, in1=mask4[:, :, :], op0=ALU.max, op1=ALU.min)
                off = pt[:, p, :, P:2 * P]
                ts(off, off, E_LO, E_HI, ALU.max, ALU.min).then_inc(s["clip_done"], 1)

            def emit(i, pre, front, vproj, attn, back, norm, route):
                g, f, v, a, r, u, q = batches(i)
                if attn:
                    clip(a, 0)
                if norm:
                    need(dve, s["t1_ready"], num(u) + 1)
                    need(dve, s["rstd2_ready"], num(u) + 1)
                    need(dve, s["pl_ready"], num(u))
                    need(dve, s["gbh_ready"], num(u))
                    for t in range(T):
                        last = stt(out=h2[:, t, :], in0=t1[:, t, :], scalar=rstd2[:, t:t + 1],
                                   in1=bc[:, par(u), 2 * D:3 * D], op0=ALU.mult, op1=ALU.add)
                    last.then_inc(s["h2_ready"], 1)
                if attn:
                    clip(a, 1)
                    clip(a, 2)
                if front:
                    need(dve, s["ab_done"], num(f) + 1)
                    need(dve, s["v_done"], num(f) - 1)
                    tt(cc[:, par(f), :], FA[:, :], cst[:, C_TRIG:C_TRIG + 2 * S], ALU.mult)\
                        .then_inc(s["c_ready"], 1)
                if back:
                    need(dve, s["ot_done"], num(r) + 1)
                    need(dve, s["at_done"], num(r))
                    for t in range(T):
                        sums = (BK, FB)[t][:, :].rearrange("p (h v) -> p h v", v=VW)[:, :, DH]
                        last = V.reciprocal(rden[:, t, :], sums)
                    last.then_inc(s["rden_ready"], 1)
                    need(dve, s["rden_ready"], num(r) + 1)
                    for t in range(T):
                        last = tt(at[:, t, :].rearrange("p (h v) -> p h v", v=DH),
                                  (BK, FB)[t][:, :].rearrange("p (h v) -> p h v", v=VW)[:, :, 0:DH],
                                  rden[:, t, :].rearrange("p (h o) -> p h o", o=1).to_broadcast([P, H, DH]), ALU.mult)
                    last.then_inc(s["norm_done"], 1)
                if attn:
                    clip(a, 3)
                    clip(a, 4)
                if route:
                    need(dve, s["rank_done"], num(q) + 1)
                    rank = FB[:, 0:3 * E]
                    tt(pos[:, :, :], rank[:, 0:T * E].rearrange("p (t e) -> p t e", e=E),
                       base[:, :].rearrange("p (o e) -> p o e", o=1).to_broadcast([P, T, E]), ALU.add)\
                        .then_inc(s["pos_ready"], 1)
                    need(dve, s["ex_ready"], num(q) + 1)
                    need(dve, s["dest_ready"], num(q))
                    ts(den[:, :], ex[:, par(q), :], 1.0, None, ALU.add).then_inc(s["den_ready"], 1)
                    need(dve, s["pos_ready"], num(q) + 1)
                    tt(base[:, :], rank[:, 2 * E:3 * E], base[:, :], ALU.add).then_inc(s["bank_free"], 1)
                if front:
                    need(dve, s["k1_ready"], num(f) + 1)
                    need(dve, s["k2_ready"], num(f))
                    need(dve, s["k3_ready"], num(f))
                    tt(rk[:, :], FA[0:QR, :], ks[:, 0, :], ALU.subtract).then_inc(s["rk_ready"], 1)
                if attn:
                    clip(a, 5)
                if back:
                    need(dve, s["wo_done"], num(r) + 1)
                    tt(xall[:, xtile(r)], BK[:, S:S + T * D], xall[:, xtile(r)], ALU.add).then_inc(s["x2_ready"], 1)
                if route:
                    ohq = oh[:, par(q), :, :, :]
                    for t in range(T):
                        last = tt(pd[:, t, :, :], ohq[:, t, :, :],
                                  pos[:, t:t + 1, :].to_broadcast([P, 2, E]), ALU.mult)
                    last.then_inc(s["pd_ready"], 1)
                    need(dve, s["pl_ready"], num(q) + 1)
                    need(dve, s["den_ready"], num(q) + 1)
                    V.reciprocal(pl[:, par(q), :, 0, D], den[:, :]).then_inc(s["c0_ready"], 1)
                if front:
                    need(dve, s["q1_ready"], num(f) + 1)
                    need(dve, s["q2_ready"], num(f))
                    need(dve, s["q3_ready"], num(f))
                    tt(rq[:, :], FB[0:QR, :], qs[:, 0, :], ALU.subtract).then_inc(s["rq_ready"], 1)
                if back:
                    apart(dve)
                    need(dve, s["x2_ready"], num(r) + 1)
                    for t in range(T):
                        last = V.bn_stats(st2[:, t, :], xall[:, xtile(r, t, 1)])
                    last.then_inc(s["st2_ready"], 1)
                if route:
                    need(dve, s["pd_ready"], num(q) + 1)
                    V.tensor_reduce(destf[:, :], pd[:, :, :, :].rearrange("p t k e -> p (t k) e"), AX.X, ALU.add)\
                        .then_inc(s["destf_ready"], 1)
                if attn:
                    clip(a, 6)
                if back:
                    apart(dve)
                    need(dve, s["st2_ready"], num(r) + 1)
                    need(dve, s["ve2_ready"], num(r))
                    for t in range(T):
                        last = V.bn_aggr(mv2[:, t, :], st2[:, t, :])
                    last.then_inc(s["mv2_ready"], 1)
                if route:
                    need(dve, s["c0_ready"], num(q) + 1)
                    tt(pl[:, par(q), :, 1, D], ex[:, par(q), :], pl[:, par(q), :, 0, D], ALU.mult)
                    cp(pl[:, par(q), :, :, D + 1].bitcast(i32), idf[:, :].rearrange("p (t k) -> p t k", k=2))\
                        .then_inc(s["id_ready"], 1)
                    need(dve, s["destf_ready"], num(q) + 1)
                    cp(dest[:, par(q), :], destf[:, :]).then_inc(s["dest_ready"], 1)
                if back:
                    need(dve, s["mv2_ready"], num(r) + 1)
                    need(dve, bc_in[par(r)], (half(r) + 1) * DMA)
                    for t in range(T):
                        last = stt(out=t1[:, t, :], in0=xall[:, xtile(r, t, 1)], scalar=mv2[:, t, 0:1],
                                   in1=bc[:, par(r), D:2 * D], op0=ALU.subtract, op1=ALU.mult)
                    last.then_inc(s["t1_ready"], 1)
                if attn:
                    clip(a, 7)
                if norm:
                    need(dve, s["lg_done"], num(u) + 1)
                    need(dve, s["rstd3_ready"], num(u) + 1)
                    for t in range(T):
                        last = ts(lg[:, t, :], BK[:, S + t * E:S + (t + 1) * E], rstd3[:, t:t + 1], None, ALU.mult)
                    last.then_inc(s["lg_ready"], 1)
                    apart(dve)
                    need(dve, s["lg_ready"], num(u) + 1)
                    for t in range(T):
                        last = V.max(mx[:, t, :], lg[:, t, :])
                    last.then_inc(s["mx_ready"], 1)
                if route:
                    need(dve, s["id_ready"], num(q) + 1)
                    ts(idf[:, :], idf[:, :], float(S), None, ALU.add).then_inc(s["base_init"], 1)
                if norm:
                    apart(dve)
                    need(dve, s["mx_ready"], num(u) + 1)
                    for t in range(T):
                        last = V.max_index(mi[:, t, :], mx[:, t, :], lg[:, t, :])
                    last.then_inc(s["mi_ready"], 1)
                    need(dve, s["ex_ready"], num(u))
                    tt(dif[:, :], mx[:, :, 1], mx[:, :, 0], ALU.subtract).then_inc(s["dif_ready"], 1)
                    need(dve, s["mi_ready"], num(u) + 1)
                    cp(mif[:, :, :], mi[:, :, 0:2]).then_inc(s["mif_ready"], 1)
                    need(dve, s["mif_ready"], num(u) + 1)
                    ohr = oh[:, par(u), :, :, :]
                    for t in range(T):
                        last = tt(ohr[:, t, :, :],
                                  cst[:, C_IOTA:C_IOTA + E].rearrange("p (o e) -> p o e", o=1).to_broadcast([P, 2, E]),
                                  mif[:, t, :].rearrange("p (k o) -> p k o", o=1).to_broadcast([P, 2, E]), ALU.is_equal)
                    last.then_inc(s["oh_ready"], 1)
                    need(dve, s["oh_ready"], num(u) + 1)
                    need(dve, s["rank_done"], num(u))
                    tt(tot[:, :].rearrange("p (t e) -> p t e", e=E), ohr[:, :, 0, :], ohr[:, :, 1, :], ALU.add)\
                        .then_inc(s["tot_ready"], 1)
                if peeled(i) in STATS_AFTER:
                    dve.wait_ge(s["x_in"], 3 * DMA)
                    stats(STATS_AFTER[peeled(i)])

            schedule(dve, emit)

            V = nc.vector
            tt, ts, stt, cp = V.tensor_tensor, V.tensor_scalar, V.scalar_tensor_tensor, V.tensor_copy
            steps = [0]

            def chain(ins):
                steps[0] += 1
                ins.then_inc(s["table_step"], 1)
                dve.wait_ge(s["table_step"], steps[0])

            dve.wait_ge(s["bank_free"], B)
            cp(padi[:, :], base[0:1, :]).then_inc(s["pad_ready"], 1)
            tt(cnt[:, :], base[:, :], cst[:, C_BASE0:C_BASE0 + E], ALU.subtract)
            chain(V.memset(wrow[:, :], 1.0))
            chain(ts(cnti[:, :], cnt[:, :], float(P - 1), None, ALU.add))
            chain(ts(cnti[:, :], cnti[:, :], P.bit_length() - 1, None, ALU.arith_shift_right))
            chain(cp(nbf[:, :], cnti[:, :]))
            chain(V.tensor_tensor_scan(bend[:, :], wrow[:, :], nbf[:, :], 0.0, ALU.mult, ALU.add))
            J = cst[0:1, C_BLK:C_BLK + NBLK]
            tt(ge[:, :, :], J.rearrange("p (j o) -> p j o", o=1).to_broadcast([1, NBLK, E]),
               bend[0:1, :].rearrange("p (o e) -> p o e", o=1).to_broadcast([1, NBLK, E]), ALU.is_ge)
            chain(ts(wrow[:, :], nbf[:, :], -1.0, float(QBLK), ALU.mult, ALU.add))
            V.tensor_reduce(bf_[:, 0, :], ge[:, :, 0:NE1], AX.X, ALU.add)
            chain(tt(gw[:, :, :], ge[:, :, 0:NE1],
                     wrow[0:1, 0:NE1].rearrange("p (o e) -> p o e", o=1).to_broadcast([1, NBLK, NE1]), ALU.mult))
            chain(V.tensor_reduce(bf_[:, 1, :], gw[:, :, :], AX.X, ALU.add))
            chain(tt(bf_[:, 1, :], bf_[:, 1, :], J, ALU.add))
            chain(ts(bf_[:, 2, :], bf_[:, 1, :], -1.0, float(DUMMY), ALU.mult, ALU.add))
            chain(tt(bf_[:, 2, :], bf_[:, 2, :], ge[:, :, NE1], ALU.mult))
            chain(tt(bf_[:, 1, :], bf_[:, 1, :], bf_[:, 2, :], ALU.add))
            cp(bi[:, 0, :], bf_[:, 0, :])
            ts(bi[:, 1, :], bf_[:, 1, :], float(P), None, ALU.mult).then_inc(s["table_ready"], 1)


            def step(k, x, g, d):
                if x:
                    b = plus(k, 2)
                    need(dve, s["xt_done"], nb_(b) + 1)
                    need(dve, s["gu_done"], nb_(b) - 1)
                    cp(xTs[:, b[1] % 2, :], XP[b[1] % 2][:, 0:P]).then_inc(s["xts_ready"], 1)
                if g:
                    b = plus(k, 1)
                    need(dve, s["sg_ready"], nb_(b) + 1)
                    need(dve, s["y_done"], nb_(b) - 1)
                    tt(hidT[:, b[1] % 2, :], sg[:, b[1] % 2, :], GUB[b[1] % 2][:, 1, 0:HW], ALU.mult)\
                        .then_inc(s["hid_ready"], 1)
                if d:
                    b = plus(k, -1)
                    need(dve, s["y_done"], nb_(b) + 1)
                    need(dve, yscat[slot(b)], uses(b) * DMA)
                    ts(ysb[:, slot(b), :], YP[b[1] % 2][:, 0:D], xb[:, slot(b), D:D + 1], None, ALU.mult)\
                        .then_inc(s["y_ready"], 1)

            block_steps(dve, step)
            dve.wait_ge(s["gba_in"], DMA)
            bch = TCH // T
            for n in range(NCH):
                dve.wait_ge(s[f"yin{n}"], 2 * DMA)
                c0, c1 = n * TCH * D, (n + 1) * TCH * D
                tt(ybuf[0][:, c0:c1], ybuf[0][:, c0:c1], ybuf[1][:, c0:c1], ALU.add).then_inc(s["sum1"], 1)
                dve.wait_ge(s["sum1"], n + 1)
                for m in range(bch):
                    y = ybuf[0][:, c0 + m * T * D:c0 + (m + 1) * T * D].rearrange("p (t d) -> p t d", d=D)
                    last = tt(y, y, gba[:, n * bch + m:n * bch + m + 1, :].to_broadcast([P, T, D]), ALU.mult)
                last.then_inc(s["sum2"], 1)

        @block.gpsimd
        def _(pool):
            G = nc.gpsimd
            G.memset(epst[:, 0:T], LN_EPS)
            G.memset(epst[:, T:2 * T], RMS_EPS)
            G.memset(mhalf[:, :], -0.5).then_inc(s["z_half"], 1)
            pool.wait_ge(s["z_half"], 1)

            def finish_stats(m):
                grp = slice(m * SG, (m + 1) * SG)
                pool.wait_ge(s["mv1_ready"], m + 1)
                G.tensor_tensor(rstd1[:, grp], var1[:, grp], mhalf[:, 0:SG], ALU.pow).then_inc(s["rstd1_ready"], 1)
                pool.wait_ge(s["rstd1_ready"], m + 1)
                G.tensor_tensor(shift1[:, grp], nmean1[:, grp], rstd1[:, grp], ALU.mult)\
                    .then_inc(s["shift1_ready"], 1)

            finish_stats(0)
            pool.wait_ge(s["shift1_ready"], 1)
            for st in (stq, stk):
                for par_ in range(2):
                    G.memset(st[64:KST, par_, :, :].rearrange("p h n -> p (h n)").bitcast(fp32), 0.0)\
                        .then_inc(s["z_stack"], 1)
            pool.wait_ge(s["z_stack"], 4)
            G.memset(wgu[:, :, :, HID:HW], 0.0).then_inc(s["z_wgu"], 1)
            G.memset(va[:, :, :, :], 1.0).then_inc(s["z_va"], 1)
            pool.wait_ge(s["z_va"], 1)

            def emit(i, pre, front, vproj, attn, back, norm, route):
                g, f, v, a, r, u, q = batches(i)
                if norm:
                    need(pool, s["ss_ready"], 2 * num(u) + 2)
                    G.tensor_tensor(ve3[:, :], ss[:, :], epst[:, T:2 * T], ALU.add)\
                        .then_inc(s["ve3_ready"], 1)
                    need(pool, s["ve3_ready"], num(u) + 1)
                    need(pool, s["lg_ready"], num(u))
                    need(pool, s["pl_ready"], num(u))
                    G.tensor_tensor(rstd3[:, :], ve3[:, :], mhalf[:, 0:T], ALU.pow).then_inc(s["rstd3_ready"], 1)
                    for t in range(T):
                        last = G.tensor_tensor(gbh[:, t, :], h2[:, t, :], bc[:, par(u), 3 * D:4 * D], ALU.mult)
                    last.then_inc(s["gbh_ready"], 1)
                if back:
                    need(pool, bc_in[par(r)], (half(r) + 1) * DMA)
                    need(pool, s["wo_done"], num(r))
                    G.tensor_tensor(wog[:, :], ws[:, W_O:W_O + D], bc[:, par(r), 0:D], ALU.mult)\
                        .then_inc(s["wog_ready"], 1)
                if norm:
                    need(pool, s["gbh_ready"], num(u) + 1)
                    G.tensor_tensor(xall[:, xtile(u)], xall[:, xtile(u)], gbh[:, :, :].rearrange("p t d -> p (t d)"),
                                    ALU.add).then_inc(s["base_ready"], 1)
                if front:
                    need(pool, s["k2_ready"], num(f) + 1)
                    G.tensor_tensor(ks[:, 2, :], rk[:, :], ks[:, 1, :], ALU.subtract).then_inc(s["k3_ready"], 1)
                    need(pool, s["q2_ready"], num(f) + 1)
                    G.tensor_tensor(qs[:, 2, :], rq[:, :], qs[:, 1, :], ALU.subtract).then_inc(s["q3_ready"], 1)
                if back:
                    need(pool, s["mv2_ready"], num(r) + 1)
                    G.tensor_tensor(ve2[:, :], mv2[:, :, 1], epst[:, 0:T], ALU.add).then_inc(s["ve2_ready"], 1)
                    need(pool, s["ve2_ready"], num(r) + 1)
                    need(pool, s["h2_ready"], num(r))
                    G.tensor_tensor(rstd2[:, :], ve2[:, :], mhalf[:, 0:T], ALU.pow).then_inc(s["rstd2_ready"], 1)
                if route:
                    apart(pool)
                    need(pool, s["dest_ready"], num(q) + 1)
                    need(pool, s["pl_ready"], num(q) + 1)
                    for t in range(T):
                        for k in range(2):
                            G.indirect_dma_start(
                                queue, bass.IndirectOffsetOnAxis(dest[:, par(q), 2 * t + k:2 * t + k + 1], 0),
                                pl[:, par(q), t, k, :], None).then_inc(scat[par(q)], DMA)
                if peeled(i) in STATS_AFTER:
                    finish_stats(STATS_AFTER[peeled(i)])

            schedule(pool, emit)

            G = nc.gpsimd
            below = G.to_reg(2 * NTOK - 2)
            bound = pool.alloc_register("bound")

            def step(k, x, g, d):
                if not d:
                    return
                b = plus(k, -1)
                need(pool, s["y_ready"], nb_(b) + 1)
                pool.reg_add(bound, below, 1)
                G.indirect_dma_start(ydram, bass.IndirectOffsetOnAxis(xb[:, slot(b), D + 1:D + 2].bitcast(u32), 0),
                                     ysb[:, slot(b), :], None, bounds_check=bound, oob_is_err=False)\
                 .then_inc(yscat[slot(b)], DMA)

            block_steps(pool, step)
            pool.wait_ge(s["base_ready"], B)
            for n in range(NCH):
                pool.wait_ge(s["sum2"], n + 1)
                c0, c1 = n * TCH * D, (n + 1) * TCH * D
                G.tensor_tensor(xall[:, c0:c1], xall[:, c0:c1], ybuf[0][:, c0:c1], ALU.add).then_inc(s["sum3"], 1)



def host_constants():
    c = np.zeros((P, CW), np.float32)
    p = np.arange(P)
    c[:, C_ID:C_ID + P] = np.eye(P)
    c[:, C_UT:C_UT + P] = p[:, None] < p[None, :]
    c[:, C_ONE:C_ONE + P] = 1.0
    c[:, C_MASK:C_MASK + P] = np.where(p[None, :] >= p[:, None], np.float32(E_HI), 0.0)
    inv = np.float32(10000.0) ** (-np.arange(0, DR, 2, dtype=np.float32) / np.float32(DR))
    ang = np.arange(S, dtype=np.float32)[:, None] * inv
    cos, sin = np.cos(ang).T, np.sin(ang).T
    for n, row in enumerate((cos[0], sin[0], cos[1], sin[1])):
        c[n * DL:(n + 1) * DL, C_TRIG:C_TRIG + S] = row
    second = slice(C_TRIG + S, C_TRIG + 2 * S)
    c[0:DL, second] = 1.0
    for d in range(DR):
        c[DL + d, second] = cos[d // 2]
        c[DL + DR + d, second] = sin[d // 2] * (1.0 if d % 2 else -1.0)
    c[2 * DL:3 * DL, second] = 1.0
    sign = np.ones((P, NG, DQK, HG), np.float32)
    sign[DL:2 * DL, :, DH, :] = -1.0
    sign[3 * DL:4 * DL, :, DH + 2, :] = -1.0
    c[:, C_SIGN:C_SIGN + NG * QR] = sign.reshape(P, -1)
    c[:, C_IOTA:C_IOTA + E] = np.arange(E)
    c[:, C_BASE0:C_BASE0 + E] = np.arange(E) * QROWS
    for t in range(T):
        for k in range(2):
            c[:, C_ID0 + 2 * t + k] = k * NTOK + t * P + p
    c[:, C_BLK:C_BLK + NBLK] = np.arange(NBLK)
    c[:, C_PAD + D + 1] = np.full(P, PADID, np.int32).view(np.float32)
    return c


def host_layout(a):
    w = np.zeros((P, WW), np.float32)
    dq, uq, qr = a["L0_attn_W_DQ"], a["L0_attn_W_UQ"], a["L0_attn_W_QR"]
    for n in range(4):
        w[:, W_A + n * DL:W_A + (n + 1) * DL] = dq
    w[:, W_B:W_B + DL] = a["L0_attn_W_DKV"]
    w[:, W_B + DL:W_B + DL + DR] = a["L0_attn_W_KR"]
    w[:, W_B + DL + DR:W_B + DL + 2 * DR] = a["L0_attn_W_KR"][:, [1, 0, 3, 2]]
    w[:, W_B + 2 * DL:W_B + 3 * DL] = dq
    qa = np.zeros((P, NG, DQK, HG), np.float32)
    q4 = qr.reshape(DL, HG, NG, DR).transpose(0, 2, 1, 3)
    for freq in range(2):
        c_rows = slice(2 * freq * DL, (2 * freq + 1) * DL)
        s_rows = slice((2 * freq + 1) * DL, (2 * freq + 2) * DL)
        for d in range(2):
            qa[c_rows, :, DH + 2 * freq + d, :] = q4[:, :, :, 2 * freq + d]
            qa[s_rows, :, DH + 2 * freq + d, :] = q4[:, :, :, 2 * freq + 1 - d]
    w[:, W_QA:W_QA + NG * QR] = qa.reshape(P, -1)
    qb = np.zeros((P, NG, DQK, HG), np.float32)
    qb[2 * DL:3 * DL, :, 0:DH, :] = uq.reshape(DL, HG, NG, DH).transpose(0, 2, 3, 1)
    w[:, W_QB:W_QB + NG * QR] = qb.reshape(P, -1)
    kb = np.zeros((P, NG, DQK, HG), np.float32)
    kb[0:DL, :, 0:DH, :] = a["L0_attn_W_UK"].reshape(DL, HG, NG, DH).transpose(0, 2, 3, 1)
    for d in range(DR):
        kb[DL + d, :, DH + d, :] = 1.0
        kb[DL + DR + d, :, DH + d, :] = 1.0
    w[:, W_K:W_K + NG * QR] = kb.reshape(P, -1)
    w[0:DL, W_V:W_V + H * DH] = a["L0_attn_W_UV"]
    w[:, W_O:W_O + D] = a["L0_attn_W_O"]
    w[:, W_R:W_R + E] = a["L0_ffn_router_weight"].T
    w[:, W_NW] = a["L0_ffn_norm_weight"]
    w[:, W_AL] = a["L0_ffn_residual_alpha"]
    w[:, W_CT:W_CT + B] = a["L0_c"].T
    gup = np.ascontiguousarray(a["L0_ffn_gate_up_weight"].transpose(2, 0, 1).reshape(P, E * 2 * HID))
    dn = np.zeros((E, 3 * P, D), np.float32)
    dn[:, 0:HID, :] = a["L0_ffn_down_weight"].transpose(0, 2, 1)
    dn = np.ascontiguousarray(dn.reshape(E, 3, P, D).transpose(2, 0, 1, 3).reshape(P, E * 3 * D))
    return w, gup, dn


def kernel(**inputs):
    import concourse.bacc as bacc
    from concourse.bass_utils import run_bass_kernel_spmd

    a = {k: np.asarray(v) for k, v in inputs.items()}
    w, gup, dn = host_layout(a)
    arrays = {"x": np.ascontiguousarray(a["L0_attn_x"]), "consts": host_constants(), "wsmall": w,
              "wmod": np.ascontiguousarray(a["L0_wmod"]), "gup": gup, "down": dn}
    nc = bacc.Bacc("TRN2", target_bir_lowering=False, num_devices=1)
    args = [nc.dram_tensor(n, v.shape, mybir.dt.float32, kind="ExternalInput").ap() for n, v in arrays.items()]
    out = nc.dram_tensor("out", (B, S, D), mybir.dt.float32, kind="ExternalOutput").ap()
    adaln_kernel(nc, *args, out)
    r = run_bass_kernel_spmd(nc, [arrays], core_ids=[0])
    return r.results[0]["out"]
```
